# Optimizing a Trainium2 kernel written in Bass

```python
import numpy as np
import jax
import jax.numpy as jnp

def _softmax(x, axis=-1):
    return jax.nn.softmax(x, axis=axis)

def _gelu(x):
    return jax.nn.gelu(x, approximate=True)

def _silu(x):
    return jax.nn.silu(x)

def _sigmoid(x):
    return jax.nn.sigmoid(x)

def _layernorm(x, axis=-1, eps=1e-05):
    m = jnp.mean(x, axis=axis, keepdims=True)
    v = jnp.var(x, axis=axis, keepdims=True)
    return (x - m) / jnp.sqrt(v + eps)

def _scatter_add(tgt, idx, src, axis=0):
    return tgt.at[idx].add(src)

def _segment_sum(src, seg, n):
    return jax.ops.segment_sum(src, seg, n)
kernel_name = 'mk_flamingo_gated_d1_seqx_r4_e53116'

def setup_inputs(seed: int=0):
    np.random.seed(seed)
    _w = jnp.asarray

    def _rec_inputs():
        import jax
        import jax.numpy as jnp
        _rk = jax.random.key(seed)
        x = 4.136e-05 + 0.9999 * jax.random.normal(jax.random.fold_in(_rk, 1), (4, 512, 512), jnp.float32)
        _lenS = 512 - jax.random.randint(jax.random.fold_in(_rk, 7), (4,), 0, max(1, 512 // 4) + 1, jnp.int32)
        _lenS2 = 512 - jax.random.randint(jax.random.fold_in(_rk, 8), (4,), 0, max(1, 512 // 4) + 1, jnp.int32)
        _ctx_1024P = jax.random.normal(jax.random.fold_in(_rk, 11), (4, 16, 256), jnp.float32)
        _ctx_1024c = jax.random.dirichlet(jax.random.fold_in(_rk, 511), 0.3 * jnp.ones((16,), jnp.float32), (4, 512))
        _ctx_1024t = jnp.einsum('bsk,bkd->bsd', _ctx_1024c, _ctx_1024P)
        _ctx_1024t = _ctx_1024t * jax.lax.rsqrt(jnp.mean(jnp.square(_ctx_1024t)) + 1e-12) * 0.953939
        ctx_1024 = -0.000292821 + 1.00034 * (_ctx_1024t + 0.3 * jax.random.normal(jax.random.fold_in(_rk, 611), (4, 512, 256), jnp.float32))
        _g = jax.random.normal(jax.random.fold_in(_rk, 9001), (2, 1), jnp.float32)
        _g = jnp.sign(_g) * jnp.maximum(jnp.abs(_g), 1.0) + (_g == 0) * 1.0
        g_xattn = _g[0]
        g_ffn = _g[1]
        return (x, ctx_1024, g_xattn, g_ffn)
    x, ctx_1024, g_xattn, g_ffn = _rec_inputs()

    def _L0_xattn_setup():
        import jax, jax.numpy as jnp
        import numpy as np
        import math
        B, L, DM = (2, 512, 256)
        DS, DC, EXP = (16, 4, 2)
        DI = EXP * DM
        DR = math.ceil(DM / 16)
        DT_MIN, DT_MAX, DT_FLOOR = (0.001, 0.1, 0.0001)

        def _ssm_forward(hidden_states, z, in_proj_w, conv_w, conv_b, x_proj_w, dt_proj_w, dt_proj_b, A_log, D):
            b = hidden_states.shape[0]
            x = jnp.einsum('ed,bld->bel', in_proj_w, hidden_states)
            xp = jnp.pad(x, ((0, 0), (0, 0), (DC - 1, 0)))
            xc = jax.lax.conv_general_dilated(xp, conv_w[:, None, :], window_strides=(1,), padding='VALID', dimension_numbers=('NCH', 'OIH', 'NCH'), feature_group_count=DI)
            u = jax.nn.silu(xc + conv_b[None, :, None])
            x_dbl = jnp.einsum('ke,bel->bkl', x_proj_w, u)
            dt_lo = x_dbl[:, :DR]
            Bm = x_dbl[:, DR:DR + DS]
            Cm = x_dbl[:, DR + DS:]
            delta = jax.nn.softplus(jnp.einsum('er,brl->bel', dt_proj_w, dt_lo) + dt_proj_b[None, :, None])
            A = -jnp.exp(A_log)

            def step(state, xs):
                d_t, B_t, C_t, u_t = xs
                dA = jnp.exp(d_t[..., None] * A)
                state = state * dA + (d_t * u_t)[..., None] * B_t[:, None, :]
                y_t = jnp.einsum('ben,bn->be', state, C_t)
                return (state, y_t)
            xs = (jnp.moveaxis(delta, -1, 0), jnp.moveaxis(Bm, -1, 0), jnp.moveaxis(Cm, -1, 0), jnp.moveaxis(u, -1, 0))
            state0 = jnp.zeros((b, DI, DS), delta.dtype)
            _, ys = jax.lax.scan(step, state0, xs)
            y = jnp.moveaxis(ys, 0, -1)
            y = y + D[None, :, None] * u
            y = y * jax.nn.silu(z)
            return jnp.swapaxes(y, 1, 2)
        key = jax.random.key(seed)
        ks = jax.random.split(key, 8)
        hidden_states = jax.random.normal(ks[0], (B, L, DM), jnp.float32)
        z = jax.random.normal(ks[1], (B, DI, L), jnp.float32)
        in_proj_w = jax.random.normal(ks[2], (DI, DM), jnp.float32) * DM ** (-0.5)
        conv_w = jax.random.normal(ks[3], (DI, DC), jnp.float32) * DC ** (-0.5)
        conv_b = jnp.zeros((DI,), jnp.float32)
        x_proj_w = jax.random.normal(ks[4], (DR + 2 * DS, DI), jnp.float32) * DI ** (-0.5)
        dt_std = DR ** (-0.5)
        dt_proj_w = jax.random.uniform(ks[5], (DI, DR), jnp.float32, -dt_std, dt_std)
        dt = jnp.exp(jax.random.uniform(ks[6], (DI,), jnp.float32) * (math.log(DT_MAX) - math.log(DT_MIN)) + math.log(DT_MIN))
        dt = jnp.clip(dt, DT_FLOOR)
        dt_proj_b = dt + jnp.log(-jnp.expm1(-dt))
        A_log = jnp.log(jnp.broadcast_to(jnp.arange(1, DS + 1, dtype=jnp.float32), (DI, DS)))
        D = jnp.ones((DI,), jnp.float32)
        return dict(hidden_states=hidden_states, z=z, in_proj_w=in_proj_w, conv_w=conv_w, conv_b=conv_b, x_proj_w=x_proj_w, dt_proj_w=dt_proj_w, dt_proj_b=dt_proj_b, A_log=A_log, D=D)
    _L0_xattn_all = _L0_xattn_setup()
    _L0_xattn_in = {k: v for k, v in _L0_xattn_all.items() if k in ('in_proj_w', 'conv_w', 'conv_b', 'x_proj_w', 'dt_proj_w', 'dt_proj_b', 'A_log', 'D')}
    del _L0_xattn_all

    def _L0_ffn_setup():
        import jax, jax.numpy as jnp
        import numpy as np
        HID = 512
        N_HEADS = 16
        N_KV = 16
        HEAD_DIM = HID // N_HEADS
        N_EXP = 8
        TOP_K = 2
        MOE_I = 352
        SH_I = 1408
        EPS = 1e-06
        ROPE_THETA = 1000000.0

        def _rms(x, w):
            v = jnp.mean(jnp.square(x), axis=-1, keepdims=True)
            return x * jax.lax.rsqrt(v + EPS) * w

        def _rope(q, k):
            S, D = (q.shape[1], q.shape[-1])
            inv = 1.0 / ROPE_THETA ** (jnp.arange(0, D, 2, dtype=jnp.float32) / D)
            freqs = jnp.arange(S, dtype=jnp.float32)[:, None] * inv[None, :]
            emb = jnp.concatenate([freqs, freqs], axis=-1)
            cos = jnp.cos(emb)[None, :, None, :]
            sin = jnp.sin(emb)[None, :, None, :]

            def rot(t):
                t1, t2 = (t[..., :D // 2], t[..., D // 2:])
                return jnp.concatenate([-t2, t1], axis=-1)
            return (q * cos + rot(q) * sin, k * cos + rot(k) * sin)
        key = jax.random.key(seed)
        ks = jax.random.split(key, 20)
        s = 0.02
        d = {'x': jax.random.normal(ks[0], (2, 256, HID), jnp.float32), 'w_ln1': jnp.ones((HID,), jnp.float32), 'wq': jax.random.normal(ks[1], (HID, N_HEADS * HEAD_DIM), jnp.float32) * s, 'bq': jnp.zeros((N_HEADS * HEAD_DIM,), jnp.float32), 'wk': jax.random.normal(ks[2], (HID, N_KV * HEAD_DIM), jnp.float32) * s, 'bk': jnp.zeros((N_KV * HEAD_DIM,), jnp.float32), 'wv': jax.random.normal(ks[3], (HID, N_KV * HEAD_DIM), jnp.float32) * s, 'bv': jnp.zeros((N_KV * HEAD_DIM,), jnp.float32), 'wo': jax.random.normal(ks[4], (N_HEADS * HEAD_DIM, HID), jnp.float32) * s, 'w_ln2': jnp.ones((HID,), jnp.float32), 'w_router': jax.random.normal(ks[5], (HID, N_EXP), jnp.float32) * s, 'w_gate_e': jax.random.normal(ks[6], (N_EXP, HID, MOE_I), jnp.float32) * s, 'w_up_e': jax.random.normal(ks[7], (N_EXP, HID, MOE_I), jnp.float32) * s, 'w_down_e': jax.random.normal(ks[8], (N_EXP, MOE_I, HID), jnp.float32) * s, 'w_sh_gate': jax.random.normal(ks[9], (HID, SH_I), jnp.float32) * s, 'w_sh_up': jax.random.normal(ks[10], (HID, SH_I), jnp.float32) * s, 'w_sh_down': jax.random.normal(ks[11], (SH_I, HID), jnp.float32) * s, 'w_sh_eg': jax.random.normal(ks[12], (HID, 1), jnp.float32) * s}
        return d
    _L0_ffn_all = _L0_ffn_setup()
    _L0_ffn_in = {k: v for k, v in _L0_ffn_all.items() if k in ('w_ln1', 'wq', 'bq', 'wk', 'bk', 'wv', 'bv', 'wo', 'w_ln2', 'w_router', 'w_gate_e', 'w_up_e', 'w_down_e', 'w_sh_gate', 'w_sh_up', 'w_sh_down', 'w_sh_eg')}
    del _L0_ffn_all
    return {'x': x, 'ctx_1024': ctx_1024, 'g_xattn': g_xattn, 'g_ffn': g_ffn, 'L0_xattn_in_proj_w': _L0_xattn_in['in_proj_w'], 'L0_xattn_conv_w': _L0_xattn_in['conv_w'], 'L0_xattn_conv_b': _L0_xattn_in['conv_b'], 'L0_xattn_x_proj_w': _L0_xattn_in['x_proj_w'], 'L0_xattn_dt_proj_w': _L0_xattn_in['dt_proj_w'], 'L0_xattn_dt_proj_b': _L0_xattn_in['dt_proj_b'], 'L0_xattn_A_log': _L0_xattn_in['A_log'], 'L0_xattn_D': _L0_xattn_in['D'], 'L0_ffn_w_ln1': _L0_ffn_in['w_ln1'], 'L0_ffn_wq': _L0_ffn_in['wq'], 'L0_ffn_bq': _L0_ffn_in['bq'], 'L0_ffn_wk': _L0_ffn_in['wk'], 'L0_ffn_bk': _L0_ffn_in['bk'], 'L0_ffn_wv': _L0_ffn_in['wv'], 'L0_ffn_bv': _L0_ffn_in['bv'], 'L0_ffn_wo': _L0_ffn_in['wo'], 'L0_ffn_w_ln2': _L0_ffn_in['w_ln2'], 'L0_ffn_w_router': _L0_ffn_in['w_router'], 'L0_ffn_w_gate_e': _L0_ffn_in['w_gate_e'], 'L0_ffn_w_up_e': _L0_ffn_in['w_up_e'], 'L0_ffn_w_down_e': _L0_ffn_in['w_down_e'], 'L0_ffn_w_sh_gate': _L0_ffn_in['w_sh_gate'], 'L0_ffn_w_sh_up': _L0_ffn_in['w_sh_up'], 'L0_ffn_w_sh_down': _L0_ffn_in['w_sh_down'], 'L0_ffn_w_sh_eg': _L0_ffn_in['w_sh_eg']}

def reference(x, ctx_1024, g_xattn, g_ffn, L0_xattn_in_proj_w, L0_xattn_conv_w, L0_xattn_conv_b, L0_xattn_x_proj_w, L0_xattn_dt_proj_w, L0_xattn_dt_proj_b, L0_xattn_A_log, L0_xattn_D, L0_ffn_w_ln1, L0_ffn_wq, L0_ffn_bq, L0_ffn_wk, L0_ffn_bk, L0_ffn_wv, L0_ffn_bv, L0_ffn_wo, L0_ffn_w_ln2, L0_ffn_w_router, L0_ffn_w_gate_e, L0_ffn_w_up_e, L0_ffn_w_down_e, L0_ffn_w_sh_gate, L0_ffn_w_sh_up, L0_ffn_w_sh_down, L0_ffn_w_sh_eg):
    import jax
    import jax.numpy as jnp

    def _L0_xattn_ref(hidden_states, z, in_proj_w, conv_w, conv_b, x_proj_w, dt_proj_w, dt_proj_b, A_log, D):
        import jax, jax.numpy as jnp
        import numpy as np
        import math
        B, L, DM = (2, 512, 256)
        DS, DC, EXP = (16, 4, 2)
        DI = EXP * DM
        DR = math.ceil(DM / 16)
        DT_MIN, DT_MAX, DT_FLOOR = (0.001, 0.1, 0.0001)

        def _ssm_forward(hidden_states, z, in_proj_w, conv_w, conv_b, x_proj_w, dt_proj_w, dt_proj_b, A_log, D):
            b = hidden_states.shape[0]
            x = jnp.einsum('ed,bld->bel', in_proj_w, hidden_states)
            xp = jnp.pad(x, ((0, 0), (0, 0), (DC - 1, 0)))
            xc = jax.lax.conv_general_dilated(xp, conv_w[:, None, :], window_strides=(1,), padding='VALID', dimension_numbers=('NCH', 'OIH', 'NCH'), feature_group_count=DI)
            u = jax.nn.silu(xc + conv_b[None, :, None])
            x_dbl = jnp.einsum('ke,bel->bkl', x_proj_w, u)
            dt_lo = x_dbl[:, :DR]
            Bm = x_dbl[:, DR:DR + DS]
            Cm = x_dbl[:, DR + DS:]
            delta = jax.nn.softplus(jnp.einsum('er,brl->bel', dt_proj_w, dt_lo) + dt_proj_b[None, :, None])
            A = -jnp.exp(A_log)

            def step(state, xs):
                d_t, B_t, C_t, u_t = xs
                dA = jnp.exp(d_t[..., None] * A)
                state = state * dA + (d_t * u_t)[..., None] * B_t[:, None, :]
                y_t = jnp.einsum('ben,bn->be', state, C_t)
                return (state, y_t)
            xs = (jnp.moveaxis(delta, -1, 0), jnp.moveaxis(Bm, -1, 0), jnp.moveaxis(Cm, -1, 0), jnp.moveaxis(u, -1, 0))
            state0 = jnp.zeros((b, DI, DS), delta.dtype)
            _, ys = jax.lax.scan(step, state0, xs)
            y = jnp.moveaxis(ys, 0, -1)
            y = y + D[None, :, None] * u
            y = y * jax.nn.silu(z)
            return jnp.swapaxes(y, 1, 2)
        return _ssm_forward(hidden_states, z, in_proj_w, conv_w, conv_b, x_proj_w, dt_proj_w, dt_proj_b, A_log, D)

    def _L0_ffn_ref(x, w_ln1, wq, bq, wk, bk, wv, bv, wo, w_ln2, w_router, w_gate_e, w_up_e, w_down_e, w_sh_gate, w_sh_up, w_sh_down, w_sh_eg):
        import jax, jax.numpy as jnp
        import numpy as np
        HID = 512
        N_HEADS = 16
        N_KV = 16
        HEAD_DIM = HID // N_HEADS
        N_EXP = 8
        TOP_K = 2
        MOE_I = 352
        SH_I = 1408
        EPS = 1e-06
        ROPE_THETA = 1000000.0

        def _rms(x, w):
            v = jnp.mean(jnp.square(x), axis=-1, keepdims=True)
            return x * jax.lax.rsqrt(v + EPS) * w

        def _rope(q, k):
            S, D = (q.shape[1], q.shape[-1])
            inv = 1.0 / ROPE_THETA ** (jnp.arange(0, D, 2, dtype=jnp.float32) / D)
            freqs = jnp.arange(S, dtype=jnp.float32)[:, None] * inv[None, :]
            emb = jnp.concatenate([freqs, freqs], axis=-1)
            cos = jnp.cos(emb)[None, :, None, :]
            sin = jnp.sin(emb)[None, :, None, :]

            def rot(t):
                t1, t2 = (t[..., :D // 2], t[..., D // 2:])
                return jnp.concatenate([-t2, t1], axis=-1)
            return (q * cos + rot(q) * sin, k * cos + rot(k) * sin)
        B, S, H = x.shape
        h = _rms(x, w_ln1)
        q = (h @ wq + bq).reshape(B, S, N_HEADS, HEAD_DIM)
        k = (h @ wk + bk).reshape(B, S, N_KV, HEAD_DIM)
        v = (h @ wv + bv).reshape(B, S, N_KV, HEAD_DIM)
        q, k = _rope(q, k)
        rep = N_HEADS // N_KV
        if rep > 1:
            k = jnp.repeat(k, rep, axis=2)
            v = jnp.repeat(v, rep, axis=2)
        scores = jnp.einsum('bqhd,bkhd->bhqk', q, k) * HEAD_DIM ** (-0.5)
        causal = jnp.tril(jnp.ones((S, S), bool))
        scores = jnp.where(causal[None, None], scores, jnp.finfo(scores.dtype).min)
        attn = jax.nn.softmax(scores, axis=-1)
        ctx = jnp.einsum('bhqk,bkhd->bqhd', attn, v).reshape(B, S, N_HEADS * HEAD_DIM)
        x = x + ctx @ wo
        h = _rms(x, w_ln2).reshape(B * S, H)
        logits = h @ w_router
        probs = jax.nn.softmax(logits, axis=-1)
        top_w, top_i = jax.lax.top_k(probs, TOP_K)
        combine = jnp.sum(jax.nn.one_hot(top_i, N_EXP, dtype=h.dtype) * top_w[..., None], axis=1)
        g = jnp.einsum('th,ehi->eti', h, w_gate_e)
        u = jnp.einsum('th,ehi->eti', h, w_up_e)
        y = jnp.einsum('eti,eih->eth', jax.nn.silu(g) * u, w_down_e)
        routed = jnp.einsum('eth,te->th', y, combine)
        sh = jax.nn.silu(h @ w_sh_gate) * (h @ w_sh_up) @ w_sh_down
        sh = sh * jax.nn.sigmoid(h @ w_sh_eg)
        x = x + (routed + sh).reshape(B, S, H)
        return x
    x = x + jnp.tanh(g_xattn[0]) * _L0_xattn_ref(ctx_1024, _layernorm(x, axis=-1), L0_xattn_in_proj_w, L0_xattn_conv_w, L0_xattn_conv_b, L0_xattn_x_proj_w, L0_xattn_dt_proj_w, L0_xattn_dt_proj_b, L0_xattn_A_log, L0_xattn_D)
    x = x + jnp.tanh(g_ffn[0]) * _L0_ffn_ref(_layernorm(x, axis=-1), L0_ffn_w_ln1, L0_ffn_wq, L0_ffn_bq, L0_ffn_wk, L0_ffn_bk, L0_ffn_wv, L0_ffn_bv, L0_ffn_wo, L0_ffn_w_ln2, L0_ffn_w_router, L0_ffn_w_gate_e, L0_ffn_w_up_e, L0_ffn_w_down_e, L0_ffn_w_sh_gate, L0_ffn_w_sh_up, L0_ffn_w_sh_down, L0_ffn_w_sh_eg)
    return x

_drawn_inputs = setup_inputs


def setup_inputs(seed=0):
    import zlib

    import numpy as np

    out = dict(_drawn_inputs(seed))
    spreads = {'L0_xattn_conv_b': (0.0, 0.1),
     'L0_xattn_D': (1.0, 0.2),
     'L0_ffn_w_ln1': (1.0, 0.2),
     'L0_ffn_bq': (0.0, 0.8),
     'L0_ffn_bk': (0.0, 0.8),
     'L0_ffn_bv': (0.0, 0.1),
     'L0_ffn_w_ln2': (1.0, 0.2)}
    factors = {'L0_xattn_dt_proj_w': 4.939}
    for name, (base, spread) in spreads.items():
        noise = np.random.default_rng([zlib.crc32(name.encode()), seed]).standard_normal(out[name].shape)
        drawn = base * np.exp(spread * noise) if base else spread * noise
        out[name] = jnp.asarray(drawn.astype(out[name].dtype))
    for name, factor in factors.items():
        out[name] = (out[name] * factor).astype(out[name].dtype)
    return out
```

```python
import numpy as np
from contextlib import ExitStack

import concourse.bass as bass
from concourse import mybir

B, L, H = 4, 512, 512
DC = 256
DI, NS, DR = 512, 16, 16
TAPS = 4
NH, HD = 16, 32
NE, EI = 8, 352
NU = 12
P = 128
T4 = L // P
KC = H // P
HB = 2
TH = HB * T4
CW = [128, 128, 96]
NCH = len(CW)
NG = HB
GW = KC * 2 * EI
DW = NCH * H
ROUTE = 10

MASKED = -3.0e38


def build(nc, x_in, ctx_in, gates_in, w_in_in, chan_in, xproj_in, dtproj_in, watt_in, bqk_in,
          bv_in, wln_in, route_in, wffn_in, rope_in, perm_in, ident_in, mask_in, iota_in, out,
          b_scratch):
    f32, f32r, bf16, u32 = (mybir.dt.float32, mybir.dt.float32r, mybir.dt.bfloat16,
                            mybir.dt.uint32)
    ALU, ACT, AX = mybir.AluOpType, mybir.ActivationFunctionType, mybir.AxisListType
    ds = bass.ds
    SCALE = float(HD) ** -0.5

    ctx = ExitStack()
    with ctx:
        def sem(name):
            return ctx.enter_context(nc.semaphore(name))

        def pb(name, shape):
            return ctx.enter_context(nc.psum_tensor(name, shape, f32))

        def arena(stack):
            return lambda name, shape, dt=f32: stack.enter_context(nc.sbuf_tensor(name, shape, dt))

        keep = arena(ctx)
        xs = keep("xs", [P, B * T4, H])
        ident = keep("ident", [P, P])
        identb = keep("identb", [P, P], bf16)
        mask = keep("mask", [P, P])
        maskb = keep("maskb", [P, P], bf16)
        chan = keep("chan", [P, T4, TAPS + 3 + NS])
        aneg = keep("aneg", [P, T4, NS])
        gates = keep("gates", [P, 2])
        tg = keep("tg", [P, 4])
        tgq = keep("tgq", [P, 1])
        mhalf, eps5, eps6, mone, perh = [keep(n, [P, T4]) for n in ("mhalf", "eps5", "eps6", "mone", "perh")]
        tick = keep("tick", [P, 1])
        wln = keep("wln", [P, 2, KC])
        cmb = keep("cmb", [P, B * T4, NU])
        iota8 = keep("iota8", [P, NE])

        sa = ExitStack()
        mid = arena(sa)
        wah = mid("wah", [P, KC, 4 * H], f32r)
        wal = mid("wal", [P, KC, 4 * H], f32r)

        s1 = ExitStack()
        scn = arena(s1)
        wraw = scn("wraw", [P, 4 * H])
        w_in = scn("w_in", [P, DC // P, DI])
        xproj = scn("xproj", [P, T4, DR + 2 * NS])
        dtproj = scn("dtproj", [DR, DI])
        ddiag = scn("ddiag", [P, T4, P])
        cT = scn("cT", [P, HB, DC // P, L])
        DL = scn("DL", [P, T4, L])
        DU = scn("DU", [P, T4, L])
        ZS = scn("ZS", [P, T4, L])
        YA = scn("YA", [P, T4, L])
        HS = scn("HS", [P, 2, T4, L])
        GB = scn("GB", [P, 2, T4, L])
        T2, T1 = HS[:, 0], HS[:, 1]
        U2 = GB[:, 0]
        xd = scn("xd", [DR + 2 * NS, L])
        Ct = scn("Ct", [P, T4, NS])
        BB = scn("BB", [P, 2, 2, L])
        bn6 = scn("bn6", [P, T4, 6])
        mv = scn("mv", [P, T4, 2])
        zst = scn("zst", [P, 4, T4])
        s1.close()

        h2h = ctx.enter_context(nc.sbuf_tensor("h2h", [P, KC, HB * L], f32r, side="right"))
        h2l = ctx.enter_context(nc.sbuf_tensor("h2l", [P, KC, HB * L], f32r, side="right"))

        s2 = ExitStack()
        att = arena(s2)
        bqk = att("bqk", [P, 2 * T4])
        bvb = att("bvb", [P, H])
        rope = att("rope", [P, 2, L])
        perm = att("perm", [P, P])
        rtw = att("rtw", [P, KC, ROUTE])
        rth = att("rth", [P, KC, ROUTE], f32r)
        rtl = att("rtl", [P, KC, ROUTE], f32r)
        XL = att("XL", [P, T4, H])
        hp = att("hp", [P, T4, H])
        h1h = att("h1h", [P, KC, L], f32r)
        h1l = att("h1l", [P, KC, L], f32r)
        QK = att("QK", [P, 2 * T4, L])
        V = att("V", [P, T4, H])
        EX = att("EX", [P, 2, 2, L])
        PT = att("PT", [P, 2, 2, L])
        QB, RC, RS = EX[:, 0], EX[:, 1], PT[:, 0]
        nm = att("nm", [P, 2, 2])
        nb = att("nb", [P, 2, 2])
        rs = att("rs", [P, T4, NH])
        ri = att("ri", [P, T4, NH])
        cn = att("cn", [P, H])
        cth = att("cth", [P, KC, P], f32r)
        ctl = att("ctl", [P, KC, P], f32r)
        sq = cn
        hw = att("hw", [P, KC, P])
        ss = att("ss", [P, T4])
        abn = att("abn", [P, T4, 6])
        amv = att("amv", [P, T4, 2])
        ast = att("ast", [P, 8, T4])
        r2 = att("r2", [P, 3, T4])
        lg = att("lg", [P, T4, ROUTE])
        pr = att("pr", [P, 3, T4, NE])
        gs = att("gs", [P, 4, T4])
        m8 = att("m8", [P, T4, 8])
        i8 = att("i8", [P, T4, 8], u32)
        i8f = att("i8f", [P, T4, 2])
        cc = att("cc", [P, 2, T4, NE])
        s2.close()
        sa.close()

        s3 = ExitStack()
        exa = arena(s3)
        wgr = exa("wgr", [P, GW])
        wdr = exa("wdr", [P, DW])
        wgh = exa("wgh", [P, KC, 2 * EI], f32r)
        wgl = exa("wgl", [P, KC, 2 * EI], f32r)
        wdh = exa("wdh", [P, NCH, H], f32r)
        wdl = exa("wdl", [P, NCH, H], f32r)
        fah = exa("fah", [P, NCH, HB * L], f32r)
        fal = exa("fal", [P, NCH, HB * L], f32r)
        ft = exa("ft", [P, 2, L])
        fp = exa("fp", [P, 2, L])
        fa = exa("fa", [P, 2, L])
        s3.close()

        A01 = pb("A01", [P, 2, L])
        A23 = pb("A23", [P, 2, L])
        A45 = pb("A45", [P, 2, L])
        A67 = pb("A67", [P, 2, L])
        bank = [t[:, k, :] for t in (A01, A23, A45, A67) for k in range(2)]
        Q = bank[0:4]
        DA = bank[4:6]
        HT = bank[6:8]
        SB = [A01, A23]
        PB = A45
        CX, WK = bank[6], bank[7]
        FG, FU, FD = bank[0:2], bank[2:4], bank[4:6]

        const_in = sem("const_in")
        x_in_s = [sem(f"x_loaded{h}") for h in range(2)]
        ctx_in_s = [sem(f"ctx_loaded{h}") for h in range(2)]
        consts = sem("consts")
        scanw_in = [sem(f"scan_weights_loaded{h}") for h in range(2)]
        ddiag_s = sem("ddiag_made")
        rows_made = sem("rows_of_constants_made")
        z_bn, z_mv, z_norm, z_n, z_t, z_done = [sem("z_" + n) for n in
                                                ("stats", "meanvar", "norm", "normed", "tanh", "done")]
        xp_mm, cv_init, cv_tap, u_t, u_done = [sem(n) for n in
                                               ("inproj_ready", "conv_started", "conv_tap", "u_tanh", "u_done")]
        xd_mm, xd_ready, b_stored = sem("xdbl_product"), sem("xdbl_ready"), sem("b_stored")
        bb_in = [sem("b_rows_loaded0"), sem("b_rows_loaded1")]
        ct_mm, ct_ready = sem("c_transposed"), sem("c_ready")
        dt_mm, dt_abs, dt_rel, dt_e, dt_l, dl_done, du_done = [sem("delta_" + n) for n in
                                                               ("product", "abs", "relu", "exp", "log", "done", "times_u")]
        yi_mm, yi_done, zT_ready = sem("du_term_product"), sem("y_started"), sem("z_transposed")
        dA_ready, gb_ready, scan_done = sem("decay_ready"), sem("input_ready"), sem("scan_done")
        hT_ready, y_acc, y_z, x1_done = sem("states_transposed"), sem("y_added"), sem("y_gated"), sem("x1_done")
        wraw_in, wah_done, wal_done = sem("att_weights_loaded"), sem("att_weights_hi"), sem("att_weights_lo")
        attc_in = [sem(f"att_consts_loaded{h}") for h in range(2)]
        rt_split = sem("router_split")
        a_bn, a_mv, a_norm, a_xl, a_hp = [sem("att_" + n) for n in ("stats", "meanvar", "norm", "normed", "scaled")]
        h1_mm, h1_hi, h1_lo = sem("h1_transposed"), sem("h1_hi"), sem("h1_lo")
        v_mm, v_done = sem("v_product"), sem("v_ready")
        qk_mm, qb_ready, rot_mm, rope_c, rope_s, qk_done = [sem(n) for n in
                                                            ("qk_product", "qk_biased", "qk_rotated", "rope_cos", "rope_sin", "qk_ready")]
        s_mm, mx_raw, mx_done, ex_done = sem("scores_ready"), sem("row_max"), sem("row_max_scaled"), sem("probs_ready")
        t_mm, pt_a, pt_b, pv_mm = sem("probs_transposed"), sem("probs_copied_even"), sem("probs_copied_odd"), sem("pv_ready")
        ri_done, cn_done, ct2_mm, cth_done, ctl_done = [sem(n) for n in
                                                        ("row_sum_inverse", "context_normed", "context_transposed", "context_hi", "context_lo")]
        wo_mm, xm_done, xacc_done, sq_done, r2_s, hp2_done = [sem(n) for n in
                                                              ("wo_product", "residual_done", "residual_summed", "square_sum", "rms2", "h2_scaled")]
        h2_mm, hw_done, h2h_done, h2l_done, h2h_kept, h2l_kept, rt_mm, lg_done = [
            sem(n) for n in ("h2_transposed", "h2_weighted", "h2_hi", "h2_lo", "h2_hi_kept", "h2_lo_kept",
                             "router_product", "logits_ready")]
        gt, gt_e, gt_t, att_done = sem("gating_step"), sem("gating_exp"), sem("gating_tanh"), sem("attention_done")
        wg_in, wd_in = sem("gate_up_loaded"), sem("down_loaded")
        wgh_s, wgl_s, wdh_s, wdl_s = sem("gate_up_hi"), sem("gate_up_lo"), sem("down_hi"), sem("down_lo")
        gu_mm, f_t, f_p, f_a, f_ah, f_al = [sem(n) for n in
                                            ("gate_up_product", "gate_tanh", "gate_done", "act_ready", "act_hi", "act_lo")]
        d_mm, d_acc, stored = sem("down_product"), sem("down_added"), sem("out_stored")

        C_X1 = 4
        C_BST = 16
        C_ZT = 1
        C_SC = 8
        C_HT = 8
        C_YA = 4
        C_GB = 4
        C_WL = 1
        C_DA = 8
        C2 = 2
        C1 = 1

        NL = 4
        GT = 27
        block = ctx.enter_context(nc.Block())

        def wait_apart(e, what, value):
            e.wait_ge(const_in, 96)
            e.wait_ge(what, value)

        def scan_ended(e, half):
            e.wait_ge(x1_done, T4 * HB * (half + 1) + C_X1)
            e.wait_ge(wal_done, KC * (half + 1) + C_WL)

        def attention_ended(e, half):
            e.wait_ge(att_done, HB * (half + 1) + C1)
            e.wait_ge(h2h_kept, T4 * HB * (half + 1))
            e.wait_ge(h2l_kept, T4 * HB * (half + 1))

        def experts_ended(e, half):
            e.wait_ge(d_acc, NU * TH * (half + 1) + C_DA)

        @block.sync
        def _(sp):
            sp.sem_inc(b_stored, C_BST)

            def load_consts():
                for dst, src in ((ident[:], ident_in), (mask[:], mask_in), (chan[:], chan_in),
                                 (gates[:], gates_in.partition_broadcast(P)), (wln[:], wln_in),
                                 (iota8[:], iota_in.partition_broadcast(P))):
                    sp.dma_start(dst, src).then_inc(const_in, 16)

            def scan_stage(half):
                if half:
                    experts_ended(sp, half - 1)
                sp.dma_start(cT[:], ctx_in[half]).then_inc(ctx_in_s[half], 16)
                for dst, src in ((w_in[:], w_in_in), (xproj[:], xproj_in), (dtproj[:], dtproj_in)):
                    sp.dma_start(dst, src).then_inc(scanw_in[half], 16)
                if half == 0:
                    load_consts()
                    for h in range(2):
                        sp.dma_start(xs[:, h * TH:(h + 1) * TH, :], x_in[h]).then_inc(x_in_s[h], 16)
                with sp.Fori(HB * half, HB * half + HB) as g:
                    for c in range(KC // HB):
                        sp.wait_ge(wal_done, (KC // HB) * g + c + C_WL)
                        sp.dma_start(wraw[:], watt_in[:, (g - HB * half) * (KC // HB) + c, :]
                                     ).then_inc(wraw_in, 16)
                    sp.wait_ge(xd_ready, g + 1)
                    sp.dma_start(b_scratch[g], xd[DR:DR + NS, :]).then_inc(b_stored, 16)
                    with sp.Fori(0, NS // NL) as i:
                        sp.wait_ge(b_stored, 16 * g + 16 + C_BST)
                        for s in range(2):
                            sp.wait_ge(gb_ready, NS * g + NL * i + 2 * s - 2 + C_GB)
                            sp.dma_start(BB[:, s], b_scratch[g, ds(NL * i + 2 * s, 2), :]
                                         .partition_broadcast(P)).then_inc(bb_in[s], 16)

            def attention_stage(half):
                scan_ended(sp, half)
                for dst, src in ((bqk[:], bqk_in), (bvb[:], bv_in.partition_broadcast(P)),
                                 (rope[:], rope_in), (perm[:], perm_in), (rtw[:], route_in)):
                    sp.dma_start(dst, src).then_inc(attc_in[half], 16)

            def expert_stage(half):
                attention_ended(sp, half)
                with sp.Fori(NU * half, NU * half + NU) as k:
                    u = k - NU * half
                    sp.wait_ge(wgl_s, k + C1)
                    sp.dma_start(wgr[:], wffn_in[u, :, 0:GW]).then_inc(wg_in, 16)
                    sp.wait_ge(wdl_s, k + C1)
                    sp.dma_start(wdr[:], wffn_in[u, :, GW:GW + DW]).then_inc(wd_in, 16)
                experts_ended(sp, half)
                sp.dma_start(out[half], xs[:, half * TH:(half + 1) * TH, :]).then_inc(stored, 16)

            for half in range(2):
                scan_stage(half)
                attention_stage(half)
                expert_stage(half)
            sp.wait_ge(stored, 32)

        @block.tensor
        def _(pe):
            pe.sem_inc(hT_ready, C_HT)
            pe.sem_inc(zT_ready, C_ZT)
            for s in (rot_mm, t_mm, pv_mm):
                pe.sem_inc(s, C2)
            for s in (gu_mm, d_mm):
                pe.sem_inc(s, C1)

            def split_product(out_, parts, rhs_parts, n):
                for k in range(n):
                    for j, (a, b) in enumerate(((0, 0), (0, 1), (1, 0))):
                        mm = nc.tensor.matmul(out_, parts[a](k), rhs_parts[b](k),
                                              start=(k == 0 and j == 0), stop=(k == n - 1 and j == 2))
                return mm

            def scan_stage(half):
                pe.wait_ge(ctx_in_s[half], 16)
                pe.wait_ge(scanw_in[half], 48)
                if half == 0:
                    pe.wait_ge(const_in, 96)
                pe.wait_ge(ddiag_s, T4 * (half + 1))
                with pe.Fori(HB * half, HB * half + HB) as g:
                    for et in range(T4):
                        pe.wait_ge(x1_done, T4 * g + et + 1 - T4 + C_X1)
                        for k in range(DC // P):
                            mm = nc.tensor.matmul(Q[et], w_in[:, k, et * P:(et + 1) * P],
                                                  cT[:, ds(g - HB * half, 1), k, :],
                                                  start=(k == 0), stop=(k == DC // P - 1))
                        mm.then_inc(xp_mm, 1)
                    pe.wait_ge(u_done, g + 1)
                    for et in range(T4):
                        mm = nc.tensor.matmul(Q[0][0:DR + 2 * NS, :], xproj[:, et, :], U2[:, et, :],
                                              start=(et == 0), stop=(et == T4 - 1))
                    mm.then_inc(xd_mm, 1)
                    wait_apart(pe, xd_ready, g + 1)
                    n3 = DR + 2 * NS
                    for tt in range(T4):
                        mm = nc.tensor.transpose(Q[1][:, tt * n3:(tt + 1) * n3],
                                                 xd[:, tt * P:(tt + 1) * P], ident[0:n3, 0:n3])
                    mm.then_inc(ct_mm, 1)
                    for et in range(T4):
                        if et == 3:
                            pe.wait_ge(ct_ready, g + 1)
                        nc.tensor.matmul(Q[(et + 2) % T4], dtproj[:, et * P:(et + 1) * P], xd[0:DR, :],
                                         start=True, stop=True).then_inc(dt_mm, 1)
                    pe.wait_ge(dt_rel, T4 * g + T4)
                    for tt in range(T4):
                        for et in range(T4):
                            mm = nc.tensor.matmul(Q[tt][:, et * P:(et + 1) * P],
                                                  U2[:, et, tt * P:(tt + 1) * P], ddiag[:, et, :],
                                                  start=True, stop=True)
                        mm.then_inc(yi_mm, 1)
                    pe.wait_ge(z_done, g + 1)
                    for tt in range(T4):
                        pe.wait_ge(yi_done, T4 * g + tt + 1)
                        for rt in range(T4):
                            mm = nc.tensor.transpose(Q[tt][:, rt * P:(rt + 1) * P],
                                                     ZS[:, rt, tt * P:(tt + 1) * P], ident[:])
                        mm.then_inc(zT_ready, 1)
                    with pe.Fori(0, NS // NL) as i:
                        for n in range(NL):
                            step = NS * g + NL * i + n
                            pe.wait_ge(scan_done, T4 * step + T4 + C_SC)
                            for tt in range(T4):
                                pe.wait_ge(y_acc, T4 * step + tt - 1 + C_YA)
                                for et in range(T4):
                                    mm = nc.tensor.transpose(HT[tt % 2][:, et * P:(et + 1) * P],
                                                             HS[:, n % 2, et, tt * P:(tt + 1) * P], ident[:])
                                mm.then_inc(hT_ready, 1)

            def attention_stage(half):
                scan_ended(pe, half)
                pe.wait_ge(attc_in[half], 80)
                pe.wait_ge(consts, 7)
                pe.wait_ge(rt_split, 2 * (half + 1))
                with pe.Fori(HB * half, HB * half + HB) as g:
                    U0 = 32 * g
                    pe.wait_ge(att_done, g + C1)
                    pe.wait_ge(a_hp, T4 * g + T4)
                    for k in range(KC):
                        for tt in range(T4):
                            mm = nc.tensor.transpose(bank[k][:, tt * P:(tt + 1) * P],
                                                     hp[:, tt, k * P:(k + 1) * P], ident[:])
                        mm.then_inc(h1_mm, 1)
                    pe.wait_ge(h1_hi, KC * g + KC)
                    pe.wait_ge(h1_lo, KC * g + KC)
                    for tt in range(T4):
                        split_product(bank[tt],
                                      [lambda k, w=w: w[:, k, tt * P:(tt + 1) * P] for w in (h1h, h1l)],
                                      [lambda k, w=w: w[:, k, 2 * H:3 * H] for w in (wah, wal)], KC
                                      ).then_inc(v_mm, 1)

                    def product(m):
                        pe.wait_ge(qb_ready, 8 * g + m - 1 + C2)
                        split_product(bank[4 + m % 2],
                                      [lambda k, w=w: w[:, k, m * P:(m + 1) * P] for w in (wah, wal)],
                                      [lambda k, w=w: w[:, k, :] for w in (h1h, h1l)], KC).then_inc(qk_mm, 1)

                    def rotate(m):
                        pe.wait_ge(qb_ready, 8 * g + m + 1 + C2)
                        pe.wait_ge(rope_s, 8 * g + m - 1 + C2)
                        nc.tensor.matmul(bank[6 + m % 2], perm[:], QB[:, m % 2, :], start=True,
                                         stop=True).then_inc(rot_mm, 1)

                    for m in range(8):
                        product(m)
                        if m:
                            rotate(m - 1)
                    rotate(7)

                    def scores(u):
                        i, hpair = divmod(u, NH // 2)
                        W = P * (i + 1)
                        if u == 0:
                            pe.wait_ge(v_done, T4 * g + T4)
                            pe.wait_ge(qk_done, 8 * g + 8 + C2)
                        pe.wait_ge(ex_done, U0 + u - 1 + C2)
                        for a in range(2):
                            h = 2 * hpair + a
                            r, m = HD * (h % 4), h // 4
                            nc.tensor.matmul(SB[u % 2][:, a, 0:W], QK[r:r + HD, m, i * P:(i + 1) * P],
                                             QK[r:r + HD, 4 + m, 0:W], start=True, stop=False)
                            mm = nc.tensor.matmul(SB[u % 2][:, a, W - P:W], identb[:], maskb[:],
                                                  start=False, stop=True)
                        mm.then_inc(s_mm, 1)

                    def turn(u):
                        i = u // (NH // 2)
                        pe.wait_ge(ex_done, U0 + u + 1 + C2)
                        pe.wait_ge(pt_a, U0 + u + C1)
                        pe.wait_ge(pt_b, U0 + u + C1)
                        for a in range(2):
                            for kb in range(i + 1):
                                mm = nc.tensor.transpose(PB[:, a, kb * P:(kb + 1) * P],
                                                         EX[:, u % 2, a, kb * P:(kb + 1) * P], ident[:])
                        mm.then_inc(t_mm, 1)

                    def weigh(u):
                        i, hpair = divmod(u, NH // 2)
                        pe.wait_ge(pt_a, U0 + u + 1 + C1)
                        pe.wait_ge(pt_b, U0 + u + 1 + C1)
                        if hpair == 0:
                            pe.wait_ge(cn_done, T4 * g + i + C1)
                        for a in range(2):
                            h = 2 * hpair + a
                            for kb in range(i + 1):
                                mm = nc.tensor.matmul(CX[:, h * HD:(h + 1) * HD],
                                                      PT[:, u % 2, a, kb * P:(kb + 1) * P],
                                                      V[:, kb, h * HD:(h + 1) * HD],
                                                      start=(kb == 0), stop=(kb == i))
                        mm.then_inc(pv_mm, 1)

                    def finish(i, step):
                        t = T4 * g + i
                        if step == 0:
                            pe.wait_ge(cn_done, t + 1 + C1)
                            pe.wait_ge(lg_done, t + C1)
                            for k in range(KC):
                                mm = nc.tensor.transpose(WK[:, k * P:(k + 1) * P],
                                                         cn[:, k * P:(k + 1) * P], ident[:])
                            mm.then_inc(ct2_mm, 1)
                        if step == 1:
                            pe.wait_ge(cth_done, t + 1)
                            pe.wait_ge(ctl_done, t + 1)
                            split_product(WK, [lambda k, w=w: w[:, k, :] for w in (cth, ctl)],
                                          [lambda k, w=w: w[:, k, 3 * H:4 * H] for w in (wah, wal)], KC
                                          ).then_inc(wo_mm, 1)
                        if step == 2:
                            pe.wait_ge(hp2_done, t + 1)
                            for k in range(KC):
                                mm = nc.tensor.transpose(WK[:, k * P:(k + 1) * P],
                                                         hp[:, i, k * P:(k + 1) * P], ident[:])
                            mm.then_inc(h2_mm, 1)
                        if step == 3:
                            pe.wait_ge(h2h_done, t + 1)
                            pe.wait_ge(h2l_done, t + 1)
                            split_product(WK[:, 0:ROUTE],
                                          [lambda k, w=w: w[:, k, :] for w in (cth, ctl)],
                                          [lambda k, w=w: w[:, k, :] for w in (rth, rtl)], KC
                                          ).then_inc(rt_mm, 1)

                    scores(0)
                    for u in range(32):
                        if u < 31:
                            scores(u + 1)
                        turn(u)
                        if u:
                            weigh(u - 1)
                        if u >= 8 and u % 8 in (1, 2, 4, 6):
                            finish(u // 8 - 1, (1, 2, 4, 6).index(u % 8))
                    weigh(31)
                    for step in range(4):
                        finish(3, step)

            def expert_stage(half):
                attention_ended(pe, half)
                with pe.Fori(NU * half, NU * half + NU) as k:
                    pe.wait_ge(wgh_s, k + 1)
                    pe.wait_ge(wgl_s, k + 1 + C1)
                    for s in range(NG * NCH):
                        grp, c = divmod(s, NCH)
                        pe.wait_ge(f_a, NG * NCH * k + s - 1 + C2)
                        for o, bk in ((0, FG), (EI, FU)):
                            mm = split_product(bk[s % 2][0:CW[c], :],
                                               [lambda j, w=w: w[:, j, o + c * P:o + c * P + CW[c]] for w in (wgh, wgl)],
                                               [lambda j, w=w: w[:, j, grp * L:(grp + 1) * L] for w in (h2h, h2l)], KC)
                        mm.then_inc(gu_mm, 1)
                    pe.wait_ge(wdh_s, k + 1)
                    pe.wait_ge(wdl_s, k + 1 + C1)
                    for tt in range(TH):
                        if tt % T4 == 0:
                            pe.wait_ge(f_ah, NG * NCH * k + NCH * (tt // T4 + 1) + C2)
                            pe.wait_ge(f_al, NG * NCH * k + NCH * (tt // T4 + 1) + C2)
                        pe.wait_ge(d_acc, TH * k + tt - 1 + C_DA)
                        split_product(FD[tt % 2],
                                      [lambda c, w=w: w[0:CW[c], c, tt * P:(tt + 1) * P] for w in (fah, fal)],
                                      [lambda c, w=w: w[0:CW[c], c, :] for w in (wdh, wdl)], NCH
                                      ).then_inc(d_mm, 1)

            for half in range(2):
                scan_stage(half)
                attention_stage(half)
                expert_stage(half)

        @block.scalar
        def _(act):
            for s in (qb_ready, ex_done, f_ah):
                act.sem_inc(s, C2)
            act.sem_inc(pt_a, C1)

            def make_consts():
                act.wait_ge(const_in, 96)
                nc.scalar.activation(identb[:], ident[:], ACT.Copy).then_inc(consts, 1)
                nc.scalar.activation(maskb[:], mask[:], ACT.Copy).then_inc(consts, 1)
                nc.scalar.activation(tg[:, 0:2], gates[:], ACT.Tanh).then_inc(consts, 1)
                nc.scalar.activation(aneg[:], chan[:, :, TAPS + 3:], ACT.Exp).then_inc(consts, 1)
                act.wait_ge(consts, 4)
                nc.scalar.activation(aneg[:], aneg[:], ACT.Copy, scale=-1.0).then_inc(consts, 1)
                nc.scalar.activation(tg[:, 2:4], tg[:, 0:2], ACT.Copy, scale=0.5).then_inc(consts, 1)
                nc.scalar.activation(tgq[:], tg[:, 1:2], ACT.Copy, scale=0.25).then_inc(consts, 1)
                act.wait_ge(consts, 7)

            def scan_stage(half):
                if half:
                    experts_ended(act, half - 1)
                act.wait_ge(x_in_s[half], 16)
                with act.Fori(HB * half, HB * half + HB) as g:
                    act.wait_ge(z_norm, 4 * g + 4)
                    act.wait_ge(zT_ready, T4 * g + C_ZT)
                    for rt in range(T4):
                        nc.scalar.activation(ZS[:, rt, :], xs[:, ds(T4 * g + rt, 1), :], ACT.Identity,
                                             bias=zst[:, 3, rt:rt + 1], scale=zst[:, 1, rt:rt + 1]
                                             ).then_inc(z_n, 1)
                    act.wait_ge(z_n, T4 * g + T4)
                    nc.scalar.activation(T2, ZS[:], ACT.Tanh, scale=0.5).then_inc(z_t, 1)
                    for et in range(T4):
                        act.wait_ge(xp_mm, T4 * g + et + 1)
                        nc.scalar.activation(T1[:, et, :], Q[et], ACT.Identity,
                                             bias=chan[:, et, TAPS:TAPS + 1],
                                             scale=chan[:, et, TAPS - 1:TAPS]).then_inc(cv_init, 1)
                    for c in range(KC // HB):
                        act.wait_ge(wraw_in, 16 * ((KC // HB) * g + c + 1))
                        nc.scalar.activation(wah[:, ds((g - HB * half) * (KC // HB) + c, 1), :], wraw[:],
                                             ACT.Copy).then_inc(wah_done, 1)
                        if c == 0:
                            act.wait_ge(cv_tap, 12 * g + 12)
                            act.wait_ge(z_done, g + 1)
                            nc.scalar.activation(T2, T1, ACT.Tanh, scale=0.5).then_inc(u_t, 1)
                    act.wait_ge(xd_mm, g + 1)
                    act.wait_ge(b_stored, 16 * g + C_BST)
                    nc.scalar.activation(xd[:], Q[0][0:DR + 2 * NS, :], ACT.Copy, scale=0.5).then_inc(xd_ready, 1)
                    act.wait_ge(ct_mm, g + 1)
                    n3 = DR + 2 * NS
                    nc.scalar.activation(Ct[:], Q[1][:, 0:T4 * n3].rearrange("p (t n) -> p t n", n=n3)[:, :, DR + NS:n3],
                                         ACT.Copy).then_inc(ct_ready, 1)
                    for et in range(T4):
                        act.wait_ge(dt_mm, T4 * g + et + 1)
                        nc.scalar.activation(T1[:, et, :], Q[(et + 2) % T4], ACT.Abs,
                                             bias=chan[:, et, TAPS + 1:TAPS + 2]).then_inc(dt_abs, 1)
                        nc.scalar.activation(DL[:, et, :], Q[(et + 2) % T4], ACT.Relu,
                                             bias=chan[:, et, TAPS + 1:TAPS + 2]).then_inc(dt_rel, 1)
                    act.wait_ge(dt_abs, T4 * g + T4)
                    nc.scalar.activation(T1, T1, ACT.Exp, scale=-1.0).then_inc(dt_e, 1)
                    act.wait_ge(dt_e, g + 1)
                    nc.scalar.activation(T1, T1, ACT.Ln, bias=1.0).then_inc(dt_l, 1)
                    for tt in range(T4):
                        act.wait_ge(yi_mm, T4 * g + tt + 1)
                        nc.scalar.activation(YA[:, tt, :], Q[tt], ACT.Copy).then_inc(yi_done, 1)
                    act.wait_ge(dl_done, g + 1)
                    with act.Fori(0, NS // NL) as i:
                        for n in range(NL):
                            step = NS * g + NL * i + n
                            for et in range(T4):
                                act.wait_ge(scan_done, T4 * step + et - 1 + C_SC)
                                nc.scalar.activation(DA[et % 2], DL[:, et, :], ACT.Exp,
                                                     scale=aneg[:, et, ds(NL * i + n, 1)]).then_inc(dA_ready, 1)

            def attention_stage(half):
                scan_ended(act, half)
                act.wait_ge(attc_in[half], 80)
                nc.scalar.activation(rth[:], rtw[:], ACT.Copy).then_inc(rt_split, 1)
                with act.Fori(HB * half, HB * half + HB) as g:
                    U0 = 32 * g
                    act.wait_ge(a_norm, 8 * g + 8)
                    act.wait_ge(att_done, g + C1)
                    for tt in range(T4):
                        nc.scalar.activation(XL[:, tt, :], xs[:, ds(T4 * g + tt, 1), :], ACT.Identity,
                                             bias=ast[:, 2, tt:tt + 1], scale=ast[:, 1, tt:tt + 1]
                                             ).then_inc(a_xl, 1)
                    for tt in range(T4):
                        act.wait_ge(a_xl, T4 * g + tt + 1)
                        nc.scalar.activation(hp[:, tt, :], XL[:, tt, :], ACT.Copy,
                                             scale=ast[:, 6, tt:tt + 1]).then_inc(a_hp, 1)
                    for k in range(KC):
                        act.wait_ge(h1_mm, KC * g + k + 1)
                        nc.scalar.activation(h1h[:, k, :], bank[k], ACT.Copy, scale=wln[:, 0, k:k + 1]
                                             ).then_inc(h1_hi, 1)
                    for m in range(8):
                        act.wait_ge(qk_mm, 8 * g + m + 1)
                        act.wait_ge(rot_mm, 8 * g + m - 1 + C2)
                        act.wait_ge(rope_c, 8 * g + m - 1 + C2)
                        nc.scalar.activation(QB[:, m % 2, :], bank[4 + m % 2], ACT.Identity,
                                             bias=bqk[:, m:m + 1]).then_inc(qb_ready, 1)

                    def probs(u):
                        i, hpair = divmod(u, NH // 2)
                        W = P * (i + 1)
                        act.wait_ge(mx_done, U0 + u + 1)
                        act.wait_ge(t_mm, U0 + u - 1 + C2)
                        for a in range(2):
                            h = 2 * hpair + a
                            ins = nc.scalar.activation(EX[:, u % 2, a, 0:W], SB[u % 2][:, a, 0:W], ACT.Exp,
                                                       bias=nb[:, u % 2, a:a + 1], scale=SCALE,
                                                       accum_out=rs[:, i, h:h + 1])
                        ins.then_inc(ex_done, 1)

                    def copy_even(u):
                        W = P * (u // (NH // 2) + 1)
                        act.wait_ge(t_mm, U0 + u + 1 + C2)
                        act.wait_ge(pv_mm, U0 + u - 1 + C2)
                        nc.scalar.activation(PT[:, u % 2, 0, 0:W], PB[:, 0, 0:W], ACT.Copy).then_inc(pt_a, 1)

                    def finish(i, step):
                        t = T4 * g + i
                        if step == 0:
                            act.wait_ge(ct2_mm, t + 1)
                            nc.scalar.activation(cth[:], WK.rearrange("p (k t) -> p k t", k=KC), ACT.Copy
                                                 ).then_inc(cth_done, 1)
                        if step == 1:
                            act.wait_ge(xm_done, t + 1)
                            nc.scalar.activation(sq[:], XL[:, i, :], ACT.Square, accum_out=ss[:, i:i + 1]
                                                 ).then_inc(sq_done, 1)
                            act.wait_ge(r2_s, 3 * t + 3)
                            nc.scalar.activation(hp[:, i, :], XL[:, i, :], ACT.Copy,
                                                 scale=r2[:, 1, i:i + 1]).then_inc(hp2_done, 1)
                        if step == 2:
                            act.wait_ge(hw_done, t + 1)
                            nc.scalar.activation(cth[:], hw[:], ACT.Copy).then_inc(h2h_done, 1)
                            nc.scalar.activation(h2h[:, :, ds((g - HB * half) * L + i * P, P)], hw[:], ACT.Copy
                                                 ).then_inc(h2h_kept, 1)

                    for u in range(32):
                        probs(u)
                        if u:
                            copy_even(u - 1)
                        if u >= 8 and u % 8 in (2, 3, 5):
                            finish(u // 8 - 1, (2, 3, 5).index(u % 8))
                    copy_even(31)
                    for step in range(3):
                        finish(3, step)
                    act.wait_ge(gt, GT * g + 2)
                    nc.scalar.activation(pr[:, 1], pr[:, 0], ACT.Exp).then_inc(gt_e, 1)
                    nc.scalar.activation(gs[:, 3, :], lg[:, :, NE], ACT.Tanh, scale=0.5).then_inc(gt_t, 1)

            def expert_stage(half):
                attention_ended(act, half)
                with act.Fori(NU * half, NU * half + NU) as k:
                    S0 = NG * NCH * k
                    act.wait_ge(wg_in, 16 * k + 16)
                    act.wait_ge(gu_mm, S0 + C1)
                    nc.scalar.activation(wgh[:], wgr[:].rearrange("p (k n) -> p k n", k=KC), ACT.Copy
                                         ).then_inc(wgh_s, 1)

                    def round_act(s):
                        grp, c = divmod(s, NCH)
                        act.wait_ge(f_a, S0 + s + 1 + C2)
                        nc.scalar.activation(fah[0:CW[c], c, grp * L:(grp + 1) * L], fa[0:CW[c], s % 2, :],
                                             ACT.Copy).then_inc(f_ah, 1)

                    for s in range(NG * NCH):
                        c = s % NCH
                        act.wait_ge(gu_mm, S0 + s + 1 + C1)
                        act.wait_ge(f_p, S0 + s - 1 + C2)
                        nc.scalar.activation(ft[0:CW[c], s % 2, :], FG[s % 2][0:CW[c], :], ACT.Tanh, scale=0.5
                                             ).then_inc(f_t, 1)
                        if s:
                            round_act(s - 1)
                        if s == 1:
                            act.wait_ge(wd_in, 16 * k + 16)
                            act.wait_ge(d_mm, TH * k + C1)
                            nc.scalar.activation(wdh[:], wdr[:].rearrange("p (c n) -> p c n", c=NCH), ACT.Copy
                                                 ).then_inc(wdh_s, 1)
                    round_act(NG * NCH - 1)

            make_consts()
            for half in range(2):
                scan_stage(half)
                attention_stage(half)
                expert_stage(half)


        @block.vector
        def _(dve):
            dve.sem_inc(x1_done, C_X1)
            dve.sem_inc(scan_done, C_SC)
            dve.sem_inc(y_acc, C_YA)
            dve.sem_inc(d_acc, C_DA)
            for s in (rope_s, qk_done, f_p, f_a):
                dve.sem_inc(s, C2)
            for s in (pt_b, cn_done, lg_done, att_done):
                dve.sem_inc(s, C1)

            def stats(rows, six, two, s_six, s_two, g):
                for t in range(T4):
                    nc.vector.bn_stats(six[:, t, :], rows[:, ds(T4 * g + t, 1), :]).then_inc(s_six, 1)
                dve.wait_ge(s_six, (T4 + 1) * g + T4)
                nc.vector.memset(tick[:], 0.0).then_inc(s_six, 1)
                for t in range(T4):
                    nc.vector.bn_aggr(two[:, t, :], six[:, t, :]).then_inc(s_two, 1)

            def scan_stage(half):
                if half:
                    experts_ended(dve, half - 1)
                dve.wait_ge(const_in, 96)
                dve.wait_ge(consts, 7)
                dve.wait_ge(x_in_s[half], 16)
                for et in range(T4):
                    nc.vector.tensor_scalar(ddiag[:, et, :], ident[:], chan[:, et, TAPS + 2:TAPS + 3], 0.5,
                                            ALU.mult, ALU.mult).then_inc(ddiag_s, 1)
                with dve.Fori(HB * half, HB * half + HB) as g:
                    stats(xs, bn6, mv, z_bn, z_mv, g)
                    dve.wait_ge(z_t, g + 1)
                    nc.vector.scalar_tensor_tensor(ZS[:], T2, 1.0, ZS[:], ALU.add, ALU.mult).then_inc(z_done, 1)
                    for j in range(TAPS - 1):
                        sh = TAPS - 1 - (TAPS - 2 - j)
                        tap = TAPS - 1 - sh
                        for et in range(T4):
                            if j == 0:
                                dve.wait_ge(cv_init, T4 * g + et + 1)
                            else:
                                dve.wait_ge(cv_tap, 12 * g + T4 * (j - 1) + et + 1)
                            nc.vector.scalar_tensor_tensor(T1[:, et, sh:L], Q[et][:, 0:L - sh],
                                                           chan[:, et, tap:tap + 1], T1[:, et, sh:L],
                                                           ALU.mult, ALU.add).then_inc(cv_tap, 1)
                    dve.wait_ge(u_t, g + 1)
                    nc.vector.scalar_tensor_tensor(U2, T2, 1.0, T1, ALU.add, ALU.mult).then_inc(u_done, 1)
                    dve.wait_ge(dt_l, g + 1)
                    nc.vector.tensor_tensor(DL[:], DL[:], T1, ALU.add).then_inc(dl_done, 1)
                    dve.wait_ge(dl_done, g + 1)
                    nc.vector.scalar_tensor_tensor(DU[:], U2, 0.5, DL[:], ALU.mult, ALU.mult).then_inc(du_done, 1)
                    wait_apart(dve, yi_done, T4 * g + T4)
                    with dve.Fori(0, NS // NL) as i:
                        def scans(n):
                            step = NS * g + NL * i + n
                            dve.wait_ge(gb_ready, step + 1 + C_GB)
                            dve.wait_ge(hT_ready, T4 * step - T4 + C_HT)
                            for et in range(T4):
                                dve.wait_ge(dA_ready, T4 * step + et + 1)
                                nc.vector.tensor_tensor_scan(HS[:, n % 2, et, :], DA[et % 2], GB[:, n % 2, et, :],
                                                             0.0, ALU.mult, ALU.add).then_inc(scan_done, 1)

                        def sums(n):
                            step = NS * g + NL * i + n
                            for tt in range(T4):
                                dve.wait_ge(hT_ready, T4 * step + tt + 1 + C_HT)
                                dve.wait_ge(y_acc, T4 * step + tt - T4 + 1 + C_YA)
                                nc.vector.scalar_tensor_tensor(YA[:, tt, :], HT[tt % 2],
                                                               Ct[:, tt, ds(NL * i + n, 1)], YA[:, tt, :],
                                                               ALU.mult, ALU.add).then_inc(y_acc, 1)

                        scans(0)
                        for n in range(1, NL):
                            scans(n)
                            sums(n - 1)
                        sums(NL - 1)
                    for tt in range(T4):
                        dve.wait_ge(y_acc, T4 * NS * g + T4 * (NS - 1) + tt + 1 + C_YA)
                        dve.wait_ge(zT_ready, T4 * g + tt + 1 + C_ZT)
                        nc.vector.tensor_tensor(YA[:, tt, :], Q[tt], YA[:, tt, :], ALU.mult).then_inc(y_z, 1)
                    for tt in range(T4):
                        dve.wait_ge(y_z, T4 * g + tt + 1)
                        nc.vector.scalar_tensor_tensor(xs[:, ds(T4 * g + tt, 1), :], YA[:, tt, :], tg[:, 2:3],
                                                       xs[:, ds(T4 * g + tt, 1), :], ALU.mult, ALU.add
                                                       ).then_inc(x1_done, 1)

            def attention_stage(half):
                scan_ended(dve, half)
                dve.wait_ge(attc_in[half], 80)
                dve.wait_ge(rt_split, 2 * half + 1)
                nc.vector.tensor_tensor(rtl[:], rtw[:], rth[:].bitcast(f32), ALU.subtract).then_inc(rt_split, 1)
                with dve.Fori(HB * half, HB * half + HB) as g:
                    U0 = 32 * g
                    stats(xs, abn, amv, a_bn, a_mv, g)
                    for k in range(KC):
                        dve.wait_ge(h1_hi, KC * g + k + 1)
                        nc.vector.scalar_tensor_tensor(h1l[:, k, :], bank[k], wln[:, 0, k:k + 1],
                                                       h1h[:, k, :].bitcast(f32), ALU.mult, ALU.subtract
                                                       ).then_inc(h1_lo, 1)
                    for tt in range(T4):
                        dve.wait_ge(v_mm, T4 * g + tt + 1)
                        nc.vector.tensor_tensor(V[:, tt, :], bank[tt], bvb[:], ALU.add).then_inc(v_done, 1)
                    for m in range(8):
                        dve.wait_ge(rot_mm, 8 * g + m + 1 + C2)
                        dve.wait_ge(qk_done, 8 * g + m - 1 + C2)
                        nc.vector.tensor_tensor(RS[:, m % 2, :], bank[6 + m % 2], rope[:, 1, :], ALU.mult
                                                ).then_inc(rope_s, 1)
                        dve.wait_ge(rope_s, 8 * g + m + 1 + C2)
                        dve.wait_ge(rope_c, 8 * g + m + 1 + C2)
                        nc.vector.tensor_tensor(QK[:, m, :], RC[:, m % 2, :], RS[:, m % 2, :], ALU.add
                                                ).then_inc(qk_done, 1)

                    def row_max(u):
                        W = P * (u // (NH // 2) + 1)
                        dve.wait_ge(s_mm, U0 + u + 1)
                        nc.vector.tensor_reduce(nm[:, u % 2, :], SB[u % 2][:, :, 0:W], AX.X, ALU.max, negate=True
                                                ).then_inc(mx_raw, 1)
                        dve.wait_ge(mx_raw, U0 + u + 1)
                        nc.vector.tensor_scalar(nb[:, u % 2, :], nm[:, u % 2, :], SCALE, None, ALU.mult
                                                ).then_inc(mx_done, 1)

                    def copy_odd(u):
                        W = P * (u // (NH // 2) + 1)
                        dve.wait_ge(t_mm, U0 + u + 1 + C2)
                        dve.wait_ge(pv_mm, U0 + u - 1 + C2)
                        nc.vector.tensor_copy(PT[:, u % 2, 1, 0:W], PB[:, 1, 0:W]).then_inc(pt_b, 1)

                    def finish(i, step):
                        t = T4 * g + i
                        if step == 0:
                            dve.wait_ge(pv_mm, U0 + 8 * i + 8 + C2)
                            nc.vector.reciprocal(ri[:, i, :], rs[:, i, :]).then_inc(ri_done, 1)
                            dve.wait_ge(ri_done, t + 1)
                            nc.vector.tensor_tensor(cn[:].rearrange("p (h d) -> p h d", h=NH),
                                                    CX.rearrange("p (h d) -> p h d", h=NH),
                                                    ri[:, i, :].unsqueeze(2).broadcast_to([P, NH, HD]),
                                                    ALU.mult).then_inc(cn_done, 1)
                        if step == 1:
                            dve.wait_ge(cth_done, t + 1)
                            nc.vector.tensor_tensor(ctl[:], WK.rearrange("p (k t) -> p k t", k=KC),
                                                    cth[:].bitcast(f32), ALU.subtract).then_inc(ctl_done, 1)
                        if step == 2:
                            dve.wait_ge(wo_mm, t + 1)
                            nc.vector.tensor_tensor(XL[:, i, :], WK, XL[:, i, :], ALU.add).then_inc(xm_done, 1)
                            dve.wait_ge(xm_done, t + 1)
                            nc.vector.scalar_tensor_tensor(xs[:, ds(t, 1), :], XL[:, i, :], tg[:, 1:2],
                                                           xs[:, ds(t, 1), :], ALU.mult, ALU.add
                                                           ).then_inc(xacc_done, 1)
                        if step == 3:
                            dve.wait_ge(h2_mm, t + 1)
                            nc.vector.tensor_tensor(hw[:], WK.rearrange("p (k t) -> p k t", k=KC),
                                                    wln[:, 1, :].unsqueeze(2).broadcast_to([P, KC, P]),
                                                    ALU.mult).then_inc(hw_done, 1)
                        if step == 4:
                            dve.wait_ge(rt_mm, t + 1)
                            nc.vector.tensor_copy(lg[:, i, :], WK[:, 0:ROUTE]).then_inc(lg_done, 1)

                    for u in range(32):
                        row_max(u)
                        if u:
                            copy_odd(u - 1)
                        if u >= 8 and u % 8 in (1, 2, 3, 5, 7):
                            finish(u // 8 - 1, (1, 2, 3, 5, 7).index(u % 8))
                    copy_odd(31)
                    for step in range(5):
                        finish(3, step)

                    n = [GT * g]

                    def step_(ins):
                        n[0] = n[0] + 1
                        ins.then_inc(gt, 1)
                        dve.wait_ge(gt, n[0])

                    dve.wait_ge(lg_done, T4 * g + T4 + C1)
                    step_(nc.vector.tensor_reduce(gs[:, 0, :], lg[:, :, 0:NE], AX.X, ALU.max, negate=True))
                    step_(nc.vector.tensor_tensor(pr[:, 0], lg[:, :, 0:NE],
                                                  gs[:, 0, :].unsqueeze(2).broadcast_to([P, T4, NE]), ALU.add))
                    dve.wait_ge(gt_e, g + 1)
                    step_(nc.vector.tensor_reduce(gs[:, 1, :], pr[:, 1], AX.X, ALU.add))
                    step_(nc.vector.reciprocal(gs[:, 2, :], gs[:, 1, :]))
                    step_(nc.vector.tensor_tensor(pr[:, 2], pr[:, 1],
                                                  gs[:, 2, :].unsqueeze(2).broadcast_to([P, T4, NE]), ALU.mult))
                    nc.vector.memset(tick[:], 0.0).then_inc(gt, 1)
                    for t in range(T4):
                        nc.vector.max(m8[:, t, :], pr[:, 2, t, :]).then_inc(gt, 1)
                    n[0] = n[0] + 1 + T4
                    dve.wait_ge(gt, n[0])
                    nc.vector.memset(tick[:], 0.0).then_inc(gt, 1)
                    for t in range(T4):
                        nc.vector.max_index(i8[:, t, :], m8[:, t, :], pr[:, 2, t, :]).then_inc(gt, 1)
                    n[0] = n[0] + 1 + T4
                    dve.wait_ge(gt, n[0])
                    step_(nc.vector.tensor_copy(i8f[:], i8[:, :, 0:2]))
                    for t in range(T4):
                        for j in range(2):
                            step_(nc.vector.tensor_scalar(cc[:, j, t, :], iota8[:], i8f[:, t, j:j + 1],
                                                          m8[:, t, j:j + 1], ALU.is_equal, ALU.mult))
                    step_(nc.vector.tensor_tensor(cc[:, 0], cc[:, 0], cc[:, 1], ALU.add))
                    dve.wait_ge(gt_t, g + 1)
                    step_(nc.vector.tensor_scalar(gs[:, 0, :], gs[:, 3, :], 1.0, tgq[:, 0:1], ALU.add, ALU.mult))
                    step_(nc.vector.tensor_scalar(cmb[:, ds(T4 * g, T4), 0:NE], cc[:, 0], tg[:, 3:4], None, ALU.mult))
                    nc.vector.tensor_copy(cmb[:, ds(T4 * g, T4), NE:NU],
                                          gs[:, 0, :].unsqueeze(2).broadcast_to([P, T4, NU - NE])
                                          ).then_inc(att_done, 1)

            def expert_stage(half):
                attention_ended(dve, half)
                with dve.Fori(NU * half, NU * half + NU) as k:
                    S0 = NG * NCH * k
                    for s in range(NG * NCH):
                        rows = slice(0, CW[s % NCH])
                        dve.wait_ge(f_t, S0 + s + 1)
                        dve.wait_ge(f_a, S0 + s - 1 + C2)
                        nc.vector.scalar_tensor_tensor(fp[rows, s % 2, :], ft[rows, s % 2, :], 1.0,
                                                       FG[s % 2][rows, :], ALU.add, ALU.mult).then_inc(f_p, 1)
                        dve.wait_ge(f_p, S0 + s + 1 + C2)
                        dve.wait_ge(f_ah, S0 + s - 1 + C2)
                        dve.wait_ge(f_al, S0 + s - 1 + C2)
                        nc.vector.tensor_tensor(fa[rows, s % 2, :], FU[s % 2][rows, :], fp[rows, s % 2, :],
                                                ALU.mult).then_inc(f_a, 1)
                    for tt in range(TH):
                        dve.wait_ge(d_mm, TH * k + tt + 1 + C1)
                        dve.wait_ge(d_acc, TH * k + tt - TH + 1 + C_DA)
                        nc.vector.scalar_tensor_tensor(xs[:, TH * half + tt, :], FD[tt % 2],
                                                       cmb[:, TH * half + tt, ds(k - NU * half, 1)],
                                                       xs[:, TH * half + tt, :], ALU.mult, ALU.add
                                                       ).then_inc(d_acc, 1)

            for half in range(2):
                scan_stage(half)
                attention_stage(half)
                expert_stage(half)

        @block.gpsimd
        def _(pool):
            pool.sem_inc(gb_ready, C_GB)
            pool.sem_inc(wal_done, C_WL)
            pool.sem_inc(rope_c, C2)
            pool.sem_inc(f_al, C2)
            pool.sem_inc(wgl_s, C1)
            pool.sem_inc(wdl_s, C1)
            for row, value in ((mhalf, -0.5), (eps5, 1e-5), (eps6, 1e-6), (mone, -1.0), (perh, 1.0 / H)):
                nc.gpsimd.memset(row[:], value).then_inc(rows_made, 1)
            pool.wait_ge(rows_made, 5)

            def scan_stage(half):
                if half:
                    experts_ended(pool, half - 1)
                with pool.Fori(HB * half, HB * half + HB) as g:
                    pool.wait_ge(z_mv, T4 * g + T4)
                    nc.gpsimd.tensor_tensor(zst[:, 0, :], mv[:, :, 1], eps5[:], ALU.add).then_inc(z_norm, 1)
                    pool.wait_ge(z_norm, 4 * g + 1)
                    nc.gpsimd.tensor_tensor(zst[:, 1, :], zst[:, 0, :], mhalf[:], ALU.pow).then_inc(z_norm, 1)
                    pool.wait_ge(z_norm, 4 * g + 2)
                    nc.gpsimd.tensor_tensor(zst[:, 2, :], mv[:, :, 0], zst[:, 1, :], ALU.mult).then_inc(z_norm, 1)
                    pool.wait_ge(z_norm, 4 * g + 3)
                    nc.gpsimd.tensor_tensor(zst[:, 3, :], zst[:, 2, :], mone[:], ALU.mult).then_inc(z_norm, 1)
                    for c in range(KC // HB):
                        q = (KC // HB) * g + c
                        pool.wait_ge(wah_done, q + 1)
                        k = (g - HB * half) * (KC // HB) + c
                        nc.gpsimd.tensor_tensor(wal[:, ds(k, 1), :], wraw[:].unsqueeze(1),
                                                wah[:, ds(k, 1), :].bitcast(f32),
                                                ALU.subtract).then_inc(wal_done, 1)
                    with pool.Fori(0, NS // NL) as i:
                        pool.wait_ge(du_done, g + 1)
                        pool.wait_ge(yi_done, T4 * g + T4)
                        for n in range(NL):
                            step = NS * g + NL * i + n
                            if n % 2 == 0:
                                pool.wait_ge(bb_in[n // 2], 16 * ((NS // NL) * g + i + 1))
                            pool.wait_ge(scan_done, T4 * step - T4 + C_SC)
                            nc.gpsimd.tensor_tensor(GB[:, n % 2], DU[:],
                                                    BB[:, n // 2, n % 2, :].unsqueeze(1).broadcast_to([P, T4, L]),
                                                    ALU.mult).then_inc(gb_ready, 1)

            def attention_stage(half):
                scan_ended(pool, half)
                pool.wait_ge(attc_in[half], 80)
                with pool.Fori(HB * half, HB * half + HB) as g:
                    def norm(n, ins):
                        ins.then_inc(a_norm, 1)
                        pool.wait_ge(a_norm, 8 * g + n)

                    pool.wait_ge(a_mv, T4 * g + T4)
                    var, mean = amv[:, :, 1], amv[:, :, 0]
                    norm(1, nc.gpsimd.tensor_tensor(ast[:, 0, :], var, eps5[:], ALU.add))
                    norm(2, nc.gpsimd.tensor_tensor(ast[:, 1, :], ast[:, 0, :], mhalf[:], ALU.pow))
                    norm(3, nc.gpsimd.tensor_tensor(ast[:, 3, :], mean, ast[:, 1, :], ALU.mult))
                    norm(4, nc.gpsimd.tensor_tensor(ast[:, 2, :], ast[:, 3, :], mone[:], ALU.mult))
                    norm(5, nc.gpsimd.tensor_tensor(ast[:, 4, :], ast[:, 1, :], ast[:, 1, :], ALU.mult))
                    norm(6, nc.gpsimd.tensor_tensor(ast[:, 5, :], var, ast[:, 4, :], ALU.mult))
                    norm(7, nc.gpsimd.tensor_tensor(ast[:, 7, :], ast[:, 5, :], eps6[:], ALU.add))
                    norm(8, nc.gpsimd.tensor_tensor(ast[:, 6, :], ast[:, 7, :], mhalf[:], ALU.pow))
                    for m in range(8):
                        pool.wait_ge(qb_ready, 8 * g + m + 1 + C2)
                        pool.wait_ge(qk_done, 8 * g + m - 1 + C2)
                        nc.gpsimd.tensor_tensor(RC[:, m % 2, :], QB[:, m % 2, :], rope[:, 0, :], ALU.mult
                                                ).then_inc(rope_c, 1)
                    for i in range(T4):
                        t = T4 * g + i
                        pool.wait_ge(sq_done, t + 1)
                        nc.gpsimd.tensor_tensor(r2[:, 2, i:i + 1], ss[:, i:i + 1], perh[:, 0:1], ALU.mult
                                                ).then_inc(r2_s, 1)
                        pool.wait_ge(r2_s, 3 * t + 1)
                        nc.gpsimd.tensor_tensor(r2[:, 0, i:i + 1], r2[:, 2, i:i + 1], eps6[:, 0:1], ALU.add
                                                ).then_inc(r2_s, 1)
                        pool.wait_ge(r2_s, 3 * t + 2)
                        nc.gpsimd.tensor_tensor(r2[:, 1, i:i + 1], r2[:, 0, i:i + 1], mhalf[:, 0:1], ALU.pow
                                                ).then_inc(r2_s, 1)
                        pool.wait_ge(h2h_done, t + 1)
                        nc.gpsimd.tensor_tensor(h2l[:, :, ds((g - HB * half) * L + i * P, P)], hw[:],
                                                cth[:].bitcast(f32), ALU.subtract).then_inc(h2l_kept, 1)
                        nc.gpsimd.tensor_tensor(ctl[:], hw[:], cth[:].bitcast(f32), ALU.subtract
                                                ).then_inc(h2l_done, 1)

            def expert_stage(half):
                attention_ended(pool, half)
                with pool.Fori(NU * half, NU * half + NU) as k:
                    S0 = NG * NCH * k
                    pool.wait_ge(wgh_s, k + 1)
                    nc.gpsimd.tensor_tensor(wgl[:], wgr[:].rearrange("p (k n) -> p k n", k=KC),
                                            wgh[:].bitcast(f32), ALU.subtract).then_inc(wgl_s, 1)
                    for s in range(NG * NCH):
                        grp, c = divmod(s, NCH)
                        pool.wait_ge(f_ah, S0 + s + 1 + C2)
                        cols = slice(grp * L, (grp + 1) * L)
                        nc.gpsimd.tensor_tensor(fal[0:CW[c], c, cols], fa[0:CW[c], s % 2, :],
                                                fah[0:CW[c], c, cols].bitcast(f32), ALU.subtract).then_inc(f_al, 1)
                        if s == 1:
                            pool.wait_ge(wdh_s, k + 1)
                            nc.gpsimd.tensor_tensor(wdl[:], wdr[:].rearrange("p (c n) -> p c n", c=NCH),
                                                    wdh[:].bitcast(f32), ALU.subtract).then_inc(wdl_s, 1)

            for half in range(2):
                scan_stage(half)
                attention_stage(half)
                expert_stage(half)


def host_layout(inputs):
    a = {k: np.asarray(v) for k, v in inputs.items()}
    f = np.float32

    def rows(w, k):
        return w.reshape(k, P, -1).transpose(1, 0, 2)

    x = a["x"].reshape(2, HB, T4, P, H).transpose(0, 3, 1, 2, 4).reshape(2, P, TH, H)
    c = a["ctx_1024"].reshape(2, HB, L, DC // P, P).transpose(0, 4, 1, 3, 2)
    chan = np.concatenate([a["L0_xattn_conv_w"], a["L0_xattn_conv_b"][:, None], a["L0_xattn_dt_proj_b"][:, None],
                           a["L0_xattn_D"][:, None], a["L0_xattn_A_log"]], axis=1)
    bqk = np.concatenate([a["L0_ffn_bq"].reshape(T4, P).T, a["L0_ffn_bk"].reshape(T4, P).T], axis=1)
    watt = np.concatenate([a["L0_ffn_wq"], a["L0_ffn_wk"], a["L0_ffn_wv"], a["L0_ffn_wo"]], axis=1)
    route = np.concatenate([a["L0_ffn_w_router"], a["L0_ffn_w_sh_eg"], np.zeros((H, 1), f)], axis=1)
    wln = np.stack([a["L0_ffn_w_ln1"].reshape(KC, P).T, a["L0_ffn_w_ln2"].reshape(KC, P).T], axis=1)

    def units(experts, shared, axis):
        return np.concatenate([experts, np.stack(np.split(shared, NU - NE, axis=axis))], axis=0)

    gate = units(a["L0_ffn_w_gate_e"], a["L0_ffn_w_sh_gate"], 1)
    up = units(a["L0_ffn_w_up_e"], a["L0_ffn_w_sh_up"], 1)
    down = units(a["L0_ffn_w_down_e"], a["L0_ffn_w_sh_down"], 0)
    gu = np.concatenate([gate, up], axis=2).reshape(NU, KC, P, 2 * EI).transpose(0, 2, 1, 3).reshape(NU, P, GW)
    dn = np.concatenate([down, np.zeros((NU, NCH * P - EI, H), f)], axis=1)
    dn = dn.reshape(NU, NCH, P, H).transpose(0, 2, 1, 3).reshape(NU, P, DW)

    inv = (f(1.0) / np.power(f(1000000.0), np.arange(0, HD, 2, dtype=f) / f(HD))).astype(f)
    ang = (np.arange(L, dtype=f)[:, None] * inv[None, :]).astype(f).T
    cos, sin = np.cos(ang).astype(f), np.sin(ang).astype(f)
    rope = np.stack([np.tile(np.concatenate([cos, cos]), (P // HD, 1)),
                     np.tile(np.concatenate([-sin, sin]), (P // HD, 1))], axis=1)
    d = np.arange(P)
    perm = np.zeros((P, P), f)
    perm[d, d ^ (HD // 2)] = 1.0
    q = np.arange(P)
    mask = np.where(q[None, :] <= q[:, None], f(0.0), f(MASKED)).astype(f)
    arrays = {
        "x_in": x, "ctx_in": c, "gates_in": np.concatenate([a["g_xattn"], a["g_ffn"]]),
        "w_in_in": rows(a["L0_xattn_in_proj_w"].T, DC // P), "chan_in": rows(chan, T4),
        "xproj_in": rows(a["L0_xattn_x_proj_w"].T, T4), "dtproj_in": a["L0_xattn_dt_proj_w"].T,
        "watt_in": rows(watt, KC), "bqk_in": bqk, "bv_in": a["L0_ffn_bv"], "wln_in": wln,
        "route_in": rows(route, KC), "wffn_in": np.concatenate([gu, dn], axis=2),
        "rope_in": rope, "perm_in": perm, "ident_in": np.eye(P, dtype=f), "mask_in": mask,
        "iota_in": np.arange(NE, dtype=f),
    }
    return {k: np.ascontiguousarray(v) for k, v in arrays.items()}


def kernel(**inputs):
    import concourse.bacc as bacc
    from concourse.bass_utils import run_bass_kernel_spmd

    nc = bacc.Bacc("TRN2", target_bir_lowering=False, num_devices=1, dynamic_dma_scratch_size=1024)
    arrays = host_layout(inputs)
    args = [nc.dram_tensor(n, v.shape, mybir.dt.from_np(v.dtype), kind="ExternalInput").ap()
            for n, v in arrays.items()]
    out = nc.dram_tensor("out", (2, P, TH, H), mybir.dt.float32, kind="ExternalOutput").ap()
    b_scratch = nc.dram_tensor("b_scratch", (B, NS, L), mybir.dt.float32).ap()
    build(nc, *args, out, b_scratch)
    r = run_bass_kernel_spmd(nc, [arrays], core_ids=[0])
    got = r.results[0]["out"]
    return got.reshape(2, P, HB, T4, H).transpose(0, 2, 3, 1, 4).reshape(B, L, H)
```

```python
import numpy as np
from contextlib import ExitStack

import concourse.bass as bass
from concourse import mybir

B, L, H = 4, 512, 512
DC = 256
DI, NS, DR = 512, 16, 16
TAPS = 4
NH, HD = 16, 32
NE, EI = 8, 352
NU = 12
P = 128
T4 = L // P
KC = H // P
HB = 2
TH = HB * T4
CW = [128, 128, 96]
NCH = len(CW)
NG = HB
GW = KC * 2 * EI
DW = NCH * H
ROUTE = 10

MASKED = -3.0e38


def build(nc, x_in, ctx_in, gates_in, w_in_in, chan_in, xproj_in, dtproj_in, watt_in, bqk_in,
          bv_in, wln_in, route_in, wffn_in, rope_in, perm_in, ident_in, mask_in, iota_in, out,
          b_scratch):
    f32, f32r, bf16, u32 = (mybir.dt.float32, mybir.dt.float32r, mybir.dt.bfloat16,
                            mybir.dt.uint32)
    ALU, ACT, AX = mybir.AluOpType, mybir.ActivationFunctionType, mybir.AxisListType
    ds = bass.ds
    SCALE = float(HD) ** -0.5

    ctx = ExitStack()
    with ctx:
        def sem(name):
            return ctx.enter_context(nc.semaphore(name))

        def pb(name, shape):
            return ctx.enter_context(nc.psum_tensor(name, shape, f32))

        def arena(stack):
            return lambda name, shape, dt=f32: stack.enter_context(nc.sbuf_tensor(name, shape, dt))

        keep = arena(ctx)
        xs = keep("xs", [P, B * T4, H])
        ident = keep("ident", [P, P])
        identb = keep("identb", [P, P], bf16)
        mask = keep("mask", [P, P])
        maskb = keep("maskb", [P, P], bf16)
        chan = keep("chan", [P, T4, TAPS + 3 + NS])
        aneg = keep("aneg", [P, T4, NS])
        gates = keep("gates", [P, 2])
        tg = keep("tg", [P, 4])
        tgq = keep("tgq", [P, 1])
        mhalf, eps5, eps6, mone, perh = [keep(n, [P, T4]) for n in ("mhalf", "eps5", "eps6", "mone", "perh")]
        tick = keep("tick", [P, 1])
        wln = keep("wln", [P, 2, KC])
        cmb = keep("cmb", [P, B * T4, NU])
        iota8 = keep("iota8", [P, NE])
        lg = keep("lg", [P, TH, ROUTE])
        pr = keep("pr", [P, 3, TH, NE])
        gs = keep("gs", [P, 4, TH])
        m8 = keep("m8", [P, TH, 8])
        i8 = keep("i8", [P, TH, 8], u32)
        i8f = keep("i8f", [P, TH, 2])
        cc = keep("cc", [P, 2, TH, NE])

        sa = ExitStack()
        mid = arena(sa)
        wah = mid("wah", [P, KC, 4 * H], f32r)
        wal = mid("wal", [P, KC, 4 * H], f32r)

        s1 = ExitStack()
        scn = arena(s1)
        wraw = scn("wraw", [P, 4 * H])
        w_in = scn("w_in", [P, DC // P, DI])
        xproj = scn("xproj", [P, T4, DR + 2 * NS])
        dtproj = scn("dtproj", [DR, DI])
        ddiag = scn("ddiag", [P, T4, P])
        cT = scn("cT", [P, HB, DC // P, L])
        DL = scn("DL", [P, T4, L])
        DU = scn("DU", [P, T4, L])
        ZS = scn("ZS", [P, T4, L])
        YA = scn("YA", [P, T4, L])
        HS = scn("HS", [P, 2, T4, L])
        GB = scn("GB", [P, 2, T4, L])
        T2, T1 = HS[:, 0], HS[:, 1]
        U2 = GB[:, 0]
        xd = scn("xd", [DR + 2 * NS, L])
        Ct = scn("Ct", [P, T4, NS])
        BB = scn("BB", [P, 2, 2, L])
        bn6 = scn("bn6", [P, T4, 6])
        mv = scn("mv", [P, T4, 2])
        zst = scn("zst", [P, 4, T4])
        s1.close()

        h2h = ctx.enter_context(nc.sbuf_tensor("h2h", [P, KC, HB * L], f32r, side="right"))
        h2l = ctx.enter_context(nc.sbuf_tensor("h2l", [P, KC, HB * L], f32r, side="right"))

        s2 = ExitStack()
        att = arena(s2)
        bqk = att("bqk", [P, 2 * T4])
        bvb = att("bvb", [P, H])
        rope = att("rope", [P, 2, L])
        perm = att("perm", [P, P])
        rtw = att("rtw", [P, KC, ROUTE])
        rth = att("rth", [P, KC, ROUTE], f32r)
        rtl = att("rtl", [P, KC, ROUTE], f32r)
        XL = att("XL", [P, T4, H])
        hp = att("hp", [P, T4, H])
        h1h = att("h1h", [P, KC, L], f32r)
        h1l = att("h1l", [P, KC, L], f32r)
        QK = att("QK", [P, 2 * T4, L])
        V = att("V", [P, T4, H])
        EX = att("EX", [P, 2, 2, L])
        PT = att("PT", [P, 2, 2, L])
        QB, RC, RS = EX[:, 0], EX[:, 1], PT[:, 0]
        wagain = [t[:].rearrange("p a b l -> p (a b l)") for t in (EX, PT)]
        nm = att("nm", [P, 2, 2])
        rs = att("rs", [P, 2, 2])
        ri = att("ri", [P, 2, 2])
        sq = att("sq", [P, H])
        cth = att("cth", [P, KC, P], f32r)
        ctl = att("ctl", [P, KC, P], f32r)
        hw = att("hw", [P, KC, P])
        ss = att("ss", [P, T4])
        abn = att("abn", [P, T4, 6])
        amv = att("amv", [P, T4, 2])
        ast = att("ast", [P, 8, T4])
        r2 = att("r2", [P, 3, T4])
        s2.close()
        sa.close()

        s3 = ExitStack()
        exa = arena(s3)
        wgr = exa("wgr", [P, GW])
        wdr = exa("wdr", [P, DW])
        wgh = exa("wgh", [P, KC, 2 * EI], f32r)
        wgl = exa("wgl", [P, KC, 2 * EI], f32r)
        wdh = exa("wdh", [P, NCH, H], f32r)
        wdl = exa("wdl", [P, NCH, H], f32r)
        fah = exa("fah", [P, NCH, HB * L], f32r)
        fal = exa("fal", [P, NCH, HB * L], f32r)
        ft = exa("ft", [P, 2, L])
        fp = exa("fp", [P, 2, L])
        fa = exa("fa", [P, 2, L])
        ew_in = exa("ew_in", [P, DC // P, DI])
        exproj = exa("exproj", [P, T4, DR + 2 * NS])
        edtproj = exa("edtproj", [DR, DI])
        eddiag = exa("eddiag", [P, T4, P])
        ecT = exa("ecT", [P, HB, DC // P, L])
        eDL = exa("eDL", [P, T4, L])
        eDU = exa("eDU", [P, T4, L])
        eZS = exa("eZS", [P, T4, L])
        eYA = exa("eYA", [P, T4, L])
        eHS = exa("eHS", [P, 2, L])
        eGB = exa("eGB", [P, 2, L])
        exd = exa("exd", [DR + 2 * NS, L])
        eCt = exa("eCt", [P, T4, NS])
        eBB = exa("eBB", [P, 2, L])
        ebn = exa("ebn", [P, T4, 6])
        emv = exa("emv", [P, T4, 2])
        ezst = exa("ezst", [P, 4, T4])
        s3.close()

        A01 = pb("A01", [P, 2, L])
        A23 = pb("A23", [P, 2, L])
        A45 = pb("A45", [P, 2, L])
        A67 = pb("A67", [P, 2, L])
        bank = [t[:, k, :] for t in (A01, A23, A45, A67) for k in range(2)]
        Q = bank[0:4]
        DA = bank[4:6]
        HT = bank[6:8]
        SB = [A01, A23]
        PB = A45
        CX, WK = bank[6], bank[7]
        FG, FU, FD = bank[0:2], bank[2:4], bank[4:6]
        EB = bank[6:8]
        UQ = NU // HB
        UP = 2
        UN = UQ - UP
        SU = 16

        const_in = sem("const_in")
        x_in_s = [sem(f"x_loaded{h}") for h in range(2)]
        ctx_in_s = [sem(f"ctx_loaded{h}") for h in range(2)]
        consts = sem("consts")
        scanw_in = [sem(f"scan_weights_loaded{h}") for h in range(2)]
        ddiag_s = sem("ddiag_made")
        rows_made = sem("rows_of_constants_made")
        z_bn, z_mv, z_norm, z_n, z_t, z_done = [sem("z_" + n) for n in
                                                ("stats", "meanvar", "norm", "normed", "tanh", "done")]
        xp_mm, cv_init, cv_tap, u_t, u_done = [sem(n) for n in
                                               ("inproj_ready", "conv_started", "conv_tap", "u_tanh", "u_done")]
        xd_mm, xd_ready, b_stored = sem("xdbl_product"), sem("xdbl_ready"), sem("b_stored")
        bb_in = [sem("b_rows_loaded0"), sem("b_rows_loaded1")]
        ct_mm, ct_ready = sem("c_transposed"), sem("c_ready")
        dt_mm, dt_abs, dt_rel, dt_e, dt_l, dl_done, du_done = [sem("delta_" + n) for n in
                                                               ("product", "abs", "relu", "exp", "log", "done", "times_u")]
        yi_mm, yi_done, zT_ready = sem("du_term_product"), sem("y_started"), sem("z_transposed")
        dA_ready, gb_ready, scan_done = sem("decay_ready"), sem("input_ready"), sem("scan_done")
        hT_ready, y_acc, y_z, x1_done = sem("states_transposed"), sem("y_added"), sem("y_gated"), sem("x1_done")
        wraw_in, wah_done, wal_done = sem("att_weights_loaded"), sem("att_weights_hi"), sem("att_weights_lo")
        attc_in = [sem(f"att_consts_loaded{h}") for h in range(2)]
        rt_split = sem("router_split")
        a_bn, a_mv, a_norm, a_xl, a_hp = [sem("att_" + n) for n in ("stats", "meanvar", "norm", "normed", "scaled")]
        h1_mm, h1_hi, h1_lo = sem("h1_transposed"), sem("h1_hi"), sem("h1_lo")
        v_mm, v_done = sem("v_product"), sem("v_ready")
        qk_mm, qb_ready, rot_mm, rope_c, rope_s, qk_done = [sem(n) for n in
                                                            ("qk_product", "qk_biased", "qk_rotated", "rope_cos", "rope_sin", "qk_ready")]
        s_mm, mx_done, ex_done = sem("scores_ready"), sem("row_max"), sem("probs_ready")
        t_mm, pt_a, pt_b, pv_mm = sem("probs_transposed"), sem("probs_copied_even"), sem("probs_copied_odd"), sem("pv_ready")
        ri_done, p_done, cth_done, ctl_done = [sem(n) for n in
                                               ("row_sum_inverse", "probs_normed", "context_hi", "context_lo")]
        wo_mm, xm_done, xacc_done, sq_done, r2_s, hp2_done = [sem(n) for n in
                                                              ("wo_product", "residual_done", "residual_summed", "square_sum", "rms2", "h2_scaled")]
        h2_mm, hw_done, h2h_done, h2l_done, h2h_kept, h2l_kept, rt_mm, lg_done = [
            sem(n) for n in ("h2_transposed", "h2_weighted", "h2_hi", "h2_lo", "h2_hi_kept", "h2_lo_kept",
                             "router_product", "logits_ready")]
        gt, gt_e, gt_t, att_done = sem("gating_step"), sem("gating_exp"), sem("gating_tanh"), sem("attention_done")
        wg_in, wd_in = sem("gate_up_loaded"), sem("down_loaded")
        wgh_s, wgl_s, wdh_s, wdl_s = sem("gate_up_hi"), sem("gate_up_lo"), sem("down_hi"), sem("down_lo")
        gu_mm, f_t, f_p, f_a, f_ah, f_al = [sem(n) for n in
                                            ("gate_up_product", "gate_tanh", "gate_done", "act_ready", "act_hi", "act_lo")]
        d_mm, d_acc, stored = sem("down_product"), sem("down_added"), sem("out_stored")

        z_t4, z_d4, u_t4, u_d4 = [sem(n) for n in ("z_tanh_part", "z_done_part", "u_tanh_part", "u_done_part")]
        dt_l4, dl4 = sem("delta_log_part"), sem("delta_done_part")
        gb4, y4 = sem("input_part_ready"), sem("y_part_added")
        watt_in_s = [sem("att_weights_loaded_even"), sem("att_weights_loaded_odd")]
        wah2, wal2 = sem("att_weights_hi_again"), sem("att_weights_lo_again")

        C_G4 = 8
        C4 = 4
        C_X1 = 4
        C_BST = 16
        C_ZT = 1
        C_SC = 8
        C_HT = 8
        C_YA = 4
        C_GB = 4
        C_WL = 1
        C_DA = 8
        C2 = 2
        C1 = 1

        NL = 4
        GT = 11 + 4 * TH
        block = ctx.enter_context(nc.Block())

        def beside(unit, before, step, after):
            def run(e, prepare=None):
                for g in range(HB, B):
                    k0 = UQ * (g - HB)
                    for n in range(UP):
                        unit(k0 + n, lambda j, *late, n=n: before(g, SU * n + j, *late))
                    prepare and prepare(g)
                    last = g == B - 1
                    with e.Fori(0, UN - last) as i:
                        unit(i + (k0 + UP), lambda j, *late: step(g, i, j, *late))
                    if last:
                        unit(k0 + UQ - 1, lambda j, *late: step(g, UN - 1, j, *late), more=False)
                    after(g)
            return run

        def nth(g, i, j):
            return T4 * NS * g + SU * i + j

        def column(i, j):
            n = i * (SU // T4) + j // T4
            return slice(n, n + 1) if isinstance(n, int) else ds(n, 1)

        def wait_apart(e, what, value):
            e.wait_ge(const_in, 96)
            e.wait_ge(what, value)

        def scan_ended(e, half):
            e.wait_ge(x1_done, T4 * HB * (half + 1) + C_X1)
            if half:
                experts_ended(e, half - 1)
            else:
                e.wait_ge(wal_done, KC + C_WL)

        def attention_ended(e, half):
            e.wait_ge(lg_done, T4 * HB * (half + 1) + C1)
            e.wait_ge(xacc_done, T4 * HB * (half + 1))
            e.wait_ge(h2h_kept, T4 * HB * (half + 1))
            e.wait_ge(h2l_kept, T4 * HB * (half + 1))

        def experts_ended(e, half):
            e.wait_ge(d_acc, NU * TH * (half + 1) + C_DA)

        @block.sync
        def _(sp):
            sp.sem_inc(b_stored, C_BST)

            def load_consts():
                for dst, src in ((ident[:], ident_in), (mask[:], mask_in), (chan[:], chan_in),
                                 (gates[:], gates_in.partition_broadcast(P)), (wln[:], wln_in),
                                 (iota8[:], iota_in.partition_broadcast(P))):
                    sp.dma_start(dst, src).then_inc(const_in, 16)

            def scan_stage(half):
                if half:
                    experts_ended(sp, half - 1)
                sp.dma_start(cT[:], ctx_in[half]).then_inc(ctx_in_s[half], 16)
                for dst, src in ((w_in[:], w_in_in), (xproj[:], xproj_in), (dtproj[:], dtproj_in)):
                    sp.dma_start(dst, src).then_inc(scanw_in[half], 16)
                if half == 0:
                    load_consts()
                    for h in range(2):
                        sp.dma_start(xs[:, h * TH:(h + 1) * TH, :], x_in[h]).then_inc(x_in_s[h], 16)
                with sp.Fori(HB * half, HB * half + HB) as g:
                    for c in range(KC // HB):
                        sp.wait_ge(wal_done, (KC // HB) * g + c + C_WL)
                        sp.dma_start(wraw[:], watt_in[:, (g - HB * half) * (KC // HB) + c, :]
                                     ).then_inc(wraw_in, 16)
                    sp.wait_ge(xd_ready, g + 1)
                    sp.dma_start(b_scratch[g], xd[DR:DR + NS, :]).then_inc(b_stored, 16)
                    with sp.Fori(0, NS // NL) as i:
                        sp.wait_ge(b_stored, 16 * g + 16 + C_BST)
                        for s in range(2):
                            sp.wait_ge(gb_ready, NS * g + NL * i + 2 * s - 2 + C_GB)
                            sp.dma_start(BB[:, s], b_scratch[g, ds(NL * i + 2 * s, 2), :]
                                         .partition_broadcast(P)).then_inc(bb_in[s], 16)

            def attention_stage(half):
                scan_ended(sp, half)
                for dst, src in ((bqk[:], bqk_in), (bvb[:], bv_in.partition_broadcast(P)),
                                 (rope[:], rope_in), (perm[:], perm_in), (rtw[:], route_in)):
                    sp.dma_start(dst, src).then_inc(attc_in[half], 16)
                if half:
                    for c in range(KC):
                        if c >= 2:
                            sp.wait_ge(wal2, c - 1)
                        sp.dma_start(wagain[c % 2], watt_in[:, c, :]).then_inc(watt_in_s[c % 2], 16)

            def expert_stage(half):
                attention_ended(sp, half)
                K0 = NU * half

                def unit(k):
                    sp.wait_ge(wgl_s, KC * k + C1)
                    sp.dma_start(wgr[:], wffn_in[k - K0, :, 0:GW]).then_inc(wg_in, 16)
                    sp.wait_ge(wdl_s, NCH * k + C1)
                    sp.dma_start(wdr[:], wffn_in[k - K0, :, GW:GW + DW]).then_inc(wd_in, 16)

                if half:
                    with sp.Fori(K0, K0 + NU) as k:
                        unit(k)
                else:
                    sp.dma_start(wgr[:], wffn_in[0, :, 0:GW]).then_inc(wg_in, 16)
                    sp.dma_start(wdr[:], wffn_in[0, :, GW:GW + DW]).then_inc(wd_in, 16)
                    sp.dma_start(ecT[:], ctx_in[1]).then_inc(ctx_in_s[1], 16)
                    for dst, src in ((ew_in[:], w_in_in), (exproj[:], xproj_in), (edtproj[:], dtproj_in)):
                        sp.dma_start(dst, src).then_inc(scanw_in[1], 16)
                    for g in range(HB, B):
                        for k in range(UQ * (g - HB), UQ * (g - HB) + UP):
                            if k:
                                unit(k)
                        sp.wait_ge(xd_ready, g + 1)
                        sp.dma_start(b_scratch[g], exd[DR:DR + NS, :]).then_inc(b_stored, 16)
                        sp.wait_ge(b_stored, 16 * g + 16 + C_BST)
                        with sp.Fori(0, UN) as i:
                            unit(i + (UQ * (g - HB) + UP))
                            for n in range(SU // T4):
                                sp.wait_ge(gb4, T4 * NS * (g - HB) + SU * i + T4 * (n - 2) + T4 + C_G4)
                                sp.dma_start(eBB[:, n % 2, :], b_scratch[g, ds(4 * i + n, 1), :]
                                             .partition_broadcast(P)).then_inc(bb_in[n % 2], 16)
                experts_ended(sp, half)
                sp.dma_start(out[half], xs[:, half * TH:(half + 1) * TH, :]).then_inc(stored, 16)

            scan_stage(0)
            for half in range(2):
                attention_stage(half)
                expert_stage(half)
            sp.wait_ge(stored, 32)

        @block.tensor
        def _(pe):
            pe.sem_inc(hT_ready, C_HT)
            pe.sem_inc(zT_ready, C_ZT)
            for s in (rot_mm, t_mm, pv_mm):
                pe.sem_inc(s, C2)
            for s in (gu_mm, d_mm):
                pe.sem_inc(s, C1)

            def split_product(out_, parts, rhs_parts, n):
                for k in range(n):
                    for j, (a, b) in enumerate(((0, 0), (0, 1), (1, 0))):
                        mm = nc.tensor.matmul(out_, parts[a](k), rhs_parts[b](k),
                                              start=(k == 0 and j == 0), stop=(k == n - 1 and j == 2))
                return mm

            def scan_stage(half):
                pe.wait_ge(ctx_in_s[half], 16)
                pe.wait_ge(scanw_in[half], 48)
                if half == 0:
                    pe.wait_ge(const_in, 96)
                pe.wait_ge(ddiag_s, T4 * (half + 1))
                with pe.Fori(HB * half, HB * half + HB) as g:
                    for et in range(T4):
                        pe.wait_ge(x1_done, T4 * g + et + 1 - T4 + C_X1)
                        for k in range(DC // P):
                            mm = nc.tensor.matmul(Q[et], w_in[:, k, et * P:(et + 1) * P],
                                                  cT[:, ds(g - HB * half, 1), k, :],
                                                  start=(k == 0), stop=(k == DC // P - 1))
                        mm.then_inc(xp_mm, 1)
                    for et in range(T4):
                        pe.wait_ge(u_done, T4 * g + et + 1)
                        mm = nc.tensor.matmul(Q[0][0:DR + 2 * NS, :], xproj[:, et, :], U2[:, et, :],
                                              start=(et == 0), stop=(et == T4 - 1))
                    mm.then_inc(xd_mm, 1)
                    pe.wait_ge(xd_ready, g + 1)
                    n3 = DR + 2 * NS
                    for et in range(T4):
                        if et == 2:
                            for tt in range(T4):
                                mm = nc.tensor.transpose(Q[1][:, tt * n3:(tt + 1) * n3],
                                                         xd[:, tt * P:(tt + 1) * P], ident[0:n3, 0:n3])
                            mm.then_inc(ct_mm, 1)
                        if et == 3:
                            pe.wait_ge(ct_ready, g + 1)
                        nc.tensor.matmul(Q[(et + 2) % T4], dtproj[:, et * P:(et + 1) * P], xd[0:DR, :],
                                         start=True, stop=True).then_inc(dt_mm, 1)
                    pe.wait_ge(dt_rel, T4 * g + T4)
                    pe.wait_ge(dt_abs, T4 * g + T4)
                    for tt in range(T4):
                        for et in range(T4):
                            mm = nc.tensor.matmul(Q[tt][:, et * P:(et + 1) * P],
                                                  U2[:, et, tt * P:(tt + 1) * P], ddiag[:, et, :],
                                                  start=True, stop=True)
                        mm.then_inc(yi_mm, 1)
                    pe.wait_ge(z_done, g + 1)
                    for tt in range(T4):
                        pe.wait_ge(yi_done, T4 * g + tt + 1)
                        for rt in range(T4):
                            mm = nc.tensor.transpose(Q[tt][:, rt * P:(rt + 1) * P],
                                                     ZS[:, rt, tt * P:(tt + 1) * P], ident[:])
                        mm.then_inc(zT_ready, 1)
                    with pe.Fori(0, NS // NL) as i:
                        for n in range(NL):
                            step = NS * g + NL * i + n
                            pe.wait_ge(scan_done, T4 * step + T4 + C_SC)
                            for tt in range(T4):
                                pe.wait_ge(y_acc, T4 * step + tt - 1 + C_YA)
                                for et in range(T4):
                                    mm = nc.tensor.transpose(HT[tt % 2][:, et * P:(et + 1) * P],
                                                             HS[:, n % 2, et, tt * P:(tt + 1) * P], ident[:])
                                mm.then_inc(hT_ready, 1)

            def attention_stage(half):
                scan_ended(pe, half)
                pe.wait_ge(attc_in[half], 80)
                pe.wait_ge(consts, 7)
                pe.wait_ge(rt_split, 2 * (half + 1))

                def turn_rows(g, tt):
                    pe.wait_ge(ex_done, 32 * g + C2)
                    pe.wait_ge(a_hp, T4 * g + tt + 1)
                    for k in range(KC):
                        mm = nc.tensor.transpose(bank[k][:, tt * P:(tt + 1) * P],
                                                 hp[:, tt, k * P:(k + 1) * P], ident[:])
                    if tt == T4 - 1:
                        mm.then_inc(h1_mm, 1)

                for tt in range(T4):
                    turn_rows(HB * half, tt)
                if half:
                    pe.wait_ge(wal2, KC)
                for g in range(HB * half, HB * half + HB):
                    U0 = 32 * g
                    pe.wait_ge(h1_hi, KC * g + KC)
                    pe.wait_ge(h1_lo, KC * g + KC)
                    for tt in range(T4):
                        split_product(bank[tt],
                                      [lambda k, w=w: w[:, k, tt * P:(tt + 1) * P] for w in (h1h, h1l)],
                                      [lambda k, w=w: w[:, k, 2 * H:3 * H] for w in (wah, wal)], KC
                                      ).then_inc(v_mm, 1)

                    def product(m):
                        pe.wait_ge(qb_ready, 8 * g + m - 1 + C2)
                        split_product(bank[4 + m % 2],
                                      [lambda k, w=w: w[:, k, m * P:(m + 1) * P] for w in (wah, wal)],
                                      [lambda k, w=w: w[:, k, :] for w in (h1h, h1l)], KC).then_inc(qk_mm, 1)

                    def rotate(m):
                        pe.wait_ge(qb_ready, 8 * g + m + 1 + C2)
                        pe.wait_ge(rope_s, 8 * g + m - 1 + C2)
                        nc.tensor.matmul(bank[6 + m % 2], perm[:], QB[:, m % 2, :], start=True,
                                         stop=True).then_inc(rot_mm, 1)

                    pe.wait_ge(lg_done, T4 * g + C1)
                    for m in range(8):
                        product(m)
                        if m:
                            rotate(m - 1)
                    rotate(7)

                    def scores(u, a):
                        i, hpair = divmod(u, NH // 2)
                        W = P * (i + 1)
                        if u == 0:
                            pe.wait_ge(v_done, T4 * g + T4)
                            pe.wait_ge(qk_done, 8 * g + 8 + C2)
                        if a == 0:
                            pe.wait_ge(ex_done, U0 + u - 1 + C2)
                        h = 2 * hpair + a
                        r, m = HD * (h % 4), h // 4
                        nc.tensor.matmul(SB[u % 2][:, a, 0:W], QK[r:r + HD, m, i * P:(i + 1) * P],
                                         QK[r:r + HD, 4 + m, 0:W], start=True, stop=False)
                        mm = nc.tensor.matmul(SB[u % 2][:, a, W - P:W], identb[:], maskb[:],
                                              start=False, stop=True)
                        if a:
                            mm.then_inc(s_mm, 1)

                    def turn(u):
                        i = u // (NH // 2)
                        pe.wait_ge(p_done, U0 + u + 1)
                        pe.wait_ge(pt_a, U0 + u + C1)
                        pe.wait_ge(pt_b, U0 + u + C1)
                        for a in range(2):
                            for kb in range(i + 1):
                                mm = nc.tensor.transpose(PB[:, a, kb * P:(kb + 1) * P],
                                                         EX[:, u % 2, a, kb * P:(kb + 1) * P], ident[:])
                        mm.then_inc(t_mm, 1)

                    def weigh(u, a):
                        i, hpair = divmod(u, NH // 2)
                        pe.wait_ge((pt_a, pt_b)[a], U0 + u + 1 + C1)
                        if hpair == 0 and a == 0 and g + i:
                            pe.wait_ge(cth_done, T4 * g + i)
                            pe.wait_ge(ctl_done, T4 * g + i)
                        h = 2 * hpair + a
                        r, m = HD * (h % 4), h // 4
                        for kb in range(i + 1):
                            mm = nc.tensor.matmul(CX[r:r + HD, m * P:(m + 1) * P],
                                                  V[:, kb, h * HD:(h + 1) * HD],
                                                  PT[:, u % 2, a, kb * P:(kb + 1) * P],
                                                  start=(kb == 0), stop=(kb == i))
                        if a:
                            mm.then_inc(pv_mm, 1)

                    def finish(i, step):
                        t = T4 * g + i
                        if step == 0:
                            pe.wait_ge(lg_done, t + C1)
                            pe.wait_ge(cth_done, t + 1)
                            pe.wait_ge(ctl_done, t + 1)
                            split_product(WK, [lambda k, w=w: w[:, k, :] for w in (cth, ctl)],
                                          [lambda k, w=w: w[:, k, 3 * H:4 * H] for w in (wah, wal)], KC
                                          ).then_inc(wo_mm, 1)
                        if step == 1:
                            pe.wait_ge(hp2_done, t + 1)
                            for k in range(KC):
                                mm = nc.tensor.transpose(WK[:, k * P:(k + 1) * P],
                                                         hp[:, i, k * P:(k + 1) * P], ident[:])
                            mm.then_inc(h2_mm, 1)
                        if step == 2:
                            pe.wait_ge(h2h_done, t + 1)
                            pe.wait_ge(h2l_done, t + 1)
                            split_product(WK[:, 0:ROUTE],
                                          [lambda k, w=w: w[:, k, :] for w in (cth, ctl)],
                                          [lambda k, w=w: w[:, k, :] for w in (rth, rtl)], KC
                                          ).then_inc(rt_mm, 1)

                    for u in range(2):
                        for a in range(2):
                            scores(u, a)
                    for u in range(32):
                        turn(u)
                        for a in range(2):
                            if u + 2 < 32:
                                scores(u + 2, a)
                            if a:
                                weigh(u, 0)
                                weigh(u, 1)
                        if u >= 8 and u % 8 in (0, 3, 5):
                            finish(u // 8 - 1, (u % 8 + 1) // 2 - (u % 8 > 0))
                    more = g % HB < HB - 1
                    finish(3, 0)
                    for tt in range(T4 - 1):
                        more and turn_rows(g + 1, tt)
                    finish(3, 1)
                    more and turn_rows(g + 1, T4 - 1)
                    finish(3, 2)

            def expert_stage(half):
                attention_ended(pe, half)

                def unit(k, place=lambda j: None, more=True):
                    pe.wait_ge(wgh_s, KC * k + KC)
                    pe.wait_ge(wgl_s, KC * k + KC + C1)
                    for s in range(NG * NCH):
                        grp, c = divmod(s, NCH)
                        pe.wait_ge(f_a, NG * NCH * k + s - 1 + C2)
                        for j, o, bk in ((0, 0, FG), (1, EI, FU)):
                            mm = split_product(bk[s % 2][0:CW[c], :],
                                               [lambda j, w=w: w[:, j, o + c * P:o + c * P + CW[c]] for w in (wgh, wgl)],
                                               [lambda j, w=w: w[:, j, grp * L:(grp + 1) * L] for w in (h2h, h2l)], KC)
                            if j:
                                mm.then_inc(gu_mm, 1)
                            place(2 * s + j)
                    pe.wait_ge(wdh_s, NCH * k + NCH)
                    pe.wait_ge(wdl_s, NCH * k + NCH + C1)
                    for tt in range(TH):
                        if tt % T4 == 0:
                            pe.wait_ge(f_ah, NG * NCH * k + NCH * (tt // T4 + 1) + C2)
                            pe.wait_ge(f_al, NG * NCH * k + NCH * (tt // T4 + 1) + C2)
                        pe.wait_ge(d_acc, TH * k + tt - 1 + C_DA)
                        split_product(FD[tt % 2],
                                      [lambda c, w=w: w[0:CW[c], c, tt * P:(tt + 1) * P] for w in (fah, fal)],
                                      [lambda c, w=w: w[0:CW[c], c, :] for w in (wdh, wdl)], NCH
                                      ).then_inc(d_mm, 1)
                        if tt % 2 == 0:
                            place(2 * NG * NCH + tt // 2)

                def before(g, j):
                    if j in (0, 2, 4, 6):
                        et = j // 2
                        if et == 0:
                            pe.wait_ge(x1_done, T4 * g + C_X1)
                        if et >= 2:
                            pe.wait_ge(cv_tap, 12 * g + 3 * (et - 2) + 3)
                        for k in range(DC // P):
                            mm = nc.tensor.matmul(EB[et % 2], ew_in[:, k, et * P:(et + 1) * P],
                                                  ecT[:, g - HB, k, :], start=(k == 0), stop=(k == DC // P - 1))
                        mm.then_inc(xp_mm, 1)
                    if j == 12:
                        pe.wait_ge(u_d4, T4 * (g - HB) + T4)
                        for et in range(T4):
                            mm = nc.tensor.matmul(EB[0][0:DR + 2 * NS, :], exproj[:, et, :], eDU[:, et, :],
                                                  start=(et == 0), stop=(et == T4 - 1))
                        mm.then_inc(xd_mm, 1)
                    if j == 13:
                        wait_apart(pe, xd_ready, g + 1)
                        n3 = DR + 2 * NS
                        for tt in range(T4):
                            mm = nc.tensor.transpose(EB[1][:, tt * n3:(tt + 1) * n3],
                                                     exd[:, tt * P:(tt + 1) * P], ident[0:n3, 0:n3])
                        mm.then_inc(ct_mm, 1)
                    if j in (15, 17, 19, 21):
                        et = (j - 15) // 2
                        if et == 1:
                            pe.wait_ge(ct_ready, g + 1)
                        if et >= 2:
                            pe.wait_ge(dt_abs, T4 * g + et - 1)
                            pe.wait_ge(dt_rel, T4 * g + et - 1)
                        nc.tensor.matmul(EB[et % 2], edtproj[:, et * P:(et + 1) * P], exd[0:DR, :],
                                         start=True, stop=True).then_inc(dt_mm, 1)
                    if j in (26, 27, 28, 29):
                        tt = j - 26
                        if tt == 0:
                            pe.wait_ge(dt_abs, T4 * g + T4)
                            pe.wait_ge(dt_rel, T4 * g + T4)
                        if tt >= 2:
                            pe.wait_ge(yi_done, T4 * g + tt - 1)
                        for et in range(T4):
                            mm = nc.tensor.matmul(EB[tt % 2][:, et * P:(et + 1) * P],
                                                  eDU[:, et, tt * P:(tt + 1) * P], eddiag[:, et, :],
                                                  start=True, stop=True)
                        mm.then_inc(yi_mm, 1)

                def step(g, i, j):
                    q = nth(g, i, j)
                    pe.wait_ge(scan_done, q + 1 + C_SC)
                    pe.wait_ge(y4, q - T4 * NS * HB + C4)
                    for tt in range(T4):
                        mm = nc.tensor.transpose(EB[1][:, tt * P:(tt + 1) * P],
                                                 eHS[:, j % 2, tt * P:(tt + 1) * P], ident[:])
                    mm.then_inc(hT_ready, 1)

                def after(g):
                    for tt in range(T4):
                        if tt == 0:
                            pe.wait_ge(scan_done, T4 * NS * (g + 1) + C_SC)
                            pe.wait_ge(y4, T4 * NS * (g + 1 - HB) + C4)
                        if tt >= 2:
                            pe.wait_ge(y_z, T4 * g + tt - 1)
                        for rt in range(T4):
                            mm = nc.tensor.transpose(EB[tt % 2][:, rt * P:(rt + 1) * P],
                                                     eZS[:, rt, tt * P:(tt + 1) * P], ident[:])
                        mm.then_inc(zT_ready, 1)

                if half:
                    with pe.Fori(NU, 2 * NU) as k:
                        unit(k)
                else:
                    pe.wait_ge(ctx_in_s[1], 16)
                    pe.wait_ge(scanw_in[1], 48)
                    pe.wait_ge(ddiag_s, 2 * T4)
                    beside(unit, before, step, after)(pe)

            scan_stage(0)
            for half in range(2):
                attention_stage(half)
                expert_stage(half)

        @block.scalar
        def _(act):
            for s in (qb_ready, ex_done, f_ah):
                act.sem_inc(s, C2)
            act.sem_inc(pt_a, C1)

            def make_consts():
                act.wait_ge(const_in, 96)
                nc.scalar.activation(identb[:], ident[:], ACT.Copy).then_inc(consts, 1)
                nc.scalar.activation(maskb[:], mask[:], ACT.Copy).then_inc(consts, 1)
                nc.scalar.activation(tg[:, 0:2], gates[:], ACT.Tanh).then_inc(consts, 1)
                nc.scalar.activation(aneg[:], chan[:, :, TAPS + 3:], ACT.Exp).then_inc(consts, 1)
                act.wait_ge(consts, 4)
                nc.scalar.activation(aneg[:], aneg[:], ACT.Copy, scale=-1.0).then_inc(consts, 1)
                nc.scalar.activation(tg[:, 2:4], tg[:, 0:2], ACT.Copy, scale=0.5).then_inc(consts, 1)
                nc.scalar.activation(tgq[:], tg[:, 1:2], ACT.Copy, scale=0.25).then_inc(consts, 1)
                act.wait_ge(consts, 7)

            def scan_stage(half):
                if half:
                    experts_ended(act, half - 1)
                act.wait_ge(x_in_s[half], 16)
                with act.Fori(HB * half, HB * half + HB) as g:
                    def round_weights(c):
                        act.wait_ge(wraw_in, 16 * ((KC // HB) * g + c + 1))
                        nc.scalar.activation(wah[:, ds(g * (KC // HB) + c, 1), :], wraw[:],
                                             ACT.Copy).then_inc(wah_done, 1)

                    for et in range(T4):
                        act.wait_ge(xp_mm, T4 * g + et + 1)
                        nc.scalar.activation(T1[:, et, :], Q[et], ACT.Identity,
                                             bias=chan[:, et, TAPS:TAPS + 1],
                                             scale=chan[:, et, TAPS - 1:TAPS]).then_inc(cv_init, 1)
                    round_weights(0)
                    act.wait_ge(z_norm, 4 * g + 4)
                    act.wait_ge(zT_ready, T4 * g + C_ZT)
                    for rt in range(T4):
                        nc.scalar.activation(ZS[:, rt, :], xs[:, ds(T4 * g + rt, 1), :], ACT.Identity,
                                             bias=zst[:, 3, rt:rt + 1], scale=zst[:, 1, rt:rt + 1]
                                             ).then_inc(z_n, 1)
                    for et in range(T4):
                        act.wait_ge(cv_tap, 12 * g + 3 * et + 3)
                        nc.scalar.activation(T2[:, et, :], T1[:, et, :], ACT.Tanh, scale=0.5).then_inc(u_t, 1)
                    act.wait_ge(z_n, T4 * g + T4)
                    act.wait_ge(u_done, T4 * g + T4)
                    nc.scalar.activation(T2, ZS[:], ACT.Tanh, scale=0.5).then_inc(z_t, 1)
                    act.wait_ge(xd_mm, g + 1)
                    act.wait_ge(b_stored, 16 * g + C_BST)
                    nc.scalar.activation(xd[:], Q[0][0:DR + 2 * NS, :], ACT.Copy, scale=0.5).then_inc(xd_ready, 1)
                    n3 = DR + 2 * NS
                    for et in range(T4):
                        if et == 2:
                            act.wait_ge(ct_mm, g + 1)
                            nc.scalar.activation(Ct[:], Q[1][:, 0:T4 * n3].rearrange("p (t n) -> p t n", n=n3)
                                                 [:, :, DR + NS:n3], ACT.Copy).then_inc(ct_ready, 1)
                        act.wait_ge(dt_mm, T4 * g + et + 1)
                        nc.scalar.activation(T1[:, et, :], Q[(et + 2) % T4], ACT.Abs,
                                             bias=chan[:, et, TAPS + 1:TAPS + 2]).then_inc(dt_abs, 1)
                    act.wait_ge(dt_abs, T4 * g + T4)
                    nc.scalar.activation(T1, T1, ACT.Exp, scale=-1.0).then_inc(dt_e, 1)
                    round_weights(1)
                    act.wait_ge(dt_e, g + 1)
                    for et in range(T4):
                        nc.scalar.activation(T1[:, et, :], T1[:, et, :], ACT.Ln, bias=1.0).then_inc(dt_l4, 1)
                    act.wait_ge(dl4, T4 * g + T4)
                    with act.Fori(0, NS // NL) as i:
                        for n in range(NL):
                            step = NS * g + NL * i + n
                            for et in range(T4):
                                act.wait_ge(scan_done, T4 * step + et - 1 + C_SC)
                                nc.scalar.activation(DA[et % 2], DL[:, et, :], ACT.Exp,
                                                     scale=aneg[:, et, ds(NL * i + n, 1)]).then_inc(dA_ready, 1)

            def attention_stage(half):
                scan_ended(act, half)
                act.wait_ge(attc_in[half], 80)
                nc.scalar.activation(rth[:], rtw[:], ACT.Copy).then_inc(rt_split, 1)

                def norm_rows(g, tt):
                    act.wait_ge(a_norm, 8 * g + 8)
                    if g % HB:
                        act.wait_ge(xacc_done, T4 * (g - 1) + tt + 1)
                        act.wait_ge(h2_mm, T4 * (g - 1) + tt + 1)
                    nc.scalar.activation(XL[:, tt, :], xs[:, T4 * g + tt, :], ACT.Identity,
                                         bias=ast[:, 2, tt:tt + 1], scale=ast[:, 1, tt:tt + 1]
                                         ).then_inc(a_xl, 1)
                    act.wait_ge(a_xl, T4 * g + tt + 1)
                    nc.scalar.activation(hp[:, tt, :], XL[:, tt, :], ACT.Copy,
                                         scale=ast[:, 6, tt:tt + 1]).then_inc(a_hp, 1)

                for tt in range(T4):
                    norm_rows(HB * half, tt)
                if half:
                    for c in range(KC):
                        act.wait_ge(watt_in_s[c % 2], 16 * (c // 2 + 1))
                        nc.scalar.activation(wah[:, c, :], wagain[c % 2], ACT.Copy).then_inc(wah2, 1)
                for g in range(HB * half, HB * half + HB):
                    U0 = 32 * g
                    more = g % HB < HB - 1
                    act.wait_ge(h1_mm, g + 1)
                    for k in range(KC):
                        nc.scalar.activation(h1h[:, k, :], bank[k], ACT.Copy, scale=wln[:, 0, k:k + 1]
                                             ).then_inc(h1_hi, 1)
                    for m in range(8):
                        act.wait_ge(qk_mm, 8 * g + m + 1)
                        act.wait_ge(rot_mm, 8 * g + m - 1 + C2)
                        act.wait_ge(rope_c, 8 * g + m - 1 + C2)
                        nc.scalar.activation(QB[:, m % 2, :], bank[4 + m % 2], ACT.Identity,
                                             bias=bqk[:, m:m + 1]).then_inc(qb_ready, 1)

                    def probs(u):
                        i, hpair = divmod(u, NH // 2)
                        W = P * (i + 1)
                        act.wait_ge(mx_done, U0 + u + 1)
                        act.wait_ge(t_mm, U0 + u - 1 + C2)
                        for a in range(2):
                            ins = nc.scalar.activation(EX[:, u % 2, a, 0:W], SB[u % 2][:, a, 0:W], ACT.Exp,
                                                       bias=nm[:, u % 2, a:a + 1],
                                                       accum_out=rs[:, u % 2, a:a + 1])
                        ins.then_inc(ex_done, 1)

                    def copy_even(u):
                        W = P * (u // (NH // 2) + 1)
                        act.wait_ge(t_mm, U0 + u + 1 + C2)
                        act.wait_ge(pv_mm, U0 + u - 1 + C2)
                        nc.scalar.activation(PT[:, u % 2, 0, 0:W], PB[:, 0, 0:W], ACT.Copy).then_inc(pt_a, 1)

                    def finish(i, step):
                        t = T4 * g + i
                        if step == 0:
                            act.wait_ge(pv_mm, U0 + 8 * i + 8 + C2)
                            nc.scalar.activation(cth[:], CX.rearrange("p (k t) -> p k t", k=KC), ACT.Copy
                                                 ).then_inc(cth_done, 1)
                        if step == 1:
                            act.wait_ge(xm_done, t + 1)
                            nc.scalar.activation(sq[:], XL[:, i, :], ACT.Square, accum_out=ss[:, i:i + 1]
                                                 ).then_inc(sq_done, 1)
                        if step == 2:
                            act.wait_ge(r2_s, 3 * t + 3)
                            nc.scalar.activation(hp[:, i, :], XL[:, i, :], ACT.Copy,
                                                 scale=r2[:, 1, i:i + 1]).then_inc(hp2_done, 1)
                        if step == 3:
                            act.wait_ge(hw_done, t + 1)
                            nc.scalar.activation(cth[:], hw[:], ACT.Copy).then_inc(h2h_done, 1)
                            nc.scalar.activation(h2h[:, :, ds((g - HB * half) * L + i * P, P)], hw[:], ACT.Copy
                                                 ).then_inc(h2h_kept, 1)

                    probs(0)
                    for u in range(32):
                        if u >= 8 and u % 8 == 0:
                            finish(u // 8 - 1, 0)
                        if u + 1 < 32:
                            probs(u + 1)
                        copy_even(u)
                        if u >= 8 and u % 8 in (2, 3, 5):
                            finish(u // 8 - 1, (2, 3, 5).index(u % 8) + 1)
                        if u in (27, 29, 31) and more:
                            norm_rows(g + 1, (u - 27) // 2)
                    for step in range(3):
                        finish(3, step)
                    more and norm_rows(g + 1, T4 - 1)
                    finish(3, 3)

            def expert_stage(half):
                attention_ended(act, half)
                act.wait_ge(gt, GT * half + 2)
                nc.scalar.activation(pr[:, 1], pr[:, 0], ACT.Exp).then_inc(gt_e, 1)
                nc.scalar.activation(gs[:, 3, :], lg[:, :, NE], ACT.Tanh, scale=0.5).then_inc(gt_t, 1)

                def split(k, c):
                    if c == 0:
                        act.wait_ge(wg_in, 16 * k + 16)
                        act.wait_ge(gu_mm, NG * NCH * k + C1)
                    nc.scalar.activation(wgh[:, c, :], wgr[:, c * 2 * EI:(c + 1) * 2 * EI], ACT.Copy
                                         ).then_inc(wgh_s, 1)

                def unit(k, place=lambda j: None, more=True):
                    S0 = NG * NCH * k

                    def tanh(s):
                        act.wait_ge(gu_mm, S0 + s + 1 + C1)
                        act.wait_ge(f_p, S0 + s - 1 + C2)
                        nc.scalar.activation(ft[0:CW[s % NCH], s % 2, :], FG[s % 2][0:CW[s % NCH], :], ACT.Tanh,
                                             scale=0.5).then_inc(f_t, 1)

                    def round_act(s):
                        grp, c = divmod(s, NCH)
                        act.wait_ge(f_a, S0 + s + 1 + C2)
                        nc.scalar.activation(fah[0:CW[c], c, grp * L:(grp + 1) * L], fa[0:CW[c], s % 2, :],
                                             ACT.Copy).then_inc(f_ah, 1)

                    for s in range(NG * NCH + 1):
                        place(2 * s)
                        if s:
                            tanh(s - 1)
                        if s < NG * NCH:
                            place(2 * s + 1)
                        if s:
                            round_act(s - 1)
                        if 1 <= s <= NCH:
                            c = s - 1
                            if c == 0:
                                act.wait_ge(wd_in, 16 * k + 16)
                                act.wait_ge(d_mm, TH * k + C1)
                            nc.scalar.activation(wdh[:, c, :], wdr[:, c * H:(c + 1) * H], ACT.Copy
                                                 ).then_inc(wdh_s, 1)
                    for c in range(KC):
                        if more:
                            split(k + 1, c)
                        if c < KC - 1:
                            place(2 * NG * NCH + 1 + c)

                def before(g, j):
                    if j in (2, 4, 6, 8):
                        et = j // 2 - 1
                        act.wait_ge(xp_mm, T4 * g + et + 1)
                        nc.scalar.activation(eDL[:, et, :], EB[et % 2], ACT.Identity,
                                             bias=chan[:, et, TAPS:TAPS + 1],
                                             scale=chan[:, et, TAPS - 1:TAPS]).then_inc(cv_init, 1)
                    if j in (4, 6, 8, 10):
                        et = j // 2 - 2
                        act.wait_ge(cv_tap, 12 * g + 3 * et + 3)
                        nc.scalar.activation(eYA[:, et, :], eDL[:, et, :], ACT.Tanh, scale=0.5).then_inc(u_t4, 1)
                    if j in (7, 9):
                        act.wait_ge(z_norm, 4 * g + 4)
                        for rt in (j - 7, j - 6):
                            nc.scalar.activation(eZS[:, rt, :], xs[:, T4 * g + rt, :], ACT.Identity,
                                                 bias=ezst[:, 3, rt:rt + 1], scale=ezst[:, 1, rt:rt + 1]
                                                 ).then_inc(z_n, 1)
                    if j in (12, 14):
                        act.wait_ge(z_n, T4 * g + T4)
                        act.wait_ge(u_d4, T4 * (g - HB) + T4)
                        nc.scalar.activation(eYA[:, j - 12:j - 10, :], eZS[:, j - 12:j - 10, :], ACT.Tanh,
                                             scale=0.5).then_inc(z_t4, 1)
                    if j == 13:
                        act.wait_ge(xd_mm, g + 1)
                        act.wait_ge(b_stored, 16 * g + C_BST)
                        nc.scalar.activation(exd[:], EB[0][0:DR + 2 * NS, :], ACT.Copy, scale=0.5
                                             ).then_inc(xd_ready, 1)
                    if j == 15:
                        act.wait_ge(ct_mm, g + 1)
                        n3 = DR + 2 * NS
                        nc.scalar.activation(eCt[:], EB[1][:, 0:T4 * n3].rearrange("p (t n) -> p t n", n=n3)
                                             [:, :, DR + NS:n3], ACT.Copy).then_inc(ct_ready, 1)
                    if j in (17, 19, 21, 23):
                        et = (j - 17) // 2
                        act.wait_ge(dt_mm, T4 * g + et + 1)
                        act.wait_ge(z_d4, 2 * (g - HB) + 2)
                        nc.scalar.activation(eYA[:, et, :], EB[et % 2], ACT.Abs,
                                             bias=chan[:, et, TAPS + 1:TAPS + 2]).then_inc(dt_abs, 1)
                    if j == 24:
                        act.wait_ge(dt_abs, T4 * g + T4)
                        nc.scalar.activation(eYA[:], eYA[:], ACT.Exp, scale=-1.0).then_inc(dt_e, 1)
                    if j == 25:
                        act.wait_ge(dt_e, g + 1)
                        nc.scalar.activation(eYA[:], eYA[:], ACT.Ln, bias=1.0).then_inc(dt_l, 1)

                def first(g):
                    act.wait_ge(dl_done, g + 1 - HB)
                    act.wait_ge(yi_done, T4 * g + T4)

                def step(g, i, j):
                    q = nth(g, i, j)
                    act.wait_ge(scan_done, q + C_SC)
                    nc.scalar.activation(EB[0], eDL[:, j % T4, :], ACT.Exp,
                                         scale=aneg[:, j % T4, column(i, j)]).then_inc(dA_ready, 1)

                for c in range(KC):
                    split(NU * half, c)
                if half:
                    with act.Fori(NU, 2 * NU - 1) as k:
                        unit(k)
                    unit(2 * NU - 1, more=False)
                else:
                    beside(unit, before, step, lambda g: None)(act, first)

            make_consts()
            scan_stage(0)
            for half in range(2):
                attention_stage(half)
                expert_stage(half)


        @block.vector
        def _(dve):
            dve.sem_inc(x1_done, C_X1)
            dve.sem_inc(scan_done, C_SC)
            dve.sem_inc(y_acc, C_YA)
            dve.sem_inc(d_acc, C_DA)
            for s in (rope_s, qk_done, f_p, f_a):
                dve.sem_inc(s, C2)
            dve.sem_inc(y4, C4)
            for s in (pt_b, lg_done, att_done):
                dve.sem_inc(s, C1)

            def stats(rows, six, two, s_six, s_two, g):
                for t in range(T4):
                    nc.vector.bn_stats(six[:, t, :], rows[:, ds(T4 * g + t, 1), :]).then_inc(s_six, 1)
                dve.wait_ge(s_six, (T4 + 1) * g + T4)
                nc.vector.memset(tick[:], 0.0).then_inc(s_six, 1)
                for t in range(T4):
                    nc.vector.bn_aggr(two[:, t, :], six[:, t, :]).then_inc(s_two, 1)

            def scan_stage(half):
                if half:
                    experts_ended(dve, half - 1)
                dve.wait_ge(const_in, 96)
                dve.wait_ge(consts, 7)
                dve.wait_ge(x_in_s[half], 16)
                for et in range(T4):
                    nc.vector.tensor_scalar(ddiag[:, et, :], ident[:], chan[:, et, TAPS + 2:TAPS + 3], 0.5,
                                            ALU.mult, ALU.mult).then_inc(ddiag_s, 1)
                with dve.Fori(HB * half, HB * half + HB) as g:
                    stats(xs, bn6, mv, z_bn, z_mv, g)
                    for et in range(T4):
                        dve.wait_ge(cv_init, T4 * g + et + 1)
                        for sh in range(1, TAPS):
                            if sh > 1:
                                dve.wait_ge(cv_tap, 12 * g + 3 * et + sh - 1)
                            tap = TAPS - 1 - sh
                            nc.vector.scalar_tensor_tensor(T1[:, et, sh:L], Q[et][:, 0:L - sh],
                                                           chan[:, et, tap:tap + 1], T1[:, et, sh:L],
                                                           ALU.mult, ALU.add).then_inc(cv_tap, 1)
                    for et in range(T4):
                        dve.wait_ge(u_t, T4 * g + et + 1)
                        nc.vector.scalar_tensor_tensor(U2[:, et, :], T2[:, et, :], 1.0, T1[:, et, :],
                                                       ALU.add, ALU.mult).then_inc(u_done, 1)
                    dve.wait_ge(z_t, g + 1)
                    nc.vector.scalar_tensor_tensor(ZS[:], T2, 1.0, ZS[:], ALU.add, ALU.mult).then_inc(z_done, 1)
                    for et in range(T4):
                        dve.wait_ge(dt_abs, T4 * g + et + 1)
                        nc.vector.tensor_scalar(DL[:, et, :], Q[(et + 2) % T4], chan[:, et, TAPS + 1:TAPS + 2],
                                                0.0, ALU.add, ALU.max).then_inc(dt_rel, 1)
                    for tt in range(T4):
                        dve.wait_ge(yi_mm, T4 * g + tt + 1)
                        nc.vector.tensor_copy(YA[:, tt, :], Q[tt]).then_inc(yi_done, 1)
                    for et in range(T4):
                        dve.wait_ge(dt_l4, T4 * g + et + 1)
                        nc.vector.tensor_tensor(DL[:, et, :], DL[:, et, :], T1[:, et, :], ALU.add).then_inc(dl4, 1)
                    for et in range(T4):
                        dve.wait_ge(dl4, T4 * g + et + 1)
                        ins = nc.vector.scalar_tensor_tensor(DU[:, et, :], U2[:, et, :], 0.5, DL[:, et, :],
                                                             ALU.mult, ALU.mult)
                    ins.then_inc(du_done, 1)
                    wait_apart(dve, yi_done, T4 * g + T4)

                    def scans(i, n, pair):
                        step = NS * g + NL * i + n
                        if pair == 0:
                            dve.wait_ge(gb_ready, step + 1 + C_GB)
                            dve.wait_ge(hT_ready, T4 * step - T4 + C_HT)
                        for et in (2 * pair, 2 * pair + 1):
                            dve.wait_ge(dA_ready, T4 * step + et + 1)
                            nc.vector.tensor_tensor_scan(HS[:, n % 2, et, :], DA[et % 2], GB[:, n % 2, et, :],
                                                         0.0, ALU.mult, ALU.add).then_inc(scan_done, 1)

                    def sums(i, n, pair):
                        step = NS * g + NL * i + n
                        for tt in (2 * pair, 2 * pair + 1):
                            dve.wait_ge(hT_ready, T4 * step + tt + 1 + C_HT)
                            dve.wait_ge(y_acc, T4 * step + tt - T4 + 1 + C_YA)
                            nc.vector.scalar_tensor_tensor(YA[:, tt, :], HT[tt % 2],
                                                           Ct[:, tt, ds(NL * i + n, 1)], YA[:, tt, :],
                                                           ALU.mult, ALU.add).then_inc(y_acc, 1)

                    scans(0, 0, 0)
                    scans(0, 0, 1)
                    with dve.Fori(0, NS // NL - 1) as i:
                        for n in range(NL):
                            for pair in range(2):
                                scans(i, n + 1, pair)
                                sums(i, n, pair)
                    for n in range(NL):
                        for pair in range(2):
                            if n < NL - 1:
                                scans(NS // NL - 1, n + 1, pair)
                            sums(NS // NL - 1, n, pair)
                    for tt in range(T4):
                        dve.wait_ge(y_acc, T4 * NS * g + T4 * (NS - 1) + tt + 1 + C_YA)
                        dve.wait_ge(zT_ready, T4 * g + tt + 1 + C_ZT)
                        nc.vector.tensor_tensor(YA[:, tt, :], Q[tt], YA[:, tt, :], ALU.mult).then_inc(y_z, 1)
                    for tt in range(T4):
                        dve.wait_ge(y_z, T4 * g + tt + 1)
                        nc.vector.scalar_tensor_tensor(xs[:, ds(T4 * g + tt, 1), :], YA[:, tt, :], tg[:, 2:3],
                                                       xs[:, ds(T4 * g + tt, 1), :], ALU.mult, ALU.add
                                                       ).then_inc(x1_done, 1)

            def attention_stage(half):
                scan_ended(dve, half)
                dve.wait_ge(attc_in[half], 80)
                dve.wait_ge(rt_split, 2 * half + 1)
                nc.vector.tensor_tensor(rtl[:], rtw[:], rth[:].bitcast(f32), ALU.subtract).then_inc(rt_split, 1)
                stats(xs, abn, amv, a_bn, a_mv, HB * half)
                if half:
                    for c in range(KC):
                        dve.wait_ge(wah2, c + 1)
                        nc.vector.tensor_tensor(wal[:, c, :], wagain[c % 2], wah[:, c, :].bitcast(f32),
                                                ALU.subtract).then_inc(wal2, 1)
                for g in range(HB * half, HB * half + HB):
                    U0 = 32 * g
                    for k in range(KC):
                        dve.wait_ge(h1_hi, KC * g + k + 1)
                        nc.vector.scalar_tensor_tensor(h1l[:, k, :], bank[k], wln[:, 0, k:k + 1],
                                                       h1h[:, k, :].bitcast(f32), ALU.mult, ALU.subtract
                                                       ).then_inc(h1_lo, 1)
                    for tt in range(T4):
                        dve.wait_ge(v_mm, T4 * g + tt + 1)
                        nc.vector.tensor_tensor(V[:, tt, :], bank[tt], bvb[:], ALU.add).then_inc(v_done, 1)
                    for m in range(8):
                        dve.wait_ge(rot_mm, 8 * g + m + 1 + C2)
                        dve.wait_ge(qk_done, 8 * g + m - 1 + C2)
                        f = SCALE if m < T4 else 1.0
                        nc.vector.scalar_tensor_tensor(RS[:, m % 2, :], bank[6 + m % 2], f, rope[:, 1, :],
                                                       ALU.mult, ALU.mult).then_inc(rope_s, 1)
                        dve.wait_ge(rope_s, 8 * g + m + 1 + C2)
                        dve.wait_ge(rope_c, 8 * g + m + 1 + C2)
                        nc.vector.scalar_tensor_tensor(QK[:, m, :], RC[:, m % 2, :], f, RS[:, m % 2, :],
                                                       ALU.mult, ALU.add).then_inc(qk_done, 1)

                    def row_max(u):
                        W = P * (u // (NH // 2) + 1)
                        dve.wait_ge(s_mm, U0 + u + 1)
                        nc.vector.tensor_reduce(nm[:, u % 2, :], SB[u % 2][:, :, 0:W], AX.X, ALU.max, negate=True
                                                ).then_inc(mx_done, 1)

                    def norm_probs(u):
                        W = P * (u // (NH // 2) + 1)
                        dve.wait_ge(ex_done, U0 + u + 1 + C2)
                        nc.vector.reciprocal(ri[:, u % 2, :], rs[:, u % 2, :]).then_inc(ri_done, 1)
                        dve.wait_ge(ri_done, U0 + u + 1)
                        for a in range(2):
                            ins = nc.vector.tensor_scalar(EX[:, u % 2, a, 0:W], EX[:, u % 2, a, 0:W],
                                                          ri[:, u % 2, a:a + 1], None, ALU.mult)
                        ins.then_inc(p_done, 1)

                    def copy_odd(u):
                        W = P * (u // (NH // 2) + 1)
                        dve.wait_ge(t_mm, U0 + u + 1 + C2)
                        dve.wait_ge(pv_mm, U0 + u - 1 + C2)
                        nc.vector.tensor_copy(PT[:, u % 2, 1, 0:W], PB[:, 1, 0:W]).then_inc(pt_b, 1)

                    def finish(i, step):
                        t = T4 * g + i
                        if step == 0:
                            dve.wait_ge(cth_done, t + 1)
                            nc.vector.tensor_tensor(ctl[:], CX.rearrange("p (k t) -> p k t", k=KC),
                                                    cth[:].bitcast(f32), ALU.subtract).then_inc(ctl_done, 1)
                        if step == 1:
                            dve.wait_ge(wo_mm, t + 1)
                            nc.vector.tensor_tensor(XL[:, i, :], WK, XL[:, i, :], ALU.add).then_inc(xm_done, 1)
                            dve.wait_ge(xm_done, t + 1)
                            nc.vector.scalar_tensor_tensor(xs[:, ds(t, 1), :], XL[:, i, :], tg[:, 1:2],
                                                           xs[:, ds(t, 1), :], ALU.mult, ALU.add
                                                           ).then_inc(xacc_done, 1)
                        if step == 2:
                            dve.wait_ge(h2_mm, t + 1)
                            nc.vector.tensor_tensor(hw[:], WK.rearrange("p (k t) -> p k t", k=KC),
                                                    wln[:, 1, :].unsqueeze(2).broadcast_to([P, KC, P]),
                                                    ALU.mult).then_inc(hw_done, 1)
                        if step == 3:
                            dve.wait_ge(rt_mm, t + 1)
                            nc.vector.tensor_copy(lg[:, T4 * (g % HB) + i, :], WK[:, 0:ROUTE]).then_inc(lg_done, 1)

                    row_max(0)
                    row_max(1)
                    norm_probs(0)
                    for u in range(32):
                        if u >= 8 and u % 8 == 0:
                            finish(u // 8 - 1, 0)
                        if u + 1 < 32:
                            norm_probs(u + 1)
                        copy_odd(u)
                        if u + 2 < 32:
                            row_max(u + 2)
                        if u >= 8 and u % 8 in (1, 4, 6):
                            finish(u // 8 - 1, (1, 4, 6).index(u % 8) + 1)
                        if u == 15 and g % HB < HB - 1:
                            stats(xs, abn, amv, a_bn, a_mv, g + 1)
                    for step in range(4):
                        finish(3, step)

            def gating(half):
                tiles = slice(TH * half, TH * half + TH)
                n = [GT * half]

                def step_(ins):
                    n[0] = n[0] + 1
                    ins.then_inc(gt, 1)
                    dve.wait_ge(gt, n[0])

                step_(nc.vector.tensor_reduce(gs[:, 0, :], lg[:, :, 0:NE], AX.X, ALU.max, negate=True))
                step_(nc.vector.tensor_tensor(pr[:, 0], lg[:, :, 0:NE],
                                              gs[:, 0, :].unsqueeze(2).broadcast_to([P, TH, NE]), ALU.add))
                dve.wait_ge(gt_e, half + 1)
                step_(nc.vector.tensor_reduce(gs[:, 1, :], pr[:, 1], AX.X, ALU.add))
                step_(nc.vector.reciprocal(gs[:, 2, :], gs[:, 1, :]))
                step_(nc.vector.tensor_tensor(pr[:, 2], pr[:, 1],
                                              gs[:, 2, :].unsqueeze(2).broadcast_to([P, TH, NE]), ALU.mult))
                nc.vector.memset(tick[:], 0.0).then_inc(gt, 1)
                for t in range(TH):
                    nc.vector.max(m8[:, t, :], pr[:, 2, t, :]).then_inc(gt, 1)
                n[0] = n[0] + 1 + TH
                dve.wait_ge(gt, n[0])
                nc.vector.memset(tick[:], 0.0).then_inc(gt, 1)
                for t in range(TH):
                    nc.vector.max_index(i8[:, t, :], m8[:, t, :], pr[:, 2, t, :]).then_inc(gt, 1)
                n[0] = n[0] + 1 + TH
                dve.wait_ge(gt, n[0])
                step_(nc.vector.tensor_copy(i8f[:], i8[:, :, 0:2]))
                for t in range(TH):
                    for j in range(2):
                        step_(nc.vector.tensor_scalar(cc[:, j, t, :], iota8[:], i8f[:, t, j:j + 1],
                                                      m8[:, t, j:j + 1], ALU.is_equal, ALU.mult))
                step_(nc.vector.tensor_tensor(cc[:, 0], cc[:, 0], cc[:, 1], ALU.add))
                dve.wait_ge(gt_t, half + 1)
                step_(nc.vector.tensor_scalar(gs[:, 0, :], gs[:, 3, :], 1.0, tgq[:, 0:1], ALU.add, ALU.mult))
                step_(nc.vector.tensor_scalar(cmb[:, tiles, 0:NE], cc[:, 0], tg[:, 3:4], None, ALU.mult))
                nc.vector.tensor_copy(cmb[:, tiles, NE:NU],
                                      gs[:, 0, :].unsqueeze(2).broadcast_to([P, TH, NU - NE])
                                      ).then_inc(att_done, 1)

            def expert_stage(half):
                attention_ended(dve, half)
                gating(half)
                dve.wait_ge(att_done, half + 1 + C1)

                def unit(k, place=lambda j, late=False: None, more=True):
                    S0 = NG * NCH * k

                    def act_of(s):
                        rows = slice(0, CW[s % NCH])
                        dve.wait_ge(f_t, S0 + s + 1)
                        dve.wait_ge(f_a, S0 + s - 1 + C2)
                        nc.vector.scalar_tensor_tensor(fp[rows, s % 2, :], ft[rows, s % 2, :], 1.0,
                                                       FG[s % 2][rows, :], ALU.add, ALU.mult).then_inc(f_p, 1)
                        dve.wait_ge(f_p, S0 + s + 1 + C2)
                        dve.wait_ge(f_ah, S0 + s - 1 + C2)
                        dve.wait_ge(f_al, S0 + s - 1 + C2)
                        nc.vector.tensor_tensor(fa[rows, s % 2, :], FU[s % 2][rows, :], fp[rows, s % 2, :],
                                                ALU.mult).then_inc(f_a, 1)

                    def add(tt):
                        dve.wait_ge(d_mm, TH * k + tt + 1 + C1)
                        dve.wait_ge(d_acc, TH * k + tt - TH + 1 + C_DA)
                        w = k - NU * half
                        w = slice(w, w + 1) if isinstance(w, int) else ds(w, 1)
                        nc.vector.scalar_tensor_tensor(xs[:, TH * half + tt, :], FD[tt % 2],
                                                       cmb[:, TH * half + tt, w],
                                                       xs[:, TH * half + tt, :], ALU.mult, ALU.add
                                                       ).then_inc(d_acc, 1)

                    for s in range(NG * NCH):
                        place(2 * s)
                        if s:
                            act_of(s - 1)
                            place(2 * s - 1, True)
                        place(2 * s + 1)
                        place(2 * s, True)
                    D0 = 2 * NG * NCH
                    place(D0)
                    act_of(NG * NCH - 1)
                    place(D0 - 1, True)
                    add(0)
                    place(D0, True)
                    for n in range(1, T4):
                        place(D0 + n)
                        add(2 * n - 1)
                        add(2 * n)
                        place(D0 + n, True)
                    add(TH - 1)

                def before(g, j, late=False):
                    if not late:
                        return
                    if j < 2:
                        for t in (2 * j, 2 * j + 1):
                            nc.vector.bn_stats(ebn[:, t, :], xs[:, T4 * g + t, :]).then_inc(z_bn, 1)
                    if j == 3:
                        dve.wait_ge(z_bn, (T4 + 1) * g + T4)
                        nc.vector.memset(tick[:], 0.0).then_inc(z_bn, 1)
                        for t in range(T4):
                            nc.vector.bn_aggr(emv[:, t, :], ebn[:, t, :]).then_inc(z_mv, 1)
                    if j in (2, 4, 6, 8):
                        et = j // 2 - 1
                        dve.wait_ge(cv_init, T4 * g + et + 1)
                        for sh in range(1, TAPS):
                            if sh > 1:
                                dve.wait_ge(cv_tap, 12 * g + 3 * et + sh - 1)
                            tap = TAPS - 1 - sh
                            nc.vector.scalar_tensor_tensor(eDL[:, et, sh:L], EB[et % 2][:, 0:L - sh],
                                                           chan[:, et, tap:tap + 1], eDL[:, et, sh:L],
                                                           ALU.mult, ALU.add).then_inc(cv_tap, 1)
                    if j in (4, 6, 8, 10):
                        et = j // 2 - 2
                        dve.wait_ge(u_t4, T4 * (g - HB) + et + 1)
                        nc.vector.scalar_tensor_tensor(eDU[:, et, :], eYA[:, et, :], 1.0, eDL[:, et, :],
                                                       ALU.add, ALU.mult).then_inc(u_d4, 1)
                    if j in (13, 15):
                        dve.wait_ge(z_t4, 2 * (g - HB) + (j - 13) // 2 + 1)
                        r = slice(j - 13, j - 11)
                        nc.vector.scalar_tensor_tensor(eZS[:, r, :], eYA[:, r, :], 1.0, eZS[:, r, :],
                                                       ALU.add, ALU.mult).then_inc(z_d4, 1)
                    if j in (17, 19, 21, 23):
                        et = (j - 17) // 2
                        dve.wait_ge(dt_abs, T4 * g + et + 1)
                        nc.vector.tensor_scalar(eDL[:, et, :], EB[et % 2], chan[:, et, TAPS + 1:TAPS + 2], 0.0,
                                                ALU.add, ALU.max).then_inc(dt_rel, 1)
                    if j == 26:
                        dve.wait_ge(dt_l, g + 1 - HB)
                        nc.vector.tensor_tensor(eDL[:], eDL[:], eYA[:], ALU.add).then_inc(dl_done, 1)
                        dve.wait_ge(dl_done, g + 1 - HB)
                    if j in (27, 28, 29, 30):
                        tt = j - 27
                        dve.wait_ge(yi_mm, T4 * g + tt + 1)
                        nc.vector.tensor_copy(eYA[:, tt, :], EB[tt % 2]).then_inc(yi_done, 1)
                    if j == 31:
                        nc.vector.scalar_tensor_tensor(eDU[:], eDU[:], 0.5, eDL[:], ALU.mult, ALU.mult
                                                       ).then_inc(du_done, 1)

                def step(g, i, j, late=False):
                    q = nth(g, i, j)
                    r = q - T4 * NS * HB
                    if not late:
                        dve.wait_ge(gb4, r + 1 + C_G4)
                        dve.wait_ge(dA_ready, q + 1)
                        dve.wait_ge(hT_ready, q - 1 + C_HT)
                        nc.vector.tensor_tensor_scan(eHS[:, j % 2, :], EB[0], eGB[:, j % 2, :],
                                                     0.0, ALU.mult, ALU.add).then_inc(scan_done, 1)
                    else:
                        dve.wait_ge(hT_ready, q + 1 + C_HT)
                        dve.wait_ge(y4, r - T4 + 1 + C4)
                        et = j % T4
                        for tt in range(T4):
                            ins = nc.vector.scalar_tensor_tensor(eYA[:, tt, et * P:(et + 1) * P],
                                                                 EB[1][:, tt * P:(tt + 1) * P],
                                                                 eCt[:, tt, column(i, j)],
                                                                 eYA[:, tt, et * P:(et + 1) * P],
                                                                 ALU.mult, ALU.add)
                        ins.then_inc(y4, 1)

                def first(g):
                    dve.wait_ge(yi_done, T4 * g + T4)
                    dve.wait_ge(du_done, g + 1)

                def after(g):
                    dve.wait_ge(y4, T4 * NS * (g + 1 - HB) + C4)
                    for tt in range(T4):
                        dve.wait_ge(zT_ready, T4 * g + tt + 1 + C_ZT)
                        nc.vector.tensor_tensor(eYA[:, tt, :], EB[tt % 2], eYA[:, tt, :], ALU.mult
                                                ).then_inc(y_z, 1)
                    for tt in range(T4):
                        dve.wait_ge(y_z, T4 * g + tt + 1)
                        nc.vector.scalar_tensor_tensor(xs[:, T4 * g + tt, :], eYA[:, tt, :], tg[:, 2:3],
                                                       xs[:, T4 * g + tt, :], ALU.mult, ALU.add
                                                       ).then_inc(x1_done, 1)

                if half:
                    with dve.Fori(NU, 2 * NU) as k:
                        unit(k)
                else:
                    for et in range(T4):
                        nc.vector.tensor_scalar(eddiag[:, et, :], ident[:], chan[:, et, TAPS + 2:TAPS + 3], 0.5,
                                                ALU.mult, ALU.mult).then_inc(ddiag_s, 1)
                    beside(unit, before, step, after)(dve, first)

            scan_stage(0)
            for half in range(2):
                attention_stage(half)
                expert_stage(half)

        @block.gpsimd
        def _(pool):
            pool.sem_inc(gb_ready, C_GB)
            pool.sem_inc(gb4, C_G4)
            pool.sem_inc(wal_done, C_WL)
            pool.sem_inc(rope_c, C2)
            pool.sem_inc(f_al, C2)
            pool.sem_inc(wgl_s, C1)
            pool.sem_inc(wdl_s, C1)
            for row, value in ((mhalf, -0.5), (eps5, 1e-5), (eps6, 1e-6), (mone, -1.0), (perh, 1.0 / H)):
                nc.gpsimd.memset(row[:], value).then_inc(rows_made, 1)
            pool.wait_ge(rows_made, 5)

            def scan_stage(half):
                if half:
                    experts_ended(pool, half - 1)
                with pool.Fori(HB * half, HB * half + HB) as g:
                    pool.wait_ge(z_mv, T4 * g + T4)
                    nc.gpsimd.tensor_tensor(zst[:, 0, :], mv[:, :, 1], eps5[:], ALU.add).then_inc(z_norm, 1)
                    pool.wait_ge(z_norm, 4 * g + 1)
                    nc.gpsimd.tensor_tensor(zst[:, 1, :], zst[:, 0, :], mhalf[:], ALU.pow).then_inc(z_norm, 1)
                    pool.wait_ge(z_norm, 4 * g + 2)
                    nc.gpsimd.tensor_tensor(zst[:, 2, :], mv[:, :, 0], zst[:, 1, :], ALU.mult).then_inc(z_norm, 1)
                    pool.wait_ge(z_norm, 4 * g + 3)
                    nc.gpsimd.tensor_tensor(zst[:, 3, :], zst[:, 2, :], mone[:], ALU.mult).then_inc(z_norm, 1)
                    for c in range(KC // HB):
                        q = (KC // HB) * g + c
                        pool.wait_ge(wah_done, q + 1)
                        k = (g - HB * half) * (KC // HB) + c
                        nc.gpsimd.tensor_tensor(wal[:, ds(k, 1), :], wraw[:].unsqueeze(1),
                                                wah[:, ds(k, 1), :].bitcast(f32),
                                                ALU.subtract).then_inc(wal_done, 1)
                    with pool.Fori(0, NS // NL) as i:
                        pool.wait_ge(du_done, g + 1)
                        pool.wait_ge(yi_done, T4 * g + T4)
                        for n in range(NL):
                            step = NS * g + NL * i + n
                            if n % 2 == 0:
                                pool.wait_ge(bb_in[n // 2], 16 * ((NS // NL) * g + i + 1))
                            pool.wait_ge(scan_done, T4 * step - T4 + C_SC)
                            nc.gpsimd.tensor_tensor(GB[:, n % 2], DU[:],
                                                    BB[:, n // 2, n % 2, :].unsqueeze(1).broadcast_to([P, T4, L]),
                                                    ALU.mult).then_inc(gb_ready, 1)

            def attention_stage(half):
                scan_ended(pool, half)
                pool.wait_ge(attc_in[half], 80)
                def norms(g):
                    def norm(n, ins):
                        ins.then_inc(a_norm, 1)
                        pool.wait_ge(a_norm, 8 * g + n)

                    if g:
                        pool.wait_ge(a_hp, T4 * g)
                    pool.wait_ge(a_mv, T4 * g + T4)
                    var, mean = amv[:, :, 1], amv[:, :, 0]
                    norm(1, nc.gpsimd.tensor_tensor(ast[:, 0, :], var, eps5[:], ALU.add))
                    norm(2, nc.gpsimd.tensor_tensor(ast[:, 1, :], ast[:, 0, :], mhalf[:], ALU.pow))
                    norm(3, nc.gpsimd.tensor_tensor(ast[:, 3, :], mean, ast[:, 1, :], ALU.mult))
                    norm(4, nc.gpsimd.tensor_tensor(ast[:, 2, :], ast[:, 3, :], mone[:], ALU.mult))
                    norm(5, nc.gpsimd.tensor_tensor(ast[:, 4, :], ast[:, 1, :], ast[:, 1, :], ALU.mult))
                    norm(6, nc.gpsimd.tensor_tensor(ast[:, 5, :], var, ast[:, 4, :], ALU.mult))
                    norm(7, nc.gpsimd.tensor_tensor(ast[:, 7, :], ast[:, 5, :], eps6[:], ALU.add))
                    norm(8, nc.gpsimd.tensor_tensor(ast[:, 6, :], ast[:, 7, :], mhalf[:], ALU.pow))

                norms(HB * half)
                for g in range(HB * half, HB * half + HB):
                    for m in range(8):
                        pool.wait_ge(qb_ready, 8 * g + m + 1 + C2)
                        pool.wait_ge(qk_done, 8 * g + m - 1 + C2)
                        nc.gpsimd.tensor_tensor(RC[:, m % 2, :], QB[:, m % 2, :], rope[:, 0, :], ALU.mult
                                                ).then_inc(rope_c, 1)
                    for i in range(T4):
                        t = T4 * g + i
                        if i == T4 - 2 and g % HB < HB - 1:
                            norms(g + 1)
                        pool.wait_ge(sq_done, t + 1)
                        nc.gpsimd.tensor_tensor(r2[:, 2, i:i + 1], ss[:, i:i + 1], perh[:, 0:1], ALU.mult
                                                ).then_inc(r2_s, 1)
                        pool.wait_ge(r2_s, 3 * t + 1)
                        nc.gpsimd.tensor_tensor(r2[:, 0, i:i + 1], r2[:, 2, i:i + 1], eps6[:, 0:1], ALU.add
                                                ).then_inc(r2_s, 1)
                        pool.wait_ge(r2_s, 3 * t + 2)
                        nc.gpsimd.tensor_tensor(r2[:, 1, i:i + 1], r2[:, 0, i:i + 1], mhalf[:, 0:1], ALU.pow
                                                ).then_inc(r2_s, 1)
                        pool.wait_ge(h2h_done, t + 1)
                        nc.gpsimd.tensor_tensor(h2l[:, :, ds((g - HB * half) * L + i * P, P)], hw[:],
                                                cth[:].bitcast(f32), ALU.subtract).then_inc(h2l_kept, 1)
                        nc.gpsimd.tensor_tensor(ctl[:], hw[:], cth[:].bitcast(f32), ALU.subtract
                                                ).then_inc(h2l_done, 1)

            def expert_stage(half):
                attention_ended(pool, half)

                def split(k, c):
                    pool.wait_ge(wgh_s, KC * k + c + 1)
                    nc.gpsimd.tensor_tensor(wgl[:, c, :], wgr[:, c * 2 * EI:(c + 1) * 2 * EI],
                                            wgh[:, c, :].bitcast(f32), ALU.subtract).then_inc(wgl_s, 1)

                def unit(k, place=lambda j: None, more=True):
                    S0 = NG * NCH * k

                    def rest(s):
                        grp, c = divmod(s, NCH)
                        pool.wait_ge(f_ah, S0 + s + 1 + C2)
                        cols = slice(grp * L, (grp + 1) * L)
                        nc.gpsimd.tensor_tensor(fal[0:CW[c], c, cols], fa[0:CW[c], s % 2, :],
                                                fah[0:CW[c], c, cols].bitcast(f32), ALU.subtract).then_inc(f_al, 1)

                    for s in range(NG * NCH + 1):
                        place(2 * s)
                        if s < NG * NCH:
                            place(2 * s + 1)
                        if s:
                            rest(s - 1)
                        if 1 <= s <= NCH:
                            c = s - 1
                            pool.wait_ge(wdh_s, NCH * k + c + 1)
                            nc.gpsimd.tensor_tensor(wdl[:, c, :], wdr[:, c * H:(c + 1) * H],
                                                    wdh[:, c, :].bitcast(f32), ALU.subtract).then_inc(wdl_s, 1)
                    for c in range(KC):
                        if c < KC - 1:
                            place(2 * NG * NCH + 1 + c)
                        if more:
                            split(k + 1, c)

                def before(g, j):
                    if j == 5:
                        pool.wait_ge(z_mv, T4 * g + T4)
                        nc.gpsimd.tensor_tensor(ezst[:, 0, :], emv[:, :, 1], eps5[:], ALU.add).then_inc(z_norm, 1)
                        pool.wait_ge(z_norm, 4 * g + 1)
                        nc.gpsimd.tensor_tensor(ezst[:, 1, :], ezst[:, 0, :], mhalf[:], ALU.pow).then_inc(z_norm, 1)
                        pool.wait_ge(z_norm, 4 * g + 2)
                        nc.gpsimd.tensor_tensor(ezst[:, 2, :], emv[:, :, 0], ezst[:, 1, :], ALU.mult
                                                ).then_inc(z_norm, 1)
                        pool.wait_ge(z_norm, 4 * g + 3)
                        nc.gpsimd.tensor_tensor(ezst[:, 3, :], ezst[:, 2, :], mone[:], ALU.mult).then_inc(z_norm, 1)

                def first(g):
                    pool.wait_ge(du_done, g + 1)

                def step(g, i, j):
                    q = nth(g, i, j)
                    if j % T4 == 0:
                        n = j // T4
                        pool.wait_ge(bb_in[n % 2], 16 * (HB * (NS // NL) + (NS // 2) * (g - HB) + n // 2 + 1) + 32 * i)
                    pool.wait_ge(scan_done, q - 1 + C_SC)
                    nc.gpsimd.tensor_tensor(eGB[:, j % 2, :], eDU[:, j % T4, :], eBB[:, (j // T4) % 2, :], ALU.mult
                                            ).then_inc(gb4, 1)

                for c in range(KC):
                    split(NU * half, c)
                if half:
                    with pool.Fori(NU, 2 * NU - 1) as k:
                        unit(k)
                    unit(2 * NU - 1, more=False)
                else:
                    beside(unit, before, step, lambda g: None)(pool, first)

            scan_stage(0)
            for half in range(2):
                attention_stage(half)
                expert_stage(half)


def host_layout(inputs):
    a = {k: np.asarray(v) for k, v in inputs.items()}
    f = np.float32

    def rows(w, k):
        return w.reshape(k, P, -1).transpose(1, 0, 2)

    x = a["x"].reshape(2, HB, T4, P, H).transpose(0, 3, 1, 2, 4).reshape(2, P, TH, H)
    c = a["ctx_1024"].reshape(2, HB, L, DC // P, P).transpose(0, 4, 1, 3, 2)
    chan = np.concatenate([a["L0_xattn_conv_w"], a["L0_xattn_conv_b"][:, None], a["L0_xattn_dt_proj_b"][:, None],
                           a["L0_xattn_D"][:, None], a["L0_xattn_A_log"]], axis=1)
    bqk = np.concatenate([a["L0_ffn_bq"].reshape(T4, P).T, a["L0_ffn_bk"].reshape(T4, P).T], axis=1)
    watt = np.concatenate([a["L0_ffn_wq"], a["L0_ffn_wk"], a["L0_ffn_wv"], a["L0_ffn_wo"]], axis=1)
    route = np.concatenate([a["L0_ffn_w_router"], a["L0_ffn_w_sh_eg"], np.zeros((H, 1), f)], axis=1)
    wln = np.stack([a["L0_ffn_w_ln1"].reshape(KC, P).T, a["L0_ffn_w_ln2"].reshape(KC, P).T], axis=1)

    def units(experts, shared, axis):
        return np.concatenate([experts, np.stack(np.split(shared, NU - NE, axis=axis))], axis=0)

    gate = units(a["L0_ffn_w_gate_e"], a["L0_ffn_w_sh_gate"], 1)
    up = units(a["L0_ffn_w_up_e"], a["L0_ffn_w_sh_up"], 1)
    down = units(a["L0_ffn_w_down_e"], a["L0_ffn_w_sh_down"], 0)
    gu = np.concatenate([gate, up], axis=2).reshape(NU, KC, P, 2 * EI).transpose(0, 2, 1, 3).reshape(NU, P, GW)
    dn = np.concatenate([down, np.zeros((NU, NCH * P - EI, H), f)], axis=1)
    dn = dn.reshape(NU, NCH, P, H).transpose(0, 2, 1, 3).reshape(NU, P, DW)

    inv = (f(1.0) / np.power(f(1000000.0), np.arange(0, HD, 2, dtype=f) / f(HD))).astype(f)
    ang = (np.arange(L, dtype=f)[:, None] * inv[None, :]).astype(f).T
    cos, sin = np.cos(ang).astype(f), np.sin(ang).astype(f)
    rope = np.stack([np.tile(np.concatenate([cos, cos]), (P // HD, 1)),
                     np.tile(np.concatenate([-sin, sin]), (P // HD, 1))], axis=1)
    d = np.arange(P)
    perm = np.zeros((P, P), f)
    perm[d, d ^ (HD // 2)] = 1.0
    q = np.arange(P)
    mask = np.where(q[None, :] <= q[:, None], f(0.0), f(MASKED)).astype(f)
    arrays = {
        "x_in": x, "ctx_in": c, "gates_in": np.concatenate([a["g_xattn"], a["g_ffn"]]),
        "w_in_in": rows(a["L0_xattn_in_proj_w"].T, DC // P), "chan_in": rows(chan, T4),
        "xproj_in": rows(a["L0_xattn_x_proj_w"].T, T4), "dtproj_in": a["L0_xattn_dt_proj_w"].T,
        "watt_in": rows(watt, KC), "bqk_in": bqk, "bv_in": a["L0_ffn_bv"], "wln_in": wln,
        "route_in": rows(route, KC), "wffn_in": np.concatenate([gu, dn], axis=2),
        "rope_in": rope, "perm_in": perm, "ident_in": np.eye(P, dtype=f), "mask_in": mask,
        "iota_in": np.arange(NE, dtype=f),
    }
    return {k: np.ascontiguousarray(v) for k, v in arrays.items()}


def kernel(**inputs):
    import concourse.bacc as bacc
    from concourse.bass_utils import run_bass_kernel_spmd

    nc = bacc.Bacc("TRN2", target_bir_lowering=False, num_devices=1, dynamic_dma_scratch_size=1024)
    arrays = host_layout(inputs)
    args = [nc.dram_tensor(n, v.shape, mybir.dt.from_np(v.dtype), kind="ExternalInput").ap()
            for n, v in arrays.items()]
    out = nc.dram_tensor("out", (2, P, TH, H), mybir.dt.float32, kind="ExternalOutput").ap()
    b_scratch = nc.dram_tensor("b_scratch", (B, NS, L), mybir.dt.float32).ap()
    build(nc, *args, out, b_scratch)
    r = run_bass_kernel_spmd(nc, [arrays], core_ids=[0])
    got = r.results[0]["out"]
    return got.reshape(2, P, HB, T4, H).transpose(0, 2, 3, 1, 4).reshape(B, L, H)
```

```python
import numpy as np
from contextlib import ExitStack

import concourse.bass as bass
from concourse import mybir

B, L, H = 4, 512, 512
DC = 256
DI, NS, DR = 512, 16, 16
TAPS = 4
NH, HD = 16, 32
NE, EI, SI = 8, 352, 1408
NU = 12
P = 128
T4 = L // P
KC = H // P
HB = 2
TH = HB * T4
NCH = -(-EI // P)
SHORT = -(-SI // P) - (NU - NE - 1) * NCH
EW = NCH * P
NG = HB
GW = KC * 2 * EW
DW = NCH * H
ROUTE = 10

MASKED = -3.0e38


def build(nc, x_in, ctx_in, gates_in, w_in_in, chan_in, xproj_in, dtproj_in, watt_in, bqk_in,
          bv_in, wln_in, route_in, wffn_in, rope_in, perm_in, ident_in, mask_in, iota_in, out,
          b_scratch):
    f32, f32r, bf16, u32 = (mybir.dt.float32, mybir.dt.float32r, mybir.dt.bfloat16,
                            mybir.dt.uint32)
    ALU, ACT, AX = mybir.AluOpType, mybir.ActivationFunctionType, mybir.AxisListType
    ds = bass.ds
    SCALE = float(HD) ** -0.5

    ctx = ExitStack()
    with ctx:
        def sem(name):
            return ctx.enter_context(nc.semaphore(name))

        def pb(name, shape):
            return ctx.enter_context(nc.psum_tensor(name, shape, f32))

        def arena(stack):
            return lambda name, shape, dt=f32: stack.enter_context(nc.sbuf_tensor(name, shape, dt))

        keep = arena(ctx)
        xs = keep("xs", [P, B * T4, H])
        ident = keep("ident", [P, P])
        identb = keep("identb", [P, P], bf16)
        mask = keep("mask", [P, P])
        maskb = keep("maskb", [P, P], bf16)
        chan = keep("chan", [P, T4, TAPS + 3 + NS])
        aneg = keep("aneg", [P, T4, NS])
        gates = keep("gates", [P, 2])
        tg = keep("tg", [P, 4])
        tgq = keep("tgq", [P, 1])
        mhalf, eps5, eps6, mone, perh = [keep(n, [P, T4]) for n in ("mhalf", "eps5", "eps6", "mone", "perh")]
        tick = keep("tick", [P, 1])
        wln = keep("wln", [P, 2, KC])
        cmb = keep("cmb", [P, B * T4, NU])
        iota8 = keep("iota8", [P, NE])
        abn = keep("abn", [P, T4, 6])
        amv = keep("amv", [P, T4, 2])
        ast = keep("ast", [P, 8, T4])
        lg = keep("lg", [P, TH, ROUTE])
        pr = keep("pr", [P, 3, TH, NE])
        gs = keep("gs", [P, 4, TH])
        m8 = keep("m8", [P, TH, 8])
        i8 = keep("i8", [P, TH, 8], u32)
        i8f = keep("i8f", [P, TH, 2])
        cc = keep("cc", [P, 2, TH, NE])

        sa = ExitStack()
        mid = arena(sa)
        h1h = mid("h1h", [P, KC, L], f32r)
        h1l = mid("h1l", [P, KC, L], f32r)
        wah = mid("wah", [P, KC, 4 * H], f32r)
        wal = mid("wal", [P, KC, 4 * H], f32r)

        s1 = ExitStack()
        scn = arena(s1)
        wraw = scn("wraw", [P, 4 * H])
        w_in = scn("w_in", [P, DC // P, DI])
        xproj = scn("xproj", [P, T4, DR + 2 * NS])
        dtproj = scn("dtproj", [DR, DI])
        ddiag = scn("ddiag", [P, T4, P])
        cT = scn("cT", [P, HB, DC // P, L])
        DL = scn("DL", [P, T4, L])
        DU = scn("DU", [P, T4, L])
        ZS = scn("ZS", [P, T4, L])
        YA = scn("YA", [P, T4, L])
        HS = scn("HS", [P, 2, T4, L])
        GB = scn("GB", [P, 2, T4, L])
        T2, T1 = HS[:, 0], HS[:, 1]
        U2 = GB[:, 0]
        xd = scn("xd", [DR + 2 * NS, L])
        Ct = scn("Ct", [P, T4, NS])
        BB = scn("BB", [P, 2, 2, L])
        bn6 = scn("bn6", [P, T4, 6])
        mv = scn("mv", [P, T4, 2])
        zst = scn("zst", [P, 4, T4])
        s1.close()

        h2h = ctx.enter_context(nc.sbuf_tensor("h2h", [P, KC, HB * L], f32r, side="right"))
        h2l = ctx.enter_context(nc.sbuf_tensor("h2l", [P, KC, HB * L], f32r, side="right"))

        s2 = ExitStack()
        att = arena(s2)
        bqk = att("bqk", [P, 2 * T4])
        bvb = att("bvb", [P, H])
        rope = att("rope", [P, 2, L])
        perm = att("perm", [P, P])
        rtw = att("rtw", [P, KC, ROUTE])
        rth = att("rth", [P, KC, ROUTE], f32r)
        rtl = att("rtl", [P, KC, ROUTE], f32r)
        XL = att("XL", [P, T4, H])
        hp = att("hp", [P, T4, H])
        QK = att("QK", [P, 2 * T4, L])
        V = att("V", [P, T4, H])
        EX = att("EX", [P, 2, 2, L])
        PT = att("PT", [P, 2, 2, L])
        QB, RC, RS = EX[:, 0], EX[:, 1], PT[:, 0]
        wagain = [t[:].rearrange("p a b l -> p (a b l)") for t in (EX, PT)] + [
            QK[:, 4 * c:4 * c + 4, :].rearrange("p a l -> p (a l)") for c in range(2)]
        nm = att("nm", [P, 2, 2])
        rs = att("rs", [P, 2, 2])
        ri = att("ri", [P, 2, 2])
        sq = att("sq", [P, H])
        cth = att("cth", [P, KC, P], f32r)
        ctl = att("ctl", [P, KC, P], f32r)
        hw = att("hw", [P, KC, P])
        ss = att("ss", [P, T4])
        r2 = att("r2", [P, 3, T4])
        s2.close()
        sa.close()

        s3 = ExitStack()
        exa = arena(s3)
        wgr = exa("wgr", [P, GW])
        ft = exa("ft", [P, 2, L])
        wdr = exa("wdr", [P, DW])
        wgh = exa("wgh", [P, KC, 2 * EW], f32r)
        wgl = exa("wgl", [P, KC, 2 * EW], f32r)
        wdh = exa("wdh", [P, NCH, H], f32r)
        wdl = exa("wdl", [P, NCH, H], f32r)
        fah = exa("fah", [P, NCH, HB * L], f32r)
        fal = exa("fal", [P, NCH, HB * L], f32r)
        fa = exa("fa", [P, 2, L])
        ew_in = exa("ew_in", [P, DC // P, DI])
        exproj = exa("exproj", [P, T4, DR + 2 * NS])
        edtproj = exa("edtproj", [DR, DI])
        eddiag = exa("eddiag", [P, T4, P])
        ecT = exa("ecT", [P, HB, DC // P, L])
        eDL = exa("eDL", [P, T4, L])
        eDU = exa("eDU", [P, T4, L])
        eZS = exa("eZS", [P, T4, L])
        eYA = exa("eYA", [P, T4, L])
        eHS = exa("eHS", [P, 2, L])
        eGB = exa("eGB", [P, 2, L])
        exd = exa("exd", [DR + 2 * NS, L])
        eCt = exa("eCt", [P, T4, NS])
        eBB = exa("eBB", [P, 2, L])
        ebn = exa("ebn", [P, T4, 6])
        emv = exa("emv", [P, T4, 2])
        ezst = exa("ezst", [P, 4, T4])
        s3.close()

        A01 = pb("A01", [P, 2, L])
        A23 = pb("A23", [P, 2, L])
        A45 = pb("A45", [P, 2, L])
        A67 = pb("A67", [P, 2, L])
        bank = [t[:, k, :] for t in (A01, A23, A45, A67) for k in range(2)]
        Q = bank[0:4]
        DA = bank[4:6]
        HT = bank[6:8]
        SB = [A01, A23]
        PB = A45
        CX, WK = bank[6], bank[7]
        FG, FU, FD = bank[0:2], bank[2:4], bank[4:6]
        EB = bank[6:8]
        UQ = NU // HB
        UP = 2
        UN = UQ - UP
        SU = 16

        const_in = sem("const_in")
        x_in_s = [sem(f"x_loaded{h}") for h in range(2)]
        ctx_in_s = [sem(f"ctx_loaded{h}") for h in range(2)]
        consts = sem("consts")
        scanw_in = [sem(f"scan_weights_loaded{h}") for h in range(2)]
        ddiag_s = sem("ddiag_made")
        rows_made = sem("rows_of_constants_made")
        z_bn, z_mv, z_norm, z_n, z_t, z_done = [sem("z_" + n) for n in
                                                ("stats", "meanvar", "norm", "normed", "tanh", "done")]
        xp_mm, cv_init, cv_tap, u_t, u_done = [sem(n) for n in
                                               ("inproj_ready", "conv_started", "conv_tap", "u_tanh", "u_done")]
        xd_mm, xd_ready, b_stored = sem("xdbl_product"), sem("xdbl_ready"), sem("b_stored")
        bb_in = [sem("b_rows_loaded0"), sem("b_rows_loaded1")]
        ct_mm, ct_ready = sem("c_transposed"), sem("c_ready")
        dt_mm, dt_abs, dt_rel, dt_e, dt_l, dl_done, du_done = [sem("delta_" + n) for n in
                                                               ("product", "abs", "relu", "exp", "log", "done", "times_u")]
        yi_mm, yi_done, zT_ready = sem("du_term_product"), sem("y_started"), sem("z_transposed")
        dA_ready, gb_ready, scan_done = sem("decay_ready"), sem("input_ready"), sem("scan_done")
        hT_ready, y_acc, y_z, x1_done = sem("states_transposed"), sem("y_added"), sem("y_gated"), sem("x1_done")
        wraw_in, wah_done, wal_done = sem("att_weights_loaded"), sem("att_weights_hi"), sem("att_weights_lo")
        attc_in = [sem(f"att_consts_loaded{h}") for h in range(2)]
        rt_split = sem("router_split")
        a_bn, a_mv, a_norm, a_xl, a_hp = [sem("att_" + n) for n in ("stats", "meanvar", "norm", "normed", "scaled")]
        h1_mm, h1_hi, h1_lo = sem("h1_transposed"), sem("h1_hi"), sem("h1_lo")
        v_mm, v_done = sem("v_product"), sem("v_ready")
        qk_mm, qb_ready, rot_mm, rope_c, rope_s, qk_done = [sem(n) for n in
                                                            ("qk_product", "qk_biased", "qk_rotated", "rope_cos", "rope_sin", "qk_ready")]
        s_mm, mx_done, ex_done = sem("scores_ready"), sem("row_max"), sem("probs_ready")
        t_mm, pt_a, pt_b, pv_mm = sem("probs_transposed"), sem("probs_copied_even"), sem("probs_copied_odd"), sem("pv_ready")
        ri_done, p_done, cth_done, ctl_done = [sem(n) for n in
                                               ("row_sum_inverse", "probs_normed", "context_hi", "context_lo")]
        wo_mm, xm_done, xacc_done, sq_done, r2_s, hp2_done = [sem(n) for n in
                                                              ("wo_product", "residual_done", "residual_summed", "square_sum", "rms2", "h2_scaled")]
        h2_mm, hw_done, h2h_kept, h2l_kept, rt_mm, lg_done = [
            sem(n) for n in ("h2_transposed", "h2_weighted", "h2_hi_kept", "h2_lo_kept",
                             "router_product", "logits_ready")]
        gt, gt_e, gt_t, att_done = sem("gating_step"), sem("gating_exp"), sem("gating_tanh"), sem("attention_done")
        wg_in, wd_in = sem("gate_up_loaded"), sem("down_loaded")
        wgh_s, wgl_s, wdh_s, wdl_s = sem("gate_up_hi"), sem("gate_up_lo"), sem("down_hi"), sem("down_lo")
        gu_mm, f_t, f_p, f_a, f_ah, f_al = [sem(n) for n in
                                            ("gate_up_product", "gate_tanh", "gate_done", "act_ready", "act_hi", "act_lo")]
        d_mm, d_acc, stored = sem("down_product"), sem("down_added"), sem("out_stored")

        z_t4, z_d4, u_t4, u_d4 = [sem(n) for n in ("z_tanh_part", "z_done_part", "u_tanh_part", "u_done_part")]
        dt_l4, dl4, du4 = sem("delta_log_part"), sem("delta_done_part"), sem("delta_times_u_part")
        gb_part = sem("input_first_parts")
        gb4, y4 = sem("input_part_ready"), sem("y_part_added")
        watt_in_s = [sem(f"att_weights_loaded_again{c}") for c in range(KC)]
        wah2 = [sem("att_weights_hi_again_even"), sem("att_weights_hi_again_odd")]
        wal2 = [sem("att_weights_lo_again_even"), sem("att_weights_lo_again_odd")]

        C_G4 = 8
        C4 = 4
        C_X1 = 4
        C_BST = 16
        C_ZT = 1
        C_SC = 8
        C_HT = 8
        C_YA = 4
        C_GB = 4
        C_WL = 1
        C_DA = 8
        C2 = 2
        C1 = 1

        NL = 4
        GT = 11 + 4 * TH
        block = ctx.enter_context(nc.Block())

        def beside(unit, before, step, after):
            def run(e, prepare=None):
                for g in range(HB, B):
                    k0 = UQ * (g - HB)
                    for n in range(UP):
                        unit(k0 + n, lambda j, *late, n=n: before(g, SU * n + j, *late))
                    prepare and prepare(g)
                    last = g == B - 1
                    with e.Fori(0, UN - last) as i:
                        unit(i + (k0 + UP), lambda j, *late: step(g, i, j, *late))
                    if last:
                        unit(k0 + UQ - 1, lambda j, *late: step(g, UN - 1, j, *late), more=False)
                    after(g)
            return run

        def chunks(short):
            n = SHORT if short else NCH
            J = 2 * NCH // n
            return [(s // n, s % n, range(J * s, J * s + J)) for s in range(NG * n)]

        def first_chunk(half, k):
            return NG * NCH * k - NG * (NCH - SHORT) * half

        def nth(g, i, j):
            return T4 * NS * g + SU * i + j

        def column(i, j):
            n = i * (SU // T4) + j // T4
            return slice(n, n + 1) if isinstance(n, int) else ds(n, 1)

        def wait_apart(e, what, value):
            e.wait_ge(const_in, 96)
            e.wait_ge(what, value)

        def scan_ended(e, half):
            e.wait_ge(x1_done, T4 * HB * (half + 1) + C_X1)
            if half:
                experts_ended(e, half - 1)
            else:
                e.wait_ge(wal_done, KC + C_WL)

        def attention_ended(e, half):
            e.wait_ge(lg_done, T4 * HB * (half + 1) + C1)
            e.wait_ge(xacc_done, T4 * HB * (half + 1))
            e.wait_ge(h2h_kept, T4 * HB * (half + 1))
            e.wait_ge(h2l_kept, T4 * HB * (half + 1))

        def experts_ended(e, half):
            e.wait_ge(d_acc, NU * TH * (half + 1) + C_DA)

        @block.sync
        def _(sp):
            sp.sem_inc(b_stored, C_BST)

            def scan_stage():
                for dst, src in ((w_in[:], w_in_in), (cT[:, 0], ctx_in[0, :, 0])):
                    sp.dma_start(dst, src).then_inc(ctx_in_s[0], 16)
                for dst, src in ((chan[:], chan_in), (ident[:], ident_in), (mask[:], mask_in),
                                 (gates[:], gates_in.partition_broadcast(P)), (wln[:], wln_in),
                                 (iota8[:], iota_in.partition_broadcast(P))):
                    sp.dma_start(dst, src).then_inc(const_in, 16)
                sp.dma_start(xs[:, 0:TH, :], x_in[0]).then_inc(x_in_s[0], 16)
                for dst, src in ((xproj[:], xproj_in), (dtproj[:], dtproj_in), (cT[:, 1], ctx_in[0, :, 1])):
                    sp.dma_start(dst, src).then_inc(scanw_in[0], 16)
                sp.dma_start(xs[:, TH:2 * TH, :], x_in[1]).then_inc(x_in_s[1], 16)
                with sp.Fori(0, HB) as g:
                    for c in range(KC // HB):
                        sp.wait_ge(wal_done, (KC // HB) * g + c + C_WL)
                        sp.dma_start(wraw[:], watt_in[:, g * (KC // HB) + c, :]
                                     ).then_inc(wraw_in, 16)
                    sp.wait_ge(xd_ready, g + 1)
                    sp.dma_start(b_scratch[g], xd[DR:DR + NS, :]).then_inc(b_stored, 16)
                    with sp.Fori(0, NS // NL) as i:
                        sp.wait_ge(b_stored, 16 * g + 16 + C_BST)
                        for s in range(2):
                            sp.wait_ge(gb_ready, NS * g + NL * i + 2 * s - 2 + C_GB)
                            sp.dma_start(BB[:, s], b_scratch[g, ds(NL * i + 2 * s, 2), :]
                                         .partition_broadcast(P)).then_inc(bb_in[s], 16)

            def attention_stage(half):
                scan_ended(sp, half)
                if half:
                    for c in range(KC):
                        sp.dma_start(wagain[c], watt_in[:, c, :]).then_inc(watt_in_s[c], 16)
                for dst, src in ((bqk[:], bqk_in), (bvb[:], bv_in.partition_broadcast(P)),
                                 (rope[:], rope_in), (perm[:], perm_in), (rtw[:], route_in)):
                    sp.dma_start(dst, src).then_inc(attc_in[half], 16)

            def expert_stage(half):
                K0 = NU * half
                sp.wait_ge(qk_mm, 8 * HB * (half + 1))
                sp.dma_start(wgr[:], wffn_in[0, :, 0:GW]).then_inc(wg_in, 16)
                attention_ended(sp, half)
                sp.dma_start(wdr[:], wffn_in[0, :, GW:GW + DW]).then_inc(wd_in, 16)

                def unit(k):
                    sp.wait_ge(wgl_s, KC * k + C1)
                    sp.dma_start(wgr[:], wffn_in[k - K0, :, 0:GW]).then_inc(wg_in, 16)
                    sp.wait_ge(wdl_s, NCH * k + C1)
                    sp.dma_start(wdr[:], wffn_in[k - K0, :, GW:GW + DW]).then_inc(wd_in, 16)

                if half:
                    with sp.Fori(K0 + 1, K0 + NU) as k:
                        unit(k)
                else:
                    sp.dma_start(ecT[:], ctx_in[1]).then_inc(ctx_in_s[1], 16)
                    for dst, src in ((ew_in[:], w_in_in), (exproj[:], xproj_in), (edtproj[:], dtproj_in)):
                        sp.dma_start(dst, src).then_inc(scanw_in[1], 16)
                    for g in range(HB, B):
                        for k in range(UQ * (g - HB), UQ * (g - HB) + UP):
                            if k:
                                unit(k)
                        sp.wait_ge(xd_ready, g + 1)
                        sp.dma_start(b_scratch[g], exd[DR:DR + NS, :]).then_inc(b_stored, 16)
                        sp.wait_ge(b_stored, 16 * g + 16 + C_BST)
                        with sp.Fori(0, UN) as i:
                            unit(i + (UQ * (g - HB) + UP))
                            for n in range(SU // T4):
                                sp.wait_ge(gb4, T4 * NS * (g - HB) + SU * i + T4 * (n - 2) + T4 + C_G4)
                                sp.dma_start(eBB[:, n % 2, :], b_scratch[g, ds(4 * i + n, 1), :]
                                             .partition_broadcast(P)).then_inc(bb_in[n % 2], 16)
                for a, b in ((0, T4), (T4, TH - 1), (TH - 1, TH)):
                    sp.wait_ge(d_acc, TH * (NU * (half + 1) - 1) + b + C_DA)
                    sp.dma_start(out[half][:, a:b, :], xs[:, half * TH + a:half * TH + b, :]).then_inc(stored, 16)

            scan_stage()
            for half in range(2):
                attention_stage(half)
                expert_stage(half)
            sp.wait_ge(stored, 2 * 3 * 16)

        @block.tensor
        def _(pe):
            pe.sem_inc(hT_ready, C_HT)
            pe.sem_inc(zT_ready, C_ZT)
            for s in (rot_mm, t_mm, pv_mm):
                pe.sem_inc(s, C2)
            for s in (gu_mm, d_mm):
                pe.sem_inc(s, C1)

            def split_product(out_, parts, rhs_parts, n, wait=lambda k: None):
                for k in range(n):
                    wait(k)
                    for j, (a, b) in enumerate(((0, 0), (0, 1), (1, 0))):
                        mm = nc.tensor.matmul(out_, parts[a](k), rhs_parts[b](k),
                                              start=(k == 0 and j == 0), stop=(k == n - 1 and j == 2))
                return mm

            def scan_stage():
                pe.wait_ge(ctx_in_s[0], 32)
                with pe.Fori(0, HB) as g:
                    for et in range(T4):
                        pe.wait_ge(x1_done, T4 * g + et + 1 - T4 + C_X1)
                        for k in range(DC // P):
                            mm = nc.tensor.matmul(Q[et], w_in[:, k, et * P:(et + 1) * P],
                                                  cT[:, ds(g, 1), k, :],
                                                  start=(k == 0), stop=(k == DC // P - 1))
                        mm.then_inc(xp_mm, 1)
                    pe.wait_ge(scanw_in[0], 48)
                    for et in range(T4):
                        pe.wait_ge(u_done, T4 * g + et + 1)
                        mm = nc.tensor.matmul(Q[0][0:DR + 2 * NS, :], xproj[:, et, :], U2[:, et, :],
                                              start=(et == 0), stop=(et == T4 - 1))
                    mm.then_inc(xd_mm, 1)
                    pe.wait_ge(xd_ready, g + 1)
                    n3 = DR + 2 * NS
                    for et in range(T4):
                        if et == 2:
                            pe.wait_ge(const_in, 96)
                            for tt in range(T4):
                                mm = nc.tensor.transpose(Q[1][:, tt * n3:(tt + 1) * n3],
                                                         xd[:, tt * P:(tt + 1) * P], ident[0:n3, 0:n3])
                            mm.then_inc(ct_mm, 1)
                        if et == 3:
                            pe.wait_ge(ct_ready, g + 1)
                        nc.tensor.matmul(Q[(et + 2) % T4], dtproj[:, et * P:(et + 1) * P], xd[0:DR, :],
                                         start=True, stop=True).then_inc(dt_mm, 1)
                    pe.wait_ge(ddiag_s, T4)
                    pe.wait_ge(dt_rel, T4 * g + T4)
                    pe.wait_ge(dt_abs, T4 * g + T4)
                    for tt in range(T4):
                        for et in range(T4):
                            mm = nc.tensor.matmul(Q[tt][:, et * P:(et + 1) * P],
                                                  U2[:, et, tt * P:(tt + 1) * P], ddiag[:, et, :],
                                                  start=True, stop=True)
                        mm.then_inc(yi_mm, 1)
                    pe.wait_ge(z_done, g + 1)
                    for tt in range(T4):
                        pe.wait_ge(yi_done, T4 * g + tt + 1)
                        for rt in range(T4):
                            mm = nc.tensor.transpose(Q[tt][:, rt * P:(rt + 1) * P],
                                                     ZS[:, rt, tt * P:(tt + 1) * P], ident[:])
                        mm.then_inc(zT_ready, 1)
                    with pe.Fori(0, NS // NL) as i:
                        for n in range(NL):
                            step = NS * g + NL * i + n
                            pe.wait_ge(scan_done, T4 * step + T4 + C_SC)
                            for tt in range(T4):
                                pe.wait_ge(y_acc, T4 * step + tt - 1 + C_YA)
                                for et in range(T4):
                                    mm = nc.tensor.transpose(HT[tt % 2][:, et * P:(et + 1) * P],
                                                             HS[:, n % 2, et, tt * P:(tt + 1) * P], ident[:])
                                mm.then_inc(hT_ready, 1)

            def attention_stage(half):
                scan_ended(pe, half)
                pe.wait_ge(consts, 7)

                def turn_rows(g, tt):
                    pe.wait_ge(ex_done, 32 * g + C2)
                    pe.wait_ge(a_hp, T4 * g + tt + 1)
                    for k in range(KC):
                        mm = nc.tensor.transpose(bank[k][:, tt * P:(tt + 1) * P],
                                                 hp[:, tt, k * P:(k + 1) * P], ident[:])
                    if tt == T4 - 1:
                        mm.then_inc(h1_mm, 1)

                for tt in range(T4):
                    turn_rows(HB * half, tt)
                pe.wait_ge(attc_in[half], 80)
                pe.wait_ge(rt_split, 2 * (half + 1))
                if half:
                    pe.wait_ge(wal2[0], 2)
                    pe.wait_ge(wal2[1], 2)
                for g in range(HB * half, HB * half + HB):
                    U0 = 32 * g
                    pe.wait_ge(h1_hi, KC * g + KC)
                    pe.wait_ge(h1_lo, KC * g + KC)
                    for tt in range(T4):
                        split_product(bank[tt],
                                      [lambda k, w=w: w[:, k, tt * P:(tt + 1) * P] for w in (h1h, h1l)],
                                      [lambda k, w=w: w[:, k, 2 * H:3 * H] for w in (wah, wal)], KC
                                      ).then_inc(v_mm, 1)

                    def product(m):
                        pe.wait_ge(qb_ready, 8 * g + m - 1 + C2)
                        split_product(bank[4 + m % 2],
                                      [lambda k, w=w: w[:, k, m * P:(m + 1) * P] for w in (wah, wal)],
                                      [lambda k, w=w: w[:, k, :] for w in (h1h, h1l)], KC).then_inc(qk_mm, 1)

                    def rotate(m):
                        pe.wait_ge(qb_ready, 8 * g + m + 1 + C2)
                        pe.wait_ge(rope_s, 8 * g + m - 1 + C2)
                        nc.tensor.matmul(bank[6 + m % 2], perm[:], QB[:, m % 2, :], start=True,
                                         stop=True).then_inc(rot_mm, 1)

                    pe.wait_ge(lg_done, T4 * g + C1)
                    for m in range(8):
                        product(m)
                        if m:
                            rotate(m - 1)
                    rotate(7)

                    def scores(u, a):
                        i, hpair = divmod(u, NH // 2)
                        W = P * (i + 1)
                        if u == 0:
                            pe.wait_ge(v_done, T4 * g + T4)
                            pe.wait_ge(qk_done, 8 * g + 8 + C2)
                        if a == 0:
                            pe.wait_ge(ex_done, U0 + u - 1 + C2)
                        h = 2 * hpair + a
                        r, m = HD * (h % 4), h // 4
                        nc.tensor.matmul(SB[u % 2][:, a, 0:W], QK[r:r + HD, m, i * P:(i + 1) * P],
                                         QK[r:r + HD, 4 + m, 0:W], start=True, stop=False)
                        mm = nc.tensor.matmul(SB[u % 2][:, a, W - P:W], identb[:], maskb[:],
                                              start=False, stop=True)
                        if a:
                            mm.then_inc(s_mm, 1)

                    def turn(u):
                        i = u // (NH // 2)
                        pe.wait_ge(p_done, U0 + u + 1)
                        pe.wait_ge(pt_a, U0 + u + C1)
                        pe.wait_ge(pt_b, U0 + u + C1)
                        for a in range(2):
                            for kb in range(i + 1):
                                mm = nc.tensor.transpose(PB[:, a, kb * P:(kb + 1) * P],
                                                         EX[:, u % 2, a, kb * P:(kb + 1) * P], ident[:])
                        mm.then_inc(t_mm, 1)

                    def weigh(u, a):
                        i, hpair = divmod(u, NH // 2)
                        pe.wait_ge((pt_a, pt_b)[a], U0 + u + 1 + C1)
                        if hpair == 0 and a == 0 and g + i:
                            pe.wait_ge(cth_done, T4 * g + i)
                            pe.wait_ge(ctl_done, T4 * g + i)
                        h = 2 * hpair + a
                        r, m = HD * (h % 4), h // 4
                        for kb in range(i + 1):
                            mm = nc.tensor.matmul(CX[r:r + HD, m * P:(m + 1) * P],
                                                  V[:, kb, h * HD:(h + 1) * HD],
                                                  PT[:, u % 2, a, kb * P:(kb + 1) * P],
                                                  start=(kb == 0), stop=(kb == i))
                        if a:
                            mm.then_inc(pv_mm, 1)

                    def finish(i, step):
                        t = T4 * g + i
                        if step == 0:
                            pe.wait_ge(lg_done, t + C1)
                            pe.wait_ge(cth_done, t + 1)
                            pe.wait_ge(ctl_done, t + 1)
                            split_product(WK, [lambda k, w=w: w[:, k, :] for w in (cth, ctl)],
                                          [lambda k, w=w: w[:, k, 3 * H:4 * H] for w in (wah, wal)], KC
                                          ).then_inc(wo_mm, 1)
                        if step == 1:
                            pe.wait_ge(hp2_done, t + 1)
                            for k in range(KC):
                                mm = nc.tensor.transpose(WK[:, k * P:(k + 1) * P],
                                                         hp[:, i, k * P:(k + 1) * P], ident[:])
                            mm.then_inc(h2_mm, 1)
                        if step == 2:
                            pe.wait_ge(h2h_kept, t + 1)
                            pe.wait_ge(h2l_kept, t + 1)
                            at = (g % HB) * L + i * P
                            split_product(WK[:, 0:ROUTE],
                                          [lambda k, w=w: w[:, k, at:at + P] for w in (h2h, h2l)],
                                          [lambda k, w=w: w[:, k, :] for w in (rth, rtl)], KC
                                          ).then_inc(rt_mm, 1)

                    for u in range(2):
                        for a in range(2):
                            scores(u, a)
                    for u in range(32):
                        turn(u)
                        for a in range(2):
                            if u + 2 < 32:
                                scores(u + 2, a)
                            if a:
                                weigh(u, 0)
                                weigh(u, 1)
                        if u >= 8 and u % 8 in (0, 3, 5):
                            finish(u // 8 - 1, (u % 8 + 1) // 2 - (u % 8 > 0))
                    more = g % HB < HB - 1
                    finish(3, 0)
                    for tt in range(T4 - 1):
                        more and turn_rows(g + 1, tt)
                    finish(3, 1)
                    more and turn_rows(g + 1, T4 - 1)
                    finish(3, 2)

            def expert_stage(half):
                attention_ended(pe, half)

                def unit(k, place=lambda j: None, more=True):
                    def weights(j):
                        pe.wait_ge(wgh_s, KC * k + j + 1)
                        pe.wait_ge(wgl_s, KC * k + j + 1 + C1)

                    S0, n = first_chunk(half, k), NCH if more else SHORT
                    for s, (grp, c, places) in enumerate(chunks(not more)):
                        pe.wait_ge(f_a, S0 + s - 1 + C2)
                        for up, bk in ((0, FG), (1, FU)):
                            o = up * EW + c * P
                            mm = split_product(bk[s % 2],
                                               [lambda j, w=w: w[:, j, o:o + P] for w in (wgh, wgl)],
                                               [lambda j, w=w: w[:, j, grp * L:(grp + 1) * L] for w in (h2h, h2l)], KC,
                                               *([] if s or up else [weights]))
                            if up:
                                mm.then_inc(gu_mm, 1)
                            for j in places[1:] if up else places[:1]:
                                place(j)
                    pe.wait_ge(wdh_s, NCH * k + NCH)
                    pe.wait_ge(wdl_s, NCH * k + NCH + C1)
                    for tt in range(TH):
                        if tt % T4 == 0:
                            pe.wait_ge(f_ah, S0 + n * (tt // T4 + 1) + C2)
                            pe.wait_ge(f_al, S0 + n * (tt // T4 + 1) + C2)
                        pe.wait_ge(d_acc, TH * k + tt - 1 + C_DA)
                        split_product(FD[tt % 2],
                                      [lambda c, w=w: w[:, c, tt * P:(tt + 1) * P] for w in (fah, fal)],
                                      [lambda c, w=w: w[:, c, :] for w in (wdh, wdl)], n
                                      ).then_inc(d_mm, 1)
                        if tt % 2 == 0:
                            place(2 * NG * NCH + tt // 2)

                def before(g, j):
                    if j in (0, 2, 4, 6):
                        et = j // 2
                        if et == 0:
                            pe.wait_ge(x1_done, T4 * g + C_X1)
                        if et >= 2:
                            pe.wait_ge(cv_tap, 12 * g + 3 * (et - 2) + 3)
                        for k in range(DC // P):
                            mm = nc.tensor.matmul(EB[et % 2], ew_in[:, k, et * P:(et + 1) * P],
                                                  ecT[:, g - HB, k, :], start=(k == 0), stop=(k == DC // P - 1))
                        mm.then_inc(xp_mm, 1)
                    if j == 12:
                        pe.wait_ge(u_d4, T4 * (g - HB) + T4)
                        for et in range(T4):
                            mm = nc.tensor.matmul(EB[0][0:DR + 2 * NS, :], exproj[:, et, :], eDU[:, et, :],
                                                  start=(et == 0), stop=(et == T4 - 1))
                        mm.then_inc(xd_mm, 1)
                    if j == 13:
                        wait_apart(pe, xd_ready, g + 1)
                        n3 = DR + 2 * NS
                        for tt in range(T4):
                            mm = nc.tensor.transpose(EB[1][:, tt * n3:(tt + 1) * n3],
                                                     exd[:, tt * P:(tt + 1) * P], ident[0:n3, 0:n3])
                        mm.then_inc(ct_mm, 1)
                    if j in (15, 17, 19, 21):
                        et = (j - 15) // 2
                        if et == 1:
                            pe.wait_ge(ct_ready, g + 1)
                        if et >= 2:
                            pe.wait_ge(dt_abs, T4 * g + et - 1)
                            pe.wait_ge(dt_rel, T4 * g + et - 1)
                        nc.tensor.matmul(EB[et % 2], edtproj[:, et * P:(et + 1) * P], exd[0:DR, :],
                                         start=True, stop=True).then_inc(dt_mm, 1)
                    if j in (26, 27, 28, 29):
                        tt = j - 26
                        if tt == 0:
                            pe.wait_ge(dt_abs, T4 * g + T4)
                            pe.wait_ge(dt_rel, T4 * g + T4)
                        if tt >= 2:
                            pe.wait_ge(yi_done, T4 * g + tt - 1)
                        for et in range(T4):
                            mm = nc.tensor.matmul(EB[tt % 2][:, et * P:(et + 1) * P],
                                                  eDU[:, et, tt * P:(tt + 1) * P], eddiag[:, et, :],
                                                  start=True, stop=True)
                        mm.then_inc(yi_mm, 1)

                def step(g, i, j):
                    q = nth(g, i, j)
                    pe.wait_ge(scan_done, q + 1 + C_SC)
                    pe.wait_ge(y4, q - T4 * NS * HB + C4)
                    for tt in range(T4):
                        mm = nc.tensor.transpose(EB[1][:, tt * P:(tt + 1) * P],
                                                 eHS[:, j % 2, tt * P:(tt + 1) * P], ident[:])
                    mm.then_inc(hT_ready, 1)

                def after(g):
                    for tt in range(T4):
                        if tt == 0:
                            pe.wait_ge(scan_done, T4 * NS * (g + 1) + C_SC)
                            pe.wait_ge(y4, T4 * NS * (g + 1 - HB) + C4)
                        if tt >= 2:
                            pe.wait_ge(y_z, T4 * g + tt - 1)
                        for rt in range(T4):
                            mm = nc.tensor.transpose(EB[tt % 2][:, rt * P:(rt + 1) * P],
                                                     eZS[:, rt, tt * P:(tt + 1) * P], ident[:])
                        mm.then_inc(zT_ready, 1)

                if half:
                    with pe.Fori(NU, 2 * NU - 1) as k:
                        unit(k)
                    unit(2 * NU - 1, more=False)
                else:
                    pe.wait_ge(ctx_in_s[1], 16)
                    pe.wait_ge(scanw_in[1], 48)
                    pe.wait_ge(ddiag_s, 2 * T4)
                    beside(unit, before, step, after)(pe)

            scan_stage()
            for half in range(2):
                attention_stage(half)
                expert_stage(half)

        @block.scalar
        def _(act):
            for s in (qb_ready, ex_done, f_ah):
                act.sem_inc(s, C2)
            act.sem_inc(pt_a, C1)

            def make_consts():
                act.wait_ge(const_in, 96)
                nc.scalar.activation(identb[:], ident[:], ACT.Copy).then_inc(consts, 1)
                nc.scalar.activation(maskb[:], mask[:], ACT.Copy).then_inc(consts, 1)
                nc.scalar.activation(tg[:, 0:2], gates[:], ACT.Tanh).then_inc(consts, 1)
                nc.scalar.activation(aneg[:], chan[:, :, TAPS + 3:], ACT.Exp).then_inc(consts, 1)
                act.wait_ge(consts, 4)
                nc.scalar.activation(aneg[:], aneg[:], ACT.Copy, scale=-1.0).then_inc(consts, 1)
                nc.scalar.activation(tg[:, 2:4], tg[:, 0:2], ACT.Copy, scale=0.5).then_inc(consts, 1)
                nc.scalar.activation(tgq[:], tg[:, 1:2], ACT.Copy, scale=0.25).then_inc(consts, 1)
                act.wait_ge(consts, 7)

            def scan_stage():
                with act.Fori(0, HB) as g:
                    def round_weights(c):
                        act.wait_ge(wraw_in, 16 * ((KC // HB) * g + c + 1))
                        nc.scalar.activation(wah[:, ds(g * (KC // HB) + c, 1), :], wraw[:],
                                             ACT.Copy).then_inc(wah_done, 1)

                    for et in range(T4):
                        act.wait_ge(xp_mm, T4 * g + et + 1)
                        nc.scalar.activation(T1[:, et, :], Q[et], ACT.Identity,
                                             bias=chan[:, et, TAPS:TAPS + 1],
                                             scale=chan[:, et, TAPS - 1:TAPS]).then_inc(cv_init, 1)
                    for et in range(T4):
                        act.wait_ge(cv_tap, 12 * g + 3 * et + 3)
                        nc.scalar.activation(T2[:, et, :], T1[:, et, :], ACT.Tanh, scale=0.5).then_inc(u_t, 1)
                    round_weights(0)
                    act.wait_ge(xd_mm, g + 1)
                    act.wait_ge(b_stored, 16 * g + C_BST)
                    nc.scalar.activation(xd[:], Q[0][0:DR + 2 * NS, :], ACT.Copy, scale=0.5).then_inc(xd_ready, 1)
                    n3 = DR + 2 * NS
                    for et in range(T4):
                        if et == 2:
                            act.wait_ge(ct_mm, g + 1)
                            nc.scalar.activation(Ct[:], Q[1][:, 0:T4 * n3].rearrange("p (t n) -> p t n", n=n3)
                                                 [:, :, DR + NS:n3], ACT.Copy).then_inc(ct_ready, 1)
                        act.wait_ge(dt_mm, T4 * g + et + 1)
                        nc.scalar.activation(T1[:, et, :], Q[(et + 2) % T4], ACT.Abs,
                                             bias=chan[:, et, TAPS + 1:TAPS + 2]).then_inc(dt_abs, 1)
                        if et == 0:
                            act.wait_ge(z_norm, 4 * g + 4)
                            act.wait_ge(zT_ready, T4 * g + C_ZT)
                        for rt in {0: (0, 1), 1: (2, 3)}.get(et, ()):
                            nc.scalar.activation(ZS[:, rt, :], xs[:, ds(T4 * g + rt, 1), :], ACT.Identity,
                                                 bias=zst[:, 3, rt:rt + 1], scale=zst[:, 1, rt:rt + 1]
                                                 ).then_inc(z_n, 1)
                        if et == 2:
                            act.wait_ge(z_n, T4 * g + T4)
                            act.wait_ge(u_done, T4 * g + T4)
                            nc.scalar.activation(T2, ZS[:], ACT.Tanh, scale=0.5).then_inc(z_t, 1)
                    act.wait_ge(dt_abs, T4 * g + T4)
                    nc.scalar.activation(T1, T1, ACT.Exp, scale=-1.0).then_inc(dt_e, 1)
                    round_weights(1)
                    act.wait_ge(dt_e, g + 1)
                    for et in range(T4):
                        nc.scalar.activation(T1[:, et, :], T1[:, et, :], ACT.Ln, bias=1.0).then_inc(dt_l4, 1)
                    act.wait_ge(dl4, T4 * g + T4)
                    with act.Fori(0, NS // NL) as i:
                        for n in range(NL):
                            step = NS * g + NL * i + n
                            for et in range(T4):
                                act.wait_ge(scan_done, T4 * step + et - 1 + C_SC)
                                nc.scalar.activation(DA[et % 2], DL[:, et, :], ACT.Exp,
                                                     scale=aneg[:, et, ds(NL * i + n, 1)]).then_inc(dA_ready, 1)

            def attention_stage(half):
                scan_ended(act, half)

                def norm_rows(g, tt):
                    act.wait_ge(a_norm, 8 * g + 8)
                    if g % HB:
                        act.wait_ge(xacc_done, T4 * (g - 1) + tt + 1)
                        act.wait_ge(h2_mm, T4 * (g - 1) + tt + 1)
                    nc.scalar.activation(XL[:, tt, :], xs[:, T4 * g + tt, :], ACT.Identity,
                                         bias=ast[:, 2, tt:tt + 1], scale=ast[:, 1, tt:tt + 1]
                                         ).then_inc(a_xl, 1)
                    act.wait_ge(a_xl, T4 * g + tt + 1)
                    nc.scalar.activation(hp[:, tt, :], XL[:, tt, :], ACT.Copy,
                                         scale=ast[:, 6, tt:tt + 1]).then_inc(a_hp, 1)

                for tt in range(T4):
                    norm_rows(HB * half, tt)
                if half:
                    for c in (0, 2):
                        act.wait_ge(watt_in_s[c], 16)
                        nc.scalar.activation(wah[:, c, :], wagain[c], ACT.Copy).then_inc(wah2[0], 1)
                act.wait_ge(attc_in[half], 80)
                nc.scalar.activation(rth[:], rtw[:], ACT.Copy).then_inc(rt_split, 1)
                for g in range(HB * half, HB * half + HB):
                    U0 = 32 * g
                    more = g % HB < HB - 1
                    act.wait_ge(h1_mm, g + 1)
                    for k in range(KC):
                        nc.scalar.activation(h1h[:, k, :], bank[k], ACT.Copy, scale=wln[:, 0, k:k + 1]
                                             ).then_inc(h1_hi, 1)
                    for m in range(8):
                        act.wait_ge(qk_mm, 8 * g + m + 1)
                        act.wait_ge(rot_mm, 8 * g + m - 1 + C2)
                        act.wait_ge(rope_c, 8 * g + m - 1 + C2)
                        nc.scalar.activation(QB[:, m % 2, :], bank[4 + m % 2], ACT.Identity,
                                             bias=bqk[:, m:m + 1]).then_inc(qb_ready, 1)

                    def probs(u):
                        i, hpair = divmod(u, NH // 2)
                        W = P * (i + 1)
                        act.wait_ge(mx_done, U0 + u + 1)
                        act.wait_ge(t_mm, U0 + u - 1 + C2)
                        for a in range(2):
                            ins = nc.scalar.activation(EX[:, u % 2, a, 0:W], SB[u % 2][:, a, 0:W], ACT.Exp,
                                                       bias=nm[:, u % 2, a:a + 1],
                                                       accum_out=rs[:, u % 2, a:a + 1])
                        ins.then_inc(ex_done, 1)

                    def copy_even(u):
                        W = P * (u // (NH // 2) + 1)
                        act.wait_ge(t_mm, U0 + u + 1 + C2)
                        act.wait_ge(pv_mm, U0 + u - 1 + C2)
                        nc.scalar.activation(PT[:, u % 2, 0, 0:W], PB[:, 0, 0:W], ACT.Copy).then_inc(pt_a, 1)

                    def finish(i, step):
                        t = T4 * g + i
                        if step == 0:
                            act.wait_ge(pv_mm, U0 + 8 * i + 8 + C2)
                            nc.scalar.activation(cth[:], CX.rearrange("p (k t) -> p k t", k=KC), ACT.Copy
                                                 ).then_inc(cth_done, 1)
                        if step == 1:
                            act.wait_ge(xm_done, t + 1)
                            nc.scalar.activation(sq[:], XL[:, i, :], ACT.Square, accum_out=ss[:, i:i + 1]
                                                 ).then_inc(sq_done, 1)
                        if step == 2:
                            act.wait_ge(r2_s, 3 * t + 3)
                            nc.scalar.activation(hp[:, i, :], XL[:, i, :], ACT.Copy,
                                                 scale=r2[:, 1, i:i + 1]).then_inc(hp2_done, 1)
                        if step == 3:
                            act.wait_ge(hw_done, t + 1)
                            at = (g % HB) * L + i * P
                            nc.scalar.activation(h2h[:, :, at:at + P], hw[:], ACT.Copy
                                                 ).then_inc(h2h_kept, 1)

                    probs(0)
                    for u in range(32):
                        if u >= 8 and u % 8 == 0:
                            finish(u // 8 - 1, 0)
                        if u + 1 < 32:
                            probs(u + 1)
                        copy_even(u)
                        if u >= 8 and u % 8 in (2, 3, 5):
                            finish(u // 8 - 1, (2, 3, 5).index(u % 8) + 1)
                        if u in (27, 29, 31) and more:
                            norm_rows(g + 1, (u - 27) // 2)
                    for step in range(3):
                        finish(3, step)
                    more and norm_rows(g + 1, T4 - 1)
                    finish(3, 3)

            def expert_stage(half):
                attention_ended(act, half)
                act.wait_ge(gt, GT * half + 2)
                nc.scalar.activation(pr[:, 1], pr[:, 0], ACT.Exp).then_inc(gt_e, 1)
                nc.scalar.activation(gs[:, 3, :], lg[:, :, NE], ACT.Tanh, scale=0.5).then_inc(gt_t, 1)

                def split(k, c):
                    if c == 0:
                        act.wait_ge(wg_in, 16 * k + 16)
                        act.wait_ge(gu_mm, first_chunk(half, k) + C1)
                    nc.scalar.activation(wgh[:, c, :], wgr[:, c * 2 * EW:(c + 1) * 2 * EW], ACT.Copy
                                         ).then_inc(wgh_s, 1)

                def unit(k, place=lambda j: None, more=True):
                    S0 = first_chunk(half, k)

                    def tanh(s):
                        act.wait_ge(gu_mm, S0 + s + 1 + C1)
                        act.wait_ge(f_a, S0 + s - 1 + C2)
                        nc.scalar.activation(ft[:, s % 2, :], FG[s % 2], ACT.Tanh, scale=0.5).then_inc(f_t, 1)

                    def round_act(s, grp, c):
                        act.wait_ge(f_a, S0 + s + 1 + C2)
                        nc.scalar.activation(fah[:, c, grp * L:(grp + 1) * L], fa[:, s % 2, :],
                                             ACT.Copy).then_inc(f_ah, 1)

                    done = None
                    for s, at in enumerate(chunks(not more) + [(0, 0, [2 * NG * NCH])]):
                        place(at[2][0])
                        if s:
                            tanh(s - 1)
                        for j in at[2][1:]:
                            place(j)
                        if s:
                            round_act(s - 1, *done)
                        done = at[:2]
                        if 1 <= s <= NCH:
                            c = s - 1
                            if c == 0:
                                act.wait_ge(wd_in, 16 * k + 16)
                                act.wait_ge(d_mm, TH * k + C1)
                            nc.scalar.activation(wdh[:, c, :], wdr[:, c * H:(c + 1) * H], ACT.Copy
                                                 ).then_inc(wdh_s, 1)
                    for c in range(KC):
                        if more:
                            split(k + 1, c)
                        if c < KC - 1:
                            place(2 * NG * NCH + 1 + c)

                def before(g, j):
                    if j in (2, 4, 6, 8):
                        et = j // 2 - 1
                        act.wait_ge(xp_mm, T4 * g + et + 1)
                        nc.scalar.activation(eDL[:, et, :], EB[et % 2], ACT.Identity,
                                             bias=chan[:, et, TAPS:TAPS + 1],
                                             scale=chan[:, et, TAPS - 1:TAPS]).then_inc(cv_init, 1)
                    if j in (4, 6, 8, 10):
                        et = j // 2 - 2
                        act.wait_ge(cv_tap, 12 * g + 3 * et + 3)
                        nc.scalar.activation(eYA[:, et, :], eDL[:, et, :], ACT.Tanh, scale=0.5).then_inc(u_t4, 1)
                    if j in (7, 9):
                        act.wait_ge(z_norm, 4 * g + 4)
                        for rt in (j - 7, j - 6):
                            nc.scalar.activation(eZS[:, rt, :], xs[:, T4 * g + rt, :], ACT.Identity,
                                                 bias=ezst[:, 3, rt:rt + 1], scale=ezst[:, 1, rt:rt + 1]
                                                 ).then_inc(z_n, 1)
                    if j in (12, 14):
                        act.wait_ge(z_n, T4 * g + T4)
                        act.wait_ge(u_d4, T4 * (g - HB) + T4)
                        nc.scalar.activation(eYA[:, j - 12:j - 10, :], eZS[:, j - 12:j - 10, :], ACT.Tanh,
                                             scale=0.5).then_inc(z_t4, 1)
                    if j == 13:
                        act.wait_ge(xd_mm, g + 1)
                        act.wait_ge(b_stored, 16 * g + C_BST)
                        nc.scalar.activation(exd[:], EB[0][0:DR + 2 * NS, :], ACT.Copy, scale=0.5
                                             ).then_inc(xd_ready, 1)
                    if j == 15:
                        act.wait_ge(ct_mm, g + 1)
                        n3 = DR + 2 * NS
                        nc.scalar.activation(eCt[:], EB[1][:, 0:T4 * n3].rearrange("p (t n) -> p t n", n=n3)
                                             [:, :, DR + NS:n3], ACT.Copy).then_inc(ct_ready, 1)
                    if j in (17, 19, 21, 23):
                        et = (j - 17) // 2
                        act.wait_ge(dt_mm, T4 * g + et + 1)
                        act.wait_ge(z_d4, 2 * (g - HB) + 2)
                        nc.scalar.activation(eYA[:, et, :], EB[et % 2], ACT.Abs,
                                             bias=chan[:, et, TAPS + 1:TAPS + 2]).then_inc(dt_abs, 1)
                    if j == 24:
                        act.wait_ge(dt_abs, T4 * g + T4)
                        nc.scalar.activation(eYA[:], eYA[:], ACT.Exp, scale=-1.0).then_inc(dt_e, 1)
                    if j == 25:
                        act.wait_ge(dt_e, g + 1)
                        nc.scalar.activation(eYA[:], eYA[:], ACT.Ln, bias=1.0).then_inc(dt_l, 1)

                def first(g):
                    act.wait_ge(dl_done, g + 1 - HB)
                    act.wait_ge(yi_done, T4 * g + T4)

                def step(g, i, j):
                    q = nth(g, i, j)
                    act.wait_ge(scan_done, q + C_SC)
                    nc.scalar.activation(EB[0], eDL[:, j % T4, :], ACT.Exp,
                                         scale=aneg[:, j % T4, column(i, j)]).then_inc(dA_ready, 1)

                for c in range(KC):
                    split(NU * half, c)
                if half:
                    with act.Fori(NU, 2 * NU - 1) as k:
                        unit(k)
                    unit(2 * NU - 1, more=False)
                else:
                    beside(unit, before, step, lambda g: None)(act, first)

            make_consts()
            scan_stage()
            for half in range(2):
                attention_stage(half)
                expert_stage(half)


        @block.vector
        def _(dve):
            dve.sem_inc(x1_done, C_X1)
            dve.sem_inc(scan_done, C_SC)
            dve.sem_inc(y_acc, C_YA)
            dve.sem_inc(d_acc, C_DA)
            for s in (rope_s, qk_done, f_p, f_a):
                dve.sem_inc(s, C2)
            dve.sem_inc(y4, C4)
            for s in (pt_b, lg_done, att_done):
                dve.sem_inc(s, C1)

            def stats(rows, six, two, s_six, s_two, g):
                for t in range(T4):
                    nc.vector.bn_stats(six[:, t, :], rows[:, ds(T4 * g + t, 1), :]).then_inc(s_six, 1)
                dve.wait_ge(s_six, (T4 + 1) * g + T4)
                nc.vector.memset(tick[:], 0.0).then_inc(s_six, 1)
                for t in range(T4):
                    nc.vector.bn_aggr(two[:, t, :], six[:, t, :]).then_inc(s_two, 1)

            def scan_stage():
                dve.wait_ge(const_in, 96)
                dve.wait_ge(consts, 7)
                for et in range(T4):
                    nc.vector.tensor_scalar(ddiag[:, et, :], ident[:], chan[:, et, TAPS + 2:TAPS + 3], 0.5,
                                            ALU.mult, ALU.mult).then_inc(ddiag_s, 1)
                with dve.Fori(0, HB) as g:
                    def silu_u(et):
                        dve.wait_ge(u_t, T4 * g + et + 1)
                        nc.vector.scalar_tensor_tensor(U2[:, et, :], T2[:, et, :], 1.0, T1[:, et, :],
                                                       ALU.add, ALU.mult).then_inc(u_done, 1)

                    for et in range(T4):
                        dve.wait_ge(cv_init, T4 * g + et + 1)
                        for sh in range(1, TAPS):
                            if sh > 1:
                                dve.wait_ge(cv_tap, 12 * g + 3 * et + sh - 1)
                            tap = TAPS - 1 - sh
                            nc.vector.scalar_tensor_tensor(T1[:, et, sh:L], Q[et][:, 0:L - sh],
                                                           chan[:, et, tap:tap + 1], T1[:, et, sh:L],
                                                           ALU.mult, ALU.add).then_inc(cv_tap, 1)
                        if et:
                            silu_u(et - 1)
                    silu_u(T4 - 1)
                    dve.wait_ge(x_in_s[0], 16)
                    stats(xs, bn6, mv, z_bn, z_mv, g)
                    for et in range(T4):
                        dve.wait_ge(dt_abs, T4 * g + et + 1)
                        nc.vector.tensor_scalar(DL[:, et, :], Q[(et + 2) % T4], chan[:, et, TAPS + 1:TAPS + 2],
                                                0.0, ALU.add, ALU.max).then_inc(dt_rel, 1)
                    dve.wait_ge(z_t, g + 1)
                    nc.vector.scalar_tensor_tensor(ZS[:], T2, 1.0, ZS[:], ALU.add, ALU.mult).then_inc(z_done, 1)
                    for tt in range(T4):
                        dve.wait_ge(yi_mm, T4 * g + tt + 1)
                        nc.vector.tensor_copy(YA[:, tt, :], Q[tt]).then_inc(yi_done, 1)
                    for et in range(T4):
                        dve.wait_ge(dt_l4, T4 * g + et + 1)
                        nc.vector.tensor_tensor(DL[:, et, :], DL[:, et, :], T1[:, et, :], ALU.add).then_inc(dl4, 1)
                    for et in range(T4):
                        dve.wait_ge(dl4, T4 * g + et + 1)
                        nc.vector.scalar_tensor_tensor(DU[:, et, :], U2[:, et, :], 0.5, DL[:, et, :],
                                                       ALU.mult, ALU.mult).then_inc(du4, 1)
                    wait_apart(dve, yi_done, T4 * g + T4)

                    def scans(i, n, pair):
                        step = NS * g + NL * i + n
                        if pair == 0:
                            dve.wait_ge(hT_ready, T4 * step - T4 + C_HT)
                        for et in (2 * pair, 2 * pair + 1):
                            if n % NL == 0 and et < T4 - 1:
                                dve.wait_ge(gb_part, (T4 - 1) * (NS // NL * g + i + n // NL) + et + 1)
                            else:
                                dve.wait_ge(gb_ready, step + 1 + C_GB)
                            dve.wait_ge(dA_ready, T4 * step + et + 1)
                            nc.vector.tensor_tensor_scan(HS[:, n % 2, et, :], DA[et % 2], GB[:, n % 2, et, :],
                                                         0.0, ALU.mult, ALU.add).then_inc(scan_done, 1)

                    def sums(i, n, pair):
                        step = NS * g + NL * i + n
                        for tt in (2 * pair, 2 * pair + 1):
                            dve.wait_ge(hT_ready, T4 * step + tt + 1 + C_HT)
                            dve.wait_ge(y_acc, T4 * step + tt - T4 + 1 + C_YA)
                            nc.vector.scalar_tensor_tensor(YA[:, tt, :], HT[tt % 2],
                                                           Ct[:, tt, ds(NL * i + n, 1)], YA[:, tt, :],
                                                           ALU.mult, ALU.add).then_inc(y_acc, 1)

                    scans(0, 0, 0)
                    scans(0, 0, 1)
                    with dve.Fori(0, NS // NL - 1) as i:
                        for n in range(NL):
                            for pair in range(2):
                                scans(i, n + 1, pair)
                                sums(i, n, pair)
                    for n in range(NL):
                        for pair in range(2):
                            if n < NL - 1:
                                scans(NS // NL - 1, n + 1, pair)
                            sums(NS // NL - 1, n, pair)
                    for tt in range(T4):
                        dve.wait_ge(y_acc, T4 * NS * g + T4 * (NS - 1) + tt + 1 + C_YA)
                        dve.wait_ge(zT_ready, T4 * g + tt + 1 + C_ZT)
                        nc.vector.tensor_tensor(YA[:, tt, :], Q[tt], YA[:, tt, :], ALU.mult).then_inc(y_z, 1)
                    for tt in range(T4):
                        dve.wait_ge(y_z, T4 * g + tt + 1)
                        nc.vector.scalar_tensor_tensor(xs[:, ds(T4 * g + tt, 1), :], YA[:, tt, :], tg[:, 2:3],
                                                       xs[:, ds(T4 * g + tt, 1), :], ALU.mult, ALU.add
                                                       ).then_inc(x1_done, 1)

            def attention_stage(half):
                scan_ended(dve, half)
                if not half:
                    stats(xs, abn, amv, a_bn, a_mv, 0)
                if half:
                    for c in (1, 3):
                        dve.wait_ge(watt_in_s[c], 16)
                        nc.vector.tensor_copy(wah[:, c, :], wagain[c]).then_inc(wah2[1], 1)
                        dve.wait_ge(wah2[1], c // 2 + 1)
                        nc.vector.tensor_tensor(wal[:, c, :], wagain[c], wah[:, c, :].bitcast(f32),
                                                ALU.subtract).then_inc(wal2[1], 1)
                dve.wait_ge(attc_in[half], 80)
                dve.wait_ge(rt_split, 2 * half + 1)
                nc.vector.tensor_tensor(rtl[:], rtw[:], rth[:].bitcast(f32), ALU.subtract).then_inc(rt_split, 1)

                def h1_rest(g):
                    for k in range(KC):
                        dve.wait_ge(h1_hi, KC * g + k + 1)
                        nc.vector.scalar_tensor_tensor(h1l[:, k, :], bank[k], wln[:, 0, k:k + 1],
                                                       h1h[:, k, :].bitcast(f32), ALU.mult, ALU.subtract
                                                       ).then_inc(h1_lo, 1)

                h1_rest(HB * half)
                for g in range(HB * half, HB * half + HB):
                    U0 = 32 * g
                    for tt in range(T4):
                        dve.wait_ge(v_mm, T4 * g + tt + 1)
                        nc.vector.tensor_tensor(V[:, tt, :], bank[tt], bvb[:], ALU.add).then_inc(v_done, 1)
                    for m in range(8):
                        dve.wait_ge(rot_mm, 8 * g + m + 1 + C2)
                        dve.wait_ge(qk_done, 8 * g + m - 1 + C2)
                        f = SCALE if m < T4 else 1.0
                        nc.vector.scalar_tensor_tensor(RS[:, m % 2, :], bank[6 + m % 2], f, rope[:, 1, :],
                                                       ALU.mult, ALU.mult).then_inc(rope_s, 1)
                        dve.wait_ge(rope_s, 8 * g + m + 1 + C2)
                        dve.wait_ge(rope_c, 8 * g + m + 1 + C2)
                        nc.vector.scalar_tensor_tensor(QK[:, m, :], RC[:, m % 2, :], f, RS[:, m % 2, :],
                                                       ALU.mult, ALU.add).then_inc(qk_done, 1)

                    def row_max(u):
                        W = P * (u // (NH // 2) + 1)
                        dve.wait_ge(s_mm, U0 + u + 1)
                        nc.vector.tensor_reduce(nm[:, u % 2, :], SB[u % 2][:, :, 0:W], AX.X, ALU.max, negate=True
                                                ).then_inc(mx_done, 1)

                    def norm_probs(u):
                        W = P * (u // (NH // 2) + 1)
                        dve.wait_ge(ex_done, U0 + u + 1 + C2)
                        nc.vector.reciprocal(ri[:, u % 2, :], rs[:, u % 2, :]).then_inc(ri_done, 1)
                        dve.wait_ge(ri_done, U0 + u + 1)
                        for a in range(2):
                            ins = nc.vector.tensor_scalar(EX[:, u % 2, a, 0:W], EX[:, u % 2, a, 0:W],
                                                          ri[:, u % 2, a:a + 1], None, ALU.mult)
                        ins.then_inc(p_done, 1)

                    def copy_odd(u):
                        W = P * (u // (NH // 2) + 1)
                        dve.wait_ge(t_mm, U0 + u + 1 + C2)
                        dve.wait_ge(pv_mm, U0 + u - 1 + C2)
                        nc.vector.tensor_copy(PT[:, u % 2, 1, 0:W], PB[:, 1, 0:W]).then_inc(pt_b, 1)

                    def finish(i, step):
                        t = T4 * g + i
                        if step == 0:
                            dve.wait_ge(cth_done, t + 1)
                            nc.vector.tensor_tensor(ctl[:], CX.rearrange("p (k t) -> p k t", k=KC),
                                                    cth[:].bitcast(f32), ALU.subtract).then_inc(ctl_done, 1)
                        if step == 1:
                            dve.wait_ge(wo_mm, t + 1)
                            nc.vector.tensor_tensor(XL[:, i, :], WK, XL[:, i, :], ALU.add).then_inc(xm_done, 1)
                            dve.wait_ge(xm_done, t + 1)
                            nc.vector.scalar_tensor_tensor(xs[:, ds(t, 1), :], XL[:, i, :], tg[:, 1:2],
                                                           xs[:, ds(t, 1), :], ALU.mult, ALU.add
                                                           ).then_inc(xacc_done, 1)
                        if step == 2:
                            dve.wait_ge(h2_mm, t + 1)
                            nc.vector.tensor_tensor(hw[:], WK.rearrange("p (k t) -> p k t", k=KC),
                                                    wln[:, 1, :].unsqueeze(2).broadcast_to([P, KC, P]),
                                                    ALU.mult).then_inc(hw_done, 1)
                        if step == 3:
                            dve.wait_ge(rt_mm, t + 1)
                            nc.vector.tensor_copy(lg[:, T4 * (g % HB) + i, :], WK[:, 0:ROUTE]).then_inc(lg_done, 1)

                    row_max(0)
                    row_max(1)
                    norm_probs(0)
                    for u in range(32):
                        if u >= 8 and u % 8 == 0:
                            finish(u // 8 - 1, 0)
                        copy_odd(u)
                        if u + 1 < 32:
                            norm_probs(u + 1)
                        if u + 2 < 32:
                            row_max(u + 2)
                        if u >= 8 and u % 8 in (1, 4, 6):
                            finish(u // 8 - 1, (1, 4, 6).index(u % 8) + 1)
                        if u == 15 and g % HB < HB - 1:
                            stats(xs, abn, amv, a_bn, a_mv, g + 1)
                    for step in range(3):
                        finish(3, step)
                    if g % HB < HB - 1:
                        h1_rest(g + 1)
                    finish(3, 3)

            def gating(half):
                tiles = slice(TH * half, TH * half + TH)
                n = [GT * half]

                def step_(ins):
                    n[0] = n[0] + 1
                    ins.then_inc(gt, 1)
                    dve.wait_ge(gt, n[0])

                step_(nc.vector.tensor_reduce(gs[:, 0, :], lg[:, :, 0:NE], AX.X, ALU.max, negate=True))
                step_(nc.vector.tensor_tensor(pr[:, 0], lg[:, :, 0:NE],
                                              gs[:, 0, :].unsqueeze(2).broadcast_to([P, TH, NE]), ALU.add))
                dve.wait_ge(gt_e, half + 1)
                step_(nc.vector.tensor_reduce(gs[:, 1, :], pr[:, 1], AX.X, ALU.add))
                step_(nc.vector.reciprocal(gs[:, 2, :], gs[:, 1, :]))
                step_(nc.vector.tensor_tensor(pr[:, 2], pr[:, 1],
                                              gs[:, 2, :].unsqueeze(2).broadcast_to([P, TH, NE]), ALU.mult))
                nc.vector.memset(tick[:], 0.0).then_inc(gt, 1)
                for t in range(TH):
                    nc.vector.max(m8[:, t, :], pr[:, 2, t, :]).then_inc(gt, 1)
                n[0] = n[0] + 1 + TH
                dve.wait_ge(gt, n[0])
                nc.vector.memset(tick[:], 0.0).then_inc(gt, 1)
                for t in range(TH):
                    nc.vector.max_index(i8[:, t, :], m8[:, t, :], pr[:, 2, t, :]).then_inc(gt, 1)
                n[0] = n[0] + 1 + TH
                dve.wait_ge(gt, n[0])
                step_(nc.vector.tensor_copy(i8f[:], i8[:, :, 0:2]))
                for t in range(TH):
                    for j in range(2):
                        step_(nc.vector.tensor_scalar(cc[:, j, t, :], iota8[:], i8f[:, t, j:j + 1],
                                                      m8[:, t, j:j + 1], ALU.is_equal, ALU.mult))
                step_(nc.vector.tensor_tensor(cc[:, 0], cc[:, 0], cc[:, 1], ALU.add))
                dve.wait_ge(gt_t, half + 1)
                step_(nc.vector.tensor_scalar(gs[:, 0, :], gs[:, 3, :], 1.0, tgq[:, 0:1], ALU.add, ALU.mult))
                step_(nc.vector.tensor_scalar(cmb[:, tiles, 0:NE], cc[:, 0], tg[:, 3:4], None, ALU.mult))
                nc.vector.tensor_copy(cmb[:, tiles, NE:NU],
                                      gs[:, 0, :].unsqueeze(2).broadcast_to([P, TH, NU - NE])
                                      ).then_inc(att_done, 1)

            def expert_stage(half):
                attention_ended(dve, half)
                gating(half)
                dve.wait_ge(att_done, half + 1 + C1)

                def unit(k, place=lambda j, late=False: None, more=True):
                    S0 = first_chunk(half, k)

                    def act_of(s):
                        dve.wait_ge(f_t, S0 + s + 1)
                        nc.vector.scalar_tensor_tensor(ft[:, s % 2, :], ft[:, s % 2, :], 1.0, FG[s % 2],
                                                       ALU.add, ALU.mult).then_inc(f_p, 1)
                        dve.wait_ge(f_p, S0 + s + 1 + C2)
                        dve.wait_ge(f_ah, S0 + s - 1 + C2)
                        dve.wait_ge(f_al, S0 + s - 1 + C2)
                        nc.vector.tensor_tensor(fa[:, s % 2, :], FU[s % 2], ft[:, s % 2, :], ALU.mult
                                                ).then_inc(f_a, 1)

                    def add(tt):
                        dve.wait_ge(d_mm, TH * k + tt + 1 + C1)
                        dve.wait_ge(d_acc, TH * k + tt - TH + 1 + C_DA)
                        w = k - NU * half
                        w = slice(w, w + 1) if isinstance(w, int) else ds(w, 1)
                        nc.vector.scalar_tensor_tensor(xs[:, TH * half + tt, :], FD[tt % 2],
                                                       cmb[:, TH * half + tt, w],
                                                       xs[:, TH * half + tt, :], ALU.mult, ALU.add
                                                       ).then_inc(d_acc, 1)

                    D0 = 2 * NG * NCH
                    for s, (_, _, places) in enumerate(chunks(not more) + [(0, 0, [D0])]):
                        place(places[0])
                        if s:
                            act_of(s - 1)
                            place(places[0] - 1, True)
                        for j in places[1:]:
                            place(j)
                            place(j - 1, True)
                    add(0)
                    place(D0, True)
                    for n in range(1, T4):
                        place(D0 + n)
                        add(2 * n - 1)
                        add(2 * n)
                        place(D0 + n, True)
                    add(TH - 1)

                def before(g, j, late=False):
                    if not late:
                        return
                    if j < 2:
                        for t in (2 * j, 2 * j + 1):
                            nc.vector.bn_stats(ebn[:, t, :], xs[:, T4 * g + t, :]).then_inc(z_bn, 1)
                    if j == 3:
                        dve.wait_ge(z_bn, (T4 + 1) * g + T4)
                        nc.vector.memset(tick[:], 0.0).then_inc(z_bn, 1)
                        for t in range(T4):
                            nc.vector.bn_aggr(emv[:, t, :], ebn[:, t, :]).then_inc(z_mv, 1)
                    if j in (2, 4, 6, 8):
                        et = j // 2 - 1
                        dve.wait_ge(cv_init, T4 * g + et + 1)
                        for sh in range(1, TAPS):
                            if sh > 1:
                                dve.wait_ge(cv_tap, 12 * g + 3 * et + sh - 1)
                            tap = TAPS - 1 - sh
                            nc.vector.scalar_tensor_tensor(eDL[:, et, sh:L], EB[et % 2][:, 0:L - sh],
                                                           chan[:, et, tap:tap + 1], eDL[:, et, sh:L],
                                                           ALU.mult, ALU.add).then_inc(cv_tap, 1)
                    if j in (4, 6, 8, 10):
                        et = j // 2 - 2
                        dve.wait_ge(u_t4, T4 * (g - HB) + et + 1)
                        nc.vector.scalar_tensor_tensor(eDU[:, et, :], eYA[:, et, :], 1.0, eDL[:, et, :],
                                                       ALU.add, ALU.mult).then_inc(u_d4, 1)
                    if j in (13, 15):
                        dve.wait_ge(z_t4, 2 * (g - HB) + (j - 13) // 2 + 1)
                        r = slice(j - 13, j - 11)
                        nc.vector.scalar_tensor_tensor(eZS[:, r, :], eYA[:, r, :], 1.0, eZS[:, r, :],
                                                       ALU.add, ALU.mult).then_inc(z_d4, 1)
                    if j in (17, 19, 21, 23):
                        et = (j - 17) // 2
                        dve.wait_ge(dt_abs, T4 * g + et + 1)
                        nc.vector.tensor_scalar(eDL[:, et, :], EB[et % 2], chan[:, et, TAPS + 1:TAPS + 2], 0.0,
                                                ALU.add, ALU.max).then_inc(dt_rel, 1)
                    if j == 26:
                        dve.wait_ge(dt_l, g + 1 - HB)
                        nc.vector.tensor_tensor(eDL[:], eDL[:], eYA[:], ALU.add).then_inc(dl_done, 1)
                        dve.wait_ge(dl_done, g + 1 - HB)
                    if j in (27, 28, 29, 30):
                        tt = j - 27
                        dve.wait_ge(yi_mm, T4 * g + tt + 1)
                        nc.vector.tensor_copy(eYA[:, tt, :], EB[tt % 2]).then_inc(yi_done, 1)
                    if j == 31:
                        nc.vector.scalar_tensor_tensor(eDU[:], eDU[:], 0.5, eDL[:], ALU.mult, ALU.mult
                                                       ).then_inc(du_done, 1)

                def step(g, i, j, late=False):
                    q = nth(g, i, j)
                    r = q - T4 * NS * HB
                    if not late:
                        dve.wait_ge(gb4, r + 1 + C_G4)
                        dve.wait_ge(dA_ready, q + 1)
                        dve.wait_ge(hT_ready, q - 1 + C_HT)
                        nc.vector.tensor_tensor_scan(eHS[:, j % 2, :], EB[0], eGB[:, j % 2, :],
                                                     0.0, ALU.mult, ALU.add).then_inc(scan_done, 1)
                    else:
                        dve.wait_ge(hT_ready, q + 1 + C_HT)
                        dve.wait_ge(y4, r - T4 + 1 + C4)
                        et = j % T4
                        for tt in range(T4):
                            ins = nc.vector.scalar_tensor_tensor(eYA[:, tt, et * P:(et + 1) * P],
                                                                 EB[1][:, tt * P:(tt + 1) * P],
                                                                 eCt[:, tt, column(i, j)],
                                                                 eYA[:, tt, et * P:(et + 1) * P],
                                                                 ALU.mult, ALU.add)
                        ins.then_inc(y4, 1)

                def first(g):
                    dve.wait_ge(yi_done, T4 * g + T4)
                    dve.wait_ge(du_done, g + 1 - HB)
                    if g == B - 1:
                        dve.wait_ge(x1_done, T4 * g + C_X1)
                        stats(xs, abn, amv, a_bn, a_mv, HB)

                def after(g):
                    dve.wait_ge(y4, T4 * NS * (g + 1 - HB) + C4)
                    for tt in range(T4):
                        dve.wait_ge(zT_ready, T4 * g + tt + 1 + C_ZT)
                        nc.vector.tensor_tensor(eYA[:, tt, :], EB[tt % 2], eYA[:, tt, :], ALU.mult
                                                ).then_inc(y_z, 1)
                    for tt in range(T4):
                        dve.wait_ge(y_z, T4 * g + tt + 1)
                        nc.vector.scalar_tensor_tensor(xs[:, T4 * g + tt, :], eYA[:, tt, :], tg[:, 2:3],
                                                       xs[:, T4 * g + tt, :], ALU.mult, ALU.add
                                                       ).then_inc(x1_done, 1)

                if half:
                    with dve.Fori(NU, 2 * NU - 1) as k:
                        unit(k)
                    unit(2 * NU - 1, more=False)
                else:
                    for et in range(T4):
                        nc.vector.tensor_scalar(eddiag[:, et, :], ident[:], chan[:, et, TAPS + 2:TAPS + 3], 0.5,
                                                ALU.mult, ALU.mult).then_inc(ddiag_s, 1)
                    beside(unit, before, step, after)(dve, first)

            scan_stage()
            for half in range(2):
                attention_stage(half)
                expert_stage(half)

        @block.gpsimd
        def _(pool):
            pool.sem_inc(gb_ready, C_GB)
            pool.sem_inc(gb4, C_G4)
            pool.sem_inc(wal_done, C_WL)
            pool.sem_inc(rope_c, C2)
            pool.sem_inc(f_al, C2)
            pool.sem_inc(wgl_s, C1)
            pool.sem_inc(wdl_s, C1)
            for row, value in ((mhalf, -0.5), (eps5, 1e-5), (eps6, 1e-6), (mone, -1.0), (perh, 1.0 / H)):
                nc.gpsimd.memset(row[:], value).then_inc(rows_made, 1)
            pool.wait_ge(rows_made, 5)

            def scan_stage():
                with pool.Fori(0, HB) as g:
                    pool.wait_ge(z_mv, T4 * g + T4)
                    nc.gpsimd.tensor_tensor(zst[:, 0, :], mv[:, :, 1], eps5[:], ALU.add).then_inc(z_norm, 1)
                    pool.wait_ge(z_norm, 4 * g + 1)
                    nc.gpsimd.tensor_tensor(zst[:, 1, :], zst[:, 0, :], mhalf[:], ALU.pow).then_inc(z_norm, 1)
                    pool.wait_ge(z_norm, 4 * g + 2)
                    nc.gpsimd.tensor_tensor(zst[:, 2, :], mv[:, :, 0], zst[:, 1, :], ALU.mult).then_inc(z_norm, 1)
                    pool.wait_ge(z_norm, 4 * g + 3)
                    nc.gpsimd.tensor_tensor(zst[:, 3, :], zst[:, 2, :], mone[:], ALU.mult).then_inc(z_norm, 1)
                    for c in range(KC // HB):
                        q = (KC // HB) * g + c
                        pool.wait_ge(wah_done, q + 1)
                        k = g * (KC // HB) + c
                        nc.gpsimd.tensor_tensor(wal[:, ds(k, 1), :], wraw[:].unsqueeze(1),
                                                wah[:, ds(k, 1), :].bitcast(f32),
                                                ALU.subtract).then_inc(wal_done, 1)
                    with pool.Fori(0, NS // NL) as i:
                        pool.wait_ge(yi_done, T4 * g + T4)
                        for n in range(NL):
                            step = NS * g + NL * i + n
                            if n % 2 == 0:
                                pool.wait_ge(bb_in[n // 2], 16 * ((NS // NL) * g + i + 1))
                            pool.wait_ge(scan_done, T4 * step - T4 + C_SC)
                            for a, b in ([(et, et + 1) for et in range(T4)] if n == 0 else [(0, T4)]):
                                pool.wait_ge(du4, T4 * g + b)
                                nc.gpsimd.tensor_tensor(GB[:, n % 2, a:b, :], DU[:, a:b, :],
                                                        BB[:, n // 2, n % 2, :].unsqueeze(1)
                                                        .broadcast_to([P, b - a, L]), ALU.mult
                                                        ).then_inc(gb_ready if b == T4 else gb_part, 1)

            def attention_stage(half):
                def norms(g):
                    def norm(n, ins):
                        ins.then_inc(a_norm, 1)
                        pool.wait_ge(a_norm, 8 * g + n)

                    if g:
                        pool.wait_ge(a_hp, T4 * g)
                    pool.wait_ge(a_mv, T4 * g + T4)
                    var, mean = amv[:, :, 1], amv[:, :, 0]
                    norm(1, nc.gpsimd.tensor_tensor(ast[:, 0, :], var, eps5[:], ALU.add))
                    norm(2, nc.gpsimd.tensor_tensor(ast[:, 1, :], ast[:, 0, :], mhalf[:], ALU.pow))
                    norm(3, nc.gpsimd.tensor_tensor(ast[:, 3, :], mean, ast[:, 1, :], ALU.mult))
                    norm(4, nc.gpsimd.tensor_tensor(ast[:, 2, :], ast[:, 3, :], mone[:], ALU.mult))
                    norm(5, nc.gpsimd.tensor_tensor(ast[:, 4, :], ast[:, 1, :], ast[:, 1, :], ALU.mult))
                    norm(6, nc.gpsimd.tensor_tensor(ast[:, 5, :], var, ast[:, 4, :], ALU.mult))
                    norm(7, nc.gpsimd.tensor_tensor(ast[:, 7, :], ast[:, 5, :], eps6[:], ALU.add))
                    norm(8, nc.gpsimd.tensor_tensor(ast[:, 6, :], ast[:, 7, :], mhalf[:], ALU.pow))

                norms(HB * half)
                scan_ended(pool, half)
                if half:
                    for c in (0, 2):
                        pool.wait_ge(wah2[0], c // 2 + 1)
                        nc.gpsimd.tensor_tensor(wal[:, c, :], wagain[c], wah[:, c, :].bitcast(f32),
                                                ALU.subtract).then_inc(wal2[0], 1)
                pool.wait_ge(attc_in[half], 80)
                for g in range(HB * half, HB * half + HB):
                    for m in range(8):
                        pool.wait_ge(qb_ready, 8 * g + m + 1 + C2)
                        pool.wait_ge(qk_done, 8 * g + m - 1 + C2)
                        nc.gpsimd.tensor_tensor(RC[:, m % 2, :], QB[:, m % 2, :], rope[:, 0, :], ALU.mult
                                                ).then_inc(rope_c, 1)
                    for i in range(T4):
                        t = T4 * g + i
                        if i == T4 - 2 and g % HB < HB - 1:
                            norms(g + 1)
                        pool.wait_ge(sq_done, t + 1)
                        nc.gpsimd.tensor_tensor(r2[:, 2, i:i + 1], ss[:, i:i + 1], perh[:, 0:1], ALU.mult
                                                ).then_inc(r2_s, 1)
                        pool.wait_ge(r2_s, 3 * t + 1)
                        nc.gpsimd.tensor_tensor(r2[:, 0, i:i + 1], r2[:, 2, i:i + 1], eps6[:, 0:1], ALU.add
                                                ).then_inc(r2_s, 1)
                        pool.wait_ge(r2_s, 3 * t + 2)
                        nc.gpsimd.tensor_tensor(r2[:, 1, i:i + 1], r2[:, 0, i:i + 1], mhalf[:, 0:1], ALU.pow
                                                ).then_inc(r2_s, 1)
                        pool.wait_ge(h2h_kept, t + 1)
                        at = (g % HB) * L + i * P
                        nc.gpsimd.tensor_tensor(h2l[:, :, at:at + P], hw[:], h2h[:, :, at:at + P].bitcast(f32),
                                                ALU.subtract).then_inc(h2l_kept, 1)

            def expert_stage(half):
                attention_ended(pool, half)

                def split(k, c):
                    pool.wait_ge(wgh_s, KC * k + c + 1)
                    nc.gpsimd.tensor_tensor(wgl[:, c, :], wgr[:, c * 2 * EW:(c + 1) * 2 * EW],
                                            wgh[:, c, :].bitcast(f32), ALU.subtract).then_inc(wgl_s, 1)

                def unit(k, place=lambda j: None, more=True):
                    S0 = first_chunk(half, k)

                    def rest(s, grp, c):
                        pool.wait_ge(f_ah, S0 + s + 1 + C2)
                        cols = slice(grp * L, (grp + 1) * L)
                        nc.gpsimd.tensor_tensor(fal[:, c, cols], fa[:, s % 2, :], fah[:, c, cols].bitcast(f32),
                                                ALU.subtract).then_inc(f_al, 1)

                    done = None
                    for s, at in enumerate(chunks(not more) + [(0, 0, [2 * NG * NCH])]):
                        for j in at[2]:
                            place(j)
                        if s:
                            rest(s - 1, *done)
                        done = at[:2]
                        if 1 <= s <= NCH:
                            c = s - 1
                            pool.wait_ge(wdh_s, NCH * k + c + 1)
                            nc.gpsimd.tensor_tensor(wdl[:, c, :], wdr[:, c * H:(c + 1) * H],
                                                    wdh[:, c, :].bitcast(f32), ALU.subtract).then_inc(wdl_s, 1)
                    for c in range(KC):
                        if c < KC - 1:
                            place(2 * NG * NCH + 1 + c)
                        if more:
                            split(k + 1, c)

                def before(g, j):
                    if j == 5:
                        pool.wait_ge(z_mv, T4 * g + T4)
                        nc.gpsimd.tensor_tensor(ezst[:, 0, :], emv[:, :, 1], eps5[:], ALU.add).then_inc(z_norm, 1)
                        pool.wait_ge(z_norm, 4 * g + 1)
                        nc.gpsimd.tensor_tensor(ezst[:, 1, :], ezst[:, 0, :], mhalf[:], ALU.pow).then_inc(z_norm, 1)
                        pool.wait_ge(z_norm, 4 * g + 2)
                        nc.gpsimd.tensor_tensor(ezst[:, 2, :], emv[:, :, 0], ezst[:, 1, :], ALU.mult
                                                ).then_inc(z_norm, 1)
                        pool.wait_ge(z_norm, 4 * g + 3)
                        nc.gpsimd.tensor_tensor(ezst[:, 3, :], ezst[:, 2, :], mone[:], ALU.mult).then_inc(z_norm, 1)

                def first(g):
                    pool.wait_ge(du_done, g + 1 - HB)

                def step(g, i, j):
                    q = nth(g, i, j)
                    if j % T4 == 0:
                        n = j // T4
                        pool.wait_ge(bb_in[n % 2], 16 * (HB * (NS // NL) + (NS // 2) * (g - HB) + n // 2 + 1) + 32 * i)
                    pool.wait_ge(scan_done, q - 1 + C_SC)
                    nc.gpsimd.tensor_tensor(eGB[:, j % 2, :], eDU[:, j % T4, :], eBB[:, (j // T4) % 2, :], ALU.mult
                                            ).then_inc(gb4, 1)

                for c in range(KC):
                    split(NU * half, c)
                if half:
                    with pool.Fori(NU, 2 * NU - 1) as k:
                        unit(k)
                    unit(2 * NU - 1, more=False)
                else:
                    beside(unit, before, step, lambda g: None)(pool, first)

            scan_stage()
            for half in range(2):
                attention_stage(half)
                expert_stage(half)


def host_layout(inputs):
    a = {k: np.asarray(v) for k, v in inputs.items()}
    f = np.float32

    def rows(w, k):
        return w.reshape(k, P, -1).transpose(1, 0, 2)

    x = a["x"].reshape(2, HB, T4, P, H).transpose(0, 3, 1, 2, 4).reshape(2, P, TH, H)
    c = a["ctx_1024"].reshape(2, HB, L, DC // P, P).transpose(0, 4, 1, 3, 2)
    chan = np.concatenate([a["L0_xattn_conv_w"], a["L0_xattn_conv_b"][:, None], a["L0_xattn_dt_proj_b"][:, None],
                           a["L0_xattn_D"][:, None], a["L0_xattn_A_log"]], axis=1)
    bqk = np.concatenate([a["L0_ffn_bq"].reshape(T4, P).T, a["L0_ffn_bk"].reshape(T4, P).T], axis=1)
    watt = np.concatenate([a["L0_ffn_wq"], a["L0_ffn_wk"], a["L0_ffn_wv"], a["L0_ffn_wo"]], axis=1)
    route = np.concatenate([a["L0_ffn_w_router"], a["L0_ffn_w_sh_eg"], np.zeros((H, 1), f)], axis=1)
    wln = np.stack([a["L0_ffn_w_ln1"].reshape(KC, P).T, a["L0_ffn_w_ln2"].reshape(KC, P).T], axis=1)

    def units(experts, shared, axis):
        def fill(w, axis, n):
            pad = [(0, 0)] * w.ndim
            pad[axis] = (0, n - w.shape[axis])
            return np.pad(w, pad)
        n = NU - NE
        return np.concatenate([fill(experts, axis + 1, EW),
                               np.stack(np.split(fill(shared, axis, n * EW), n, axis=axis))], axis=0)

    gate = units(a["L0_ffn_w_gate_e"], a["L0_ffn_w_sh_gate"], 1)
    up = units(a["L0_ffn_w_up_e"], a["L0_ffn_w_sh_up"], 1)
    down = units(a["L0_ffn_w_down_e"], a["L0_ffn_w_sh_down"], 0)
    gu = np.concatenate([gate, up], axis=2).reshape(NU, KC, P, 2 * EW).transpose(0, 2, 1, 3).reshape(NU, P, GW)
    dn = down.reshape(NU, NCH, P, H).transpose(0, 2, 1, 3).reshape(NU, P, DW)

    inv = (f(1.0) / np.power(f(1000000.0), np.arange(0, HD, 2, dtype=f) / f(HD))).astype(f)
    ang = (np.arange(L, dtype=f)[:, None] * inv[None, :]).astype(f).T
    cos, sin = np.cos(ang).astype(f), np.sin(ang).astype(f)
    rope = np.stack([np.tile(np.concatenate([cos, cos]), (P // HD, 1)),
                     np.tile(np.concatenate([-sin, sin]), (P // HD, 1))], axis=1)
    d = np.arange(P)
    perm = np.zeros((P, P), f)
    perm[d, d ^ (HD // 2)] = 1.0
    q = np.arange(P)
    mask = np.where(q[None, :] <= q[:, None], f(0.0), f(MASKED)).astype(f)
    arrays = {
        "x_in": x, "ctx_in": c, "gates_in": np.concatenate([a["g_xattn"], a["g_ffn"]]),
        "w_in_in": rows(a["L0_xattn_in_proj_w"].T, DC // P), "chan_in": rows(chan, T4),
        "xproj_in": rows(a["L0_xattn_x_proj_w"].T, T4), "dtproj_in": a["L0_xattn_dt_proj_w"].T,
        "watt_in": rows(watt, KC), "bqk_in": bqk, "bv_in": a["L0_ffn_bv"], "wln_in": wln,
        "route_in": rows(route, KC), "wffn_in": np.concatenate([gu, dn], axis=2),
        "rope_in": rope, "perm_in": perm, "ident_in": np.eye(P, dtype=f), "mask_in": mask,
        "iota_in": np.arange(NE, dtype=f),
    }
    return {k: np.ascontiguousarray(v) for k, v in arrays.items()}


def kernel(**inputs):
    import concourse.bacc as bacc
    from concourse.bass_utils import run_bass_kernel_spmd

    nc = bacc.Bacc("TRN2", target_bir_lowering=False, num_devices=1, dynamic_dma_scratch_size=1024)
    arrays = host_layout(inputs)
    args = [nc.dram_tensor(n, v.shape, mybir.dt.from_np(v.dtype), kind="ExternalInput").ap()
            for n, v in arrays.items()]
    out = nc.dram_tensor("out", (2, P, TH, H), mybir.dt.float32, kind="ExternalOutput").ap()
    b_scratch = nc.dram_tensor("b_scratch", (B, NS, L), mybir.dt.float32).ap()
    build(nc, *args, out, b_scratch)
    r = run_bass_kernel_spmd(nc, [arrays], core_ids=[0])
    got = r.results[0]["out"]
    return got.reshape(2, P, HB, T4, H).transpose(0, 2, 3, 1, 4).reshape(B, L, H)
```
